# Optimizing a Trainium2 kernel written in Bass

```python
import numpy as np
import jax
import jax.numpy as jnp

def _softmax(x, axis=-1):
    return jax.nn.softmax(x, axis=axis)

def _gelu(x):
    return jax.nn.gelu(x, approximate=True)

def _silu(x):
    return jax.nn.silu(x)

def _sigmoid(x):
    return jax.nn.sigmoid(x)

def _layernorm(x, axis=-1, eps=1e-05):
    m = jnp.mean(x, axis=axis, keepdims=True)
    v = jnp.var(x, axis=axis, keepdims=True)
    return (x - m) / jnp.sqrt(v + eps)

def _scatter_add(tgt, idx, src, axis=0):
    return tgt.at[idx].add(src)

def _segment_sum(src, seg, n):
    return jax.ops.segment_sum(src, seg, n)
kernel_name = 'mk_flamingo_gated_d2_seqx_r8_701911'

def setup_inputs(seed: int=0):
    np.random.seed(seed)
    _w = jnp.asarray

    def _rec_inputs():
        import jax
        import jax.numpy as jnp
        _rk = jax.random.key(seed)
        x = 7.22e-05 + 1 * jax.random.normal(jax.random.fold_in(_rk, 1), (4, 512, 128), jnp.float32)
        _lenS = 512 - jax.random.randint(jax.random.fold_in(_rk, 7), (4,), 0, max(1, 512 // 4) + 1, jnp.int32)
        _lenS2 = 154 - jax.random.randint(jax.random.fold_in(_rk, 8), (4,), 0, max(1, 154 // 4) + 1, jnp.int32)
        _ctx_768P = jax.random.normal(jax.random.fold_in(_rk, 11), (4, 16, 96), jnp.float32)
        _ctx_768c = jax.random.dirichlet(jax.random.fold_in(_rk, 511), 0.3 * jnp.ones((16,), jnp.float32), (4, 154))
        _ctx_768t = jnp.einsum('bsk,bkd->bsd', _ctx_768c, _ctx_768P)
        _ctx_768t = _ctx_768t * jax.lax.rsqrt(jnp.mean(jnp.square(_ctx_768t)) + 1e-12) * 0.953939
        ctx_768 = 2.09791e-05 + 1.00001 * (_ctx_768t + 0.3 * jax.random.normal(jax.random.fold_in(_rk, 611), (4, 154, 96), jnp.float32))
        _validS = jnp.arange(512)[None, :] < _lenS[:, None]
        _validS2 = jnp.arange(154)[None, :] < _lenS2[:, None]
        _causal = jnp.tril(jnp.ones((512, 512), dtype=bool))
        mask_BxS2_bf1 = jnp.ones((4, 154), dtype=bool)
        _g = jax.random.normal(jax.random.fold_in(_rk, 9001), (2, 2), jnp.float32)
        _g = jnp.sign(_g) * jnp.maximum(jnp.abs(_g), 1.0) + (_g == 0) * 1.0
        g_xattn = _g[0]
        g_ffn = _g[1]
        return (x, ctx_768, mask_BxS2_bf1, g_xattn, g_ffn)
    x, ctx_768, mask_BxS2_bf1, g_xattn, g_ffn = _rec_inputs()

    def _L0_xattn_setup():
        import jax, jax.numpy as jnp
        import numpy as np
        HEADS = 8
        DIM_HEAD = 64
        SCALE = DIM_HEAD ** (-0.5)
        key = jax.random.key(seed)
        ks = jax.random.split(key, 7)
        b, n, m = (4, 256, 128)
        qd, cd, inner = (128, 96, HEADS * DIM_HEAD)
        s = lambda fan_in: 1.0 / np.sqrt(fan_in)
        return {'x': jax.random.normal(ks[0], (b, n, qd), jnp.float32), 'context': jax.random.normal(ks[1], (b, m, cd), jnp.float32), 'Wq': jax.random.normal(ks[2], (qd, inner), jnp.float32) * s(qd), 'Wk': jax.random.normal(ks[3], (cd, inner), jnp.float32) * s(cd), 'Wv': jax.random.normal(ks[4], (cd, inner), jnp.float32) * s(cd), 'Wout': jax.random.normal(ks[5], (inner, qd), jnp.float32) * s(inner), 'bout': jax.random.normal(ks[6], (qd,), jnp.float32) * 0.01}
    _L0_xattn_all = _L0_xattn_setup()
    _L0_xattn_in = {k: v for k, v in _L0_xattn_all.items() if k in ('Wq', 'Wk', 'Wv', 'Wout', 'bout')}
    del _L0_xattn_all

    def _L0_ffn_setup():
        import jax, jax.numpy as jnp
        import numpy as np
        D = 128
        H = 16
        HD = D // H
        L = 64
        E = 8
        B, T = (4, 256)
        EPS = 1e-06

        def _glorot(k, shape):
            fan_in, fan_out = (shape[-2], shape[-1])
            lim = np.sqrt(6.0 / (fan_in + fan_out)).astype(np.float32)
            return jax.random.uniform(k, shape, jnp.float32, -lim, lim)

        def _rmsnorm(x, gamma):
            return gamma * x * jax.lax.rsqrt(jnp.mean(x * x, axis=-1, keepdims=True) + EPS)
        key = jax.random.key(seed)
        ks = jax.random.split(key, 8)
        return {'x': jax.random.normal(ks[0], (B, T, D), jnp.float32), 'gamma1': jnp.ones((D,), jnp.float32), 'Wq': _glorot(ks[1], (D, D)), 'bq': jnp.zeros((D,), jnp.float32), 'Wdown': _glorot(ks[2], (D, L)), 'bdown': jnp.zeros((L,), jnp.float32), 'Wup': _glorot(ks[3], (L, 2 * D)), 'bup': jnp.zeros((2 * D,), jnp.float32), 'Wo': _glorot(ks[4], (D, D)), 'bo': jnp.zeros((D,), jnp.float32), 'gamma2': jnp.ones((D,), jnp.float32), 'Wg': _glorot(ks[5], (D, E)), 'bg': jnp.zeros((E,), jnp.float32), 'We': _glorot(ks[6], (E, D, D))}
    _L0_ffn_all = _L0_ffn_setup()
    _L0_ffn_in = {k: v for k, v in _L0_ffn_all.items() if k in ('gamma1', 'Wq', 'bq', 'Wdown', 'bdown', 'Wup', 'bup', 'Wo', 'bo', 'gamma2', 'Wg', 'bg', 'We')}
    del _L0_ffn_all

    def _L1_xattn_setup():
        import jax, jax.numpy as jnp
        import numpy as np
        DIM = 128
        CTX_DIM = 96
        HEADS = 16
        key = jax.random.key(seed)
        ks = jax.random.split(key, 7)
        B, N, M = (4, 512, 32)
        x = jax.random.normal(ks[0], (B, N, DIM), dtype=jnp.float32)
        context = jax.random.normal(ks[1], (B, M, CTX_DIM), dtype=jnp.float32)
        context_mask = jnp.ones((B, M), dtype=bool)
        s_d = 1.0 / np.sqrt(DIM)
        s_c = 1.0 / np.sqrt(CTX_DIM)
        Wq = jax.random.normal(ks[2], (DIM, DIM), dtype=jnp.float32) * s_d
        Wk = jax.random.normal(ks[3], (CTX_DIM, DIM), dtype=jnp.float32) * s_c
        Wv = jax.random.normal(ks[4], (CTX_DIM, DIM), dtype=jnp.float32) * s_c
        Wo = jax.random.normal(ks[5], (DIM, DIM), dtype=jnp.float32) * s_d
        return {'x': x, 'context': context, 'context_mask': context_mask, 'Wq': Wq, 'Wk': Wk, 'Wv': Wv, 'Wo': Wo}
    _L1_xattn_all = _L1_xattn_setup()
    _L1_xattn_in = {k: v for k, v in _L1_xattn_all.items() if k in ('Wq', 'Wk', 'Wv', 'Wo')}
    del _L1_xattn_all

    def _L1_ffn_setup():
        import jax, jax.numpy as jnp
        import numpy as np
        DIM = 128
        HEADS = 8
        NUM_EXPERTS = 8192
        NUM_KEYS = 32
        DIM_KEY = 64
        TOPK = 16

        def _rmsnorm(v, g):
            scale = jnp.sqrt(jnp.asarray(v.shape[-1], v.dtype))
            n = jnp.maximum(jnp.linalg.norm(v, axis=-1, keepdims=True), 1e-12)
            return v / n * g * scale
        key = jax.random.key(seed)
        ks = jax.random.split(key, 6)
        B, N = (2, 64)
        x = jax.random.normal(ks[0], (B, N, DIM), dtype=jnp.float32)
        gamma = jnp.ones((DIM,), dtype=jnp.float32)
        wq = jax.random.normal(ks[1], (2 * HEADS * DIM_KEY, DIM), dtype=jnp.float32) * 0.02
        keys = jax.random.normal(ks[2], (HEADS, NUM_KEYS, 2, DIM_KEY), dtype=jnp.float32) * 0.02
        table_down = jax.random.normal(ks[3], (NUM_EXPERTS, DIM), dtype=jnp.float32) * 0.02
        table_up = jax.random.normal(ks[4], (NUM_EXPERTS, DIM), dtype=jnp.float32) * 0.02
        return {'x': x, 'gamma': gamma, 'wq': wq, 'keys': keys, 'table_down': table_down, 'table_up': table_up}
    _L1_ffn_all = _L1_ffn_setup()
    _L1_ffn_in = {k: v for k, v in _L1_ffn_all.items() if k in ('gamma', 'wq', 'keys', 'table_down', 'table_up')}
    del _L1_ffn_all
    return {'x': x, 'ctx_768': ctx_768, 'mask_BxS2_bf1': mask_BxS2_bf1, 'g_xattn': g_xattn, 'g_ffn': g_ffn, 'L0_xattn_Wq': _L0_xattn_in['Wq'], 'L0_xattn_Wk': _L0_xattn_in['Wk'], 'L0_xattn_Wv': _L0_xattn_in['Wv'], 'L0_xattn_Wout': _L0_xattn_in['Wout'], 'L0_xattn_bout': _L0_xattn_in['bout'], 'L0_ffn_gamma1': _L0_ffn_in['gamma1'], 'L0_ffn_Wq': _L0_ffn_in['Wq'], 'L0_ffn_bq': _L0_ffn_in['bq'], 'L0_ffn_Wdown': _L0_ffn_in['Wdown'], 'L0_ffn_bdown': _L0_ffn_in['bdown'], 'L0_ffn_Wup': _L0_ffn_in['Wup'], 'L0_ffn_bup': _L0_ffn_in['bup'], 'L0_ffn_Wo': _L0_ffn_in['Wo'], 'L0_ffn_bo': _L0_ffn_in['bo'], 'L0_ffn_gamma2': _L0_ffn_in['gamma2'], 'L0_ffn_Wg': _L0_ffn_in['Wg'], 'L0_ffn_bg': _L0_ffn_in['bg'], 'L0_ffn_We': _L0_ffn_in['We'], 'L1_xattn_Wq': _L1_xattn_in['Wq'], 'L1_xattn_Wk': _L1_xattn_in['Wk'], 'L1_xattn_Wv': _L1_xattn_in['Wv'], 'L1_xattn_Wo': _L1_xattn_in['Wo'], 'L1_ffn_gamma': _L1_ffn_in['gamma'], 'L1_ffn_wq': _L1_ffn_in['wq'], 'L1_ffn_keys': _L1_ffn_in['keys'], 'L1_ffn_table_down': _L1_ffn_in['table_down'], 'L1_ffn_table_up': _L1_ffn_in['table_up']}

def reference(x, ctx_768, mask_BxS2_bf1, g_xattn, g_ffn, L0_xattn_Wq, L0_xattn_Wk, L0_xattn_Wv, L0_xattn_Wout, L0_xattn_bout, L0_ffn_gamma1, L0_ffn_Wq, L0_ffn_bq, L0_ffn_Wdown, L0_ffn_bdown, L0_ffn_Wup, L0_ffn_bup, L0_ffn_Wo, L0_ffn_bo, L0_ffn_gamma2, L0_ffn_Wg, L0_ffn_bg, L0_ffn_We, L1_xattn_Wq, L1_xattn_Wk, L1_xattn_Wv, L1_xattn_Wo, L1_ffn_gamma, L1_ffn_wq, L1_ffn_keys, L1_ffn_table_down, L1_ffn_table_up):
    import jax
    import jax.numpy as jnp

    def _L0_xattn_ref(x, context, Wq, Wk, Wv, Wout, bout):
        import jax, jax.numpy as jnp
        import numpy as np
        HEADS = 8
        DIM_HEAD = 64
        SCALE = DIM_HEAD ** (-0.5)
        b, n, _ = x.shape
        m = context.shape[1]
        q = (x @ Wq).reshape(b, n, HEADS, DIM_HEAD)
        k = (context @ Wk).reshape(b, m, HEADS, DIM_HEAD)
        v = (context @ Wv).reshape(b, m, HEADS, DIM_HEAD)
        sim = jnp.einsum('bihd,bjhd->bhij', q, k) * SCALE
        attn = jax.nn.softmax(sim, axis=-1)
        out = jnp.einsum('bhij,bjhd->bihd', attn, v).reshape(b, n, HEADS * DIM_HEAD)
        return out @ Wout + bout

    def _L0_ffn_ref(x, gamma1, Wq, bq, Wdown, bdown, Wup, bup, Wo, bo, gamma2, Wg, bg, We):
        import jax, jax.numpy as jnp
        import numpy as np
        D = 128
        H = 16
        HD = D // H
        L = 64
        E = 8
        B, T = (4, 256)
        EPS = 1e-06

        def _glorot(k, shape):
            fan_in, fan_out = (shape[-2], shape[-1])
            lim = np.sqrt(6.0 / (fan_in + fan_out)).astype(np.float32)
            return jax.random.uniform(k, shape, jnp.float32, -lim, lim)

        def _rmsnorm(x, gamma):
            return gamma * x * jax.lax.rsqrt(jnp.mean(x * x, axis=-1, keepdims=True) + EPS)
        b, t = (x.shape[0], x.shape[1])
        h = _rmsnorm(x, gamma1)
        q = (h @ Wq + bq).reshape(b, t, H, HD)
        kv = ((h @ Wdown + bdown) @ Wup + bup).reshape(b, t, H, 2 * HD)
        k, v = jnp.split(kv, 2, axis=-1)
        att = jnp.einsum('bthd,btgd->bthg', q, k) / np.sqrt(HD).astype(np.float32)
        att = jax.nn.softmax(att, axis=-1)
        out = jnp.einsum('bthg,btgd->bthd', att, v).reshape(b, t, D)
        x = x + (out @ Wo + bo)
        h2 = _rmsnorm(x, gamma2)
        gate = jax.nn.softmax(h2 @ Wg + bg, axis=-1)
        combined = jnp.einsum('btd,edf,bte->btf', h2, We, gate)
        return x + combined

    def _L1_xattn_ref(x, context, context_mask, Wq, Wk, Wv, Wo):
        import jax, jax.numpy as jnp
        import numpy as np
        DIM = 128
        CTX_DIM = 96
        HEADS = 16
        B, N, _ = x.shape
        M = context.shape[1]
        hd = DIM // HEADS
        scale = hd ** (-0.5)
        q = (x @ Wq).reshape(B, N, HEADS, hd).transpose(0, 2, 1, 3)
        k = (context @ Wk).reshape(B, M, HEADS, hd).transpose(0, 2, 1, 3)
        v = (context @ Wv).reshape(B, M, HEADS, hd).transpose(0, 2, 1, 3)
        scores = jnp.einsum('bhid,bhjd->bhij', q, k) * scale
        max_neg = -jnp.finfo(scores.dtype).max
        scores = jnp.where(context_mask[:, None, None, :], scores, max_neg)
        attn = jax.nn.softmax(scores, axis=-1)
        out = jnp.einsum('bhij,bhjd->bhid', attn, v)
        out = out.transpose(0, 2, 1, 3).reshape(B, N, DIM)
        return out @ Wo

    def _L1_ffn_ref(x, gamma, wq, keys, table_down, table_up):
        import jax, jax.numpy as jnp
        import numpy as np
        DIM = 128
        HEADS = 8
        NUM_EXPERTS = 8192
        NUM_KEYS = 32
        DIM_KEY = 64
        TOPK = 16

        def _rmsnorm(v, g):
            scale = jnp.sqrt(jnp.asarray(v.shape[-1], v.dtype))
            n = jnp.maximum(jnp.linalg.norm(v, axis=-1, keepdims=True), 1e-12)
            return v / n * g * scale
        B, N, D = x.shape
        xn = _rmsnorm(x, gamma)
        gate = xn
        q = gate @ wq.T
        q = q.reshape(B, N, 2, HEADS, DIM_KEY).transpose(2, 0, 1, 3, 4)
        sim = jnp.einsum('pbnhd,hkpd->pbnhk', q, keys)
        sx, ix = jax.lax.top_k(sim[0], TOPK)
        sy, iy = jax.lax.top_k(sim[1], TOPK)
        all_scores = (sx[..., :, None] + sy[..., None, :]).reshape(B, N, HEADS, TOPK * TOPK)
        all_indices = (ix[..., :, None] * NUM_KEYS + iy[..., None, :]).reshape(B, N, HEADS, TOPK * TOPK)
        scores, pk = jax.lax.top_k(all_scores, TOPK)
        indices = jnp.take_along_axis(all_indices, pk, axis=-1)
        wd = table_down[indices]
        wu = table_up[indices]
        h = jnp.einsum('bnd,bnhkd->bnhk', xn, wd)
        h = jax.nn.gelu(h, approximate=False) * jax.nn.softmax(scores, axis=-1)
        out = jnp.einsum('bnhk,bnhkd->bnd', h, wu)
        return out
    x = x + jnp.tanh(g_xattn[0]) * _L0_xattn_ref(_layernorm(x, axis=-1), ctx_768, L0_xattn_Wq, L0_xattn_Wk, L0_xattn_Wv, L0_xattn_Wout, L0_xattn_bout)
    x = x + jnp.tanh(g_ffn[0]) * _L0_ffn_ref(_layernorm(x, axis=-1), L0_ffn_gamma1, L0_ffn_Wq, L0_ffn_bq, L0_ffn_Wdown, L0_ffn_bdown, L0_ffn_Wup, L0_ffn_bup, L0_ffn_Wo, L0_ffn_bo, L0_ffn_gamma2, L0_ffn_Wg, L0_ffn_bg, L0_ffn_We)
    x = x + jnp.tanh(g_xattn[1]) * _L1_xattn_ref(_layernorm(x, axis=-1), ctx_768, mask_BxS2_bf1, L1_xattn_Wq, L1_xattn_Wk, L1_xattn_Wv, L1_xattn_Wo)
    x = x + jnp.tanh(g_ffn[1]) * _L1_ffn_ref(_layernorm(x, axis=-1), L1_ffn_gamma, L1_ffn_wq, L1_ffn_keys, L1_ffn_table_down, L1_ffn_table_up)
    return x

_drawn_inputs = setup_inputs


def setup_inputs(seed=0):
    import zlib

    import numpy as np

    out = dict(_drawn_inputs(seed))
    spreads = {'g_ffn': (-1.0, 0.6),
     'L0_ffn_gamma1': (1.0, 0.2),
     'L0_ffn_bq': (0.0, 0.344),
     'L0_ffn_bdown': (0.0, 0.279),
     'L0_ffn_bup': (0.0, 0.1),
     'L0_ffn_bo': (0.0, 0.1),
     'L0_ffn_gamma2': (1.0, 0.2),
     'L0_ffn_bg': (0.0, 0.284),
     'L1_ffn_gamma': (1.0, 0.6)}
    factors = {'L0_xattn_bout': 6.703,
     'L1_ffn_wq': 8.0,
     'L1_ffn_keys': 8.0,
     'L1_ffn_table_down': 8.0,
     'L1_ffn_table_up': 8.0}
    for name, (base, spread) in spreads.items():
        noise = np.random.default_rng([zlib.crc32(name.encode()), seed]).standard_normal(out[name].shape)
        drawn = base * np.exp(spread * noise) if base else spread * noise
        out[name] = jnp.asarray(drawn.astype(out[name].dtype))
    for name, factor in factors.items():
        out[name] = (out[name] * factor).astype(out[name].dtype)
    return out
```

```python
from contextlib import ExitStack

import concourse.bass as bass
from concourse import mybir

F32 = mybir.dt.float32
BF16 = mybir.dt.bfloat16
U8 = mybir.dt.uint8
ALU = mybir.AluOpType
ACT = mybir.ActivationFunctionType
X_AXIS = mybir.AxisListType.X

P = 128
BANK = 512
BATCH, SEQ, D = 4, 512, 128
CTX, CD = 154, 96
TILES = BATCH * SEQ // P
PER_BATCH = SEQ // P
UNIT = 8
FLAT = UNIT * CTX
CHUNKS = -(-FLAT // P)
TAIL = FLAT - (CHUNKS - 1) * P
HD0, HD1 = 64, 8
FH, FD = 16, 8
EXPERTS = 8
PH, KEYS, PK, TOP = 8, 32, 64, 16
GRID = KEYS * KEYS
STAIRS = [TOP // (i + 1) for i in range(TOP)]
CANDS = sum(STAIRS)
LOW = -3.0e38
FAR = -(2.0 ** 126)
BANK_HEADS = [3, 3, 2]

ROW_SIZES = [("bout", D), ("bq", D), ("bup", 2 * D), ("bo", D), ("bg", EXPERTS), ("gx", 2), ("gf", 2)]
ROWS = {}
_at = 0
for _name, _size in ROW_SIZES:
    ROWS[_name] = (_at, _at + _size)
    _at += _size
ROW_TOTAL = _at


class Steps:

    def __init__(self, sem, names):
        self.sem = sem
        self.names = names.split()
        self.n = 0

    def __call__(self, name):
        assert self.names[self.n % len(self.names)] == name, (self.names[self.n % len(self.names)], name)
        self.n += 1
        return self.sem

    def after(self, name, tile):
        return tile * len(self.names) + (self.names.index(name) + 1)


def flamingo_kernel(nc, d_x, d_ctx_t, d_mask, d_rows, d_cols, d_wk0, d_wqt0, d_wvt0, d_wout0, d_f_wq, d_f_wdt, d_f_wup, d_f_bd, d_f_wo, d_f_wg, d_f_we, d_wk1, d_wqt1, d_wvt1, d_wo1, d_pk_wq, d_pk_keys, d_pk_down, d_pk_up, d_out):
    es = ExitStack()
    with es:
        def sb(name, shape, dt=F32, stack=es):
            return stack.enter_context(nc.sbuf_tensor(name, shape, dt))

        def sem(name):
            return es.enter_context(nc.semaphore(name))

        ps = es.enter_context(nc.psum_tensor("ps", [P, 8, BANK], F32))

        xs = sb("xs", [P, TILES, D])
        G = sb("G", [P, BATCH, 3, FLAT])
        VW = sb("VW", [P, BATCH, 3, CHUNKS * D])
        far_row = sb("far_row", [1, BATCH, CTX], BF16)
        bo_row = sb("bo_row", [1, D])
        bg = sb("bg", [P, EXPERTS])
        col_sb = sb("col_sb", [P, 3])
        tg = sb("tg", [P, 4])
        ident = sb("ident", [P, P])
        ones_row = sb("ones_row", [1, P])
        ones_bf = sb("ones_bf", [1, P], BF16)
        wqkv = sb("wqkv", [P, 3 * D])
        bqkv = sb("bqkv", [P, 3 * D])
        wo_f = sb("wo_f", [P, D])
        bout_g = sb("bout_g", [1, D])
        wg = sb("wg", [P, EXPERTS])
        we = sb("we", [P, EXPERTS * D])
        wc = sb("wc", [P, 2 * PH * KEYS])
        down = sb("down", [P, GRID])
        up = sb("up", [P, GRID // P, D])

        def bank(n, cols=BANK):
            return ps[:, n, 0:cols]


        with ExitStack() as tmp:
            def scratch(name, shape, dt=F32):
                return tmp.enter_context(nc.sbuf_tensor(name, shape, dt))

            row_sb = scratch("row_sb", [P, ROW_TOTAL])

            def row(name):
                a, b = ROWS[name]
                return row_sb[:, a:b]

            cbuf = scratch("cbuf", [CD, 2 * P + CTX])
            wk0 = scratch("wk0", [CD, 4 * P])
            wqt0 = scratch("wqt0", [HD0, UNIT, D])
            wvt0 = scratch("wvt0", [HD0, UNIT, CD])
            wout0 = scratch("wout0", [HD0, UNIT, D])
            wk1 = scratch("wk1", [CD, D])
            wqt1 = scratch("wqt1", [P, D])
            wvt1 = scratch("wvt1", [P, CD])
            wo1 = scratch("wo1", [P, D])
            f_wdt = scratch("f_wdt", [64, D])
            f_wup = scratch("f_wup", [64, 2 * D])
            f_bd = scratch("f_bd", [64, P])
            pk_wq = scratch("pk_wq", [PK, 2 * PH, D])
            pk_keys = scratch("pk_keys", [PK, 2 * PH, KEYS])
            blk = scratch("blk", [P, 2 * UNIT])
            cw = scratch("cw", [CD, 3, UNIT * D])
            kt0 = scratch("kt0", [HD0, UNIT, CTX])
            kt1 = scratch("kt1", [P, CTX])
            by_head = scratch("by_head", [P, 2 * UNIT * CTX])
            wo_blk = by_head[:, 0:2 * UNIT * D].rearrange("p (h n) -> p h n", n=D)
            k_blk = by_head[:, :].rearrange("p (h m) -> p h m", m=CTX)
            mask8 = scratch("mask8", [P, BATCH, CTX], U8)

            ctx_in, small, wt, xt_in = sem("ctx_in"), sem("loaded_small"), sem("loaded_weights"), sem("loaded_x")
            V = Steps(sem("fold_v"), "wq bq bout bo bg wg we far_row wo_blk wdu bkv wc down up")
            A = Steps(sem("fold_a"), "tanh cw0 cw1")
            T = Steps(sem("fold_t"), "wdu wc cw0 cw1")
            I = Steps(sem("const_p"), "z1 z2 o1 o2 eye b1 b2")
            BT = Steps(sem("ctx_t"), "k u0 u1 u2")
            BV = Steps(sem("ctx_v"), "kt1 k_blk vw0 vw1 vw2")
            BA = Steps(sem("ctx_a"), "kt0 g0 g1 g2")
            NS, NW = 10, 11

            block = tmp.enter_context(nc.Block())

            @block.sync
            def _(sp):
                sp.dma_start(row_sb[:, :], d_rows).then_inc(small, 16)
                sp.dma_start(col_sb[:, :], d_cols).then_inc(small, 16)
                sp.dma_start(mask8[:, :, :], d_mask).then_inc(small, 16)
                sp.dma_start(f_wdt[:, :], d_f_wdt).then_inc(small, 16)
                sp.dma_start(f_wup[:, :], d_f_wup).then_inc(small, 16)
                sp.dma_start(f_bd[:, :], d_f_bd).then_inc(small, 16)
                sp.dma_start(pk_wq[:, :, :], d_pk_wq).then_inc(small, 16)
                sp.dma_start(pk_keys[:, :, :], d_pk_keys).then_inc(small, 16)
                sp.dma_start(wqkv[:, 0:D], d_f_wq).then_inc(small, 16)
                sp.dma_start(wg[:, :], d_f_wg).then_inc(small, 16)
                with sp.Fori(0, BATCH) as b:
                    sp.wait_ge(BT.sem, b * len(BT.names))
                    sp.dma_start(cbuf[:, :], d_ctx_t[bass.ds(b, 1), :, :].rearrange("a c m -> (a c) m"))\
                        .then_inc(ctx_in, 16)
                sp.wait_ge(xt_in, 32)

            @block.scalar
            def _(act):
                act.dma_start(wvt0[:, :, :], d_wvt0).then_inc(wt, 16)
                act.dma_start(wout0[:, :, :], d_wout0).then_inc(wt, 16)
                act.dma_start(wvt1[:, :], d_wvt1).then_inc(wt, 16)
                act.dma_start(wo1[:, :], d_wo1).then_inc(wt, 16)
                act.dma_start(wk0[:, :], d_wk0).then_inc(wt, 16)
                act.dma_start(wqt0[:, :, :], d_wqt0).then_inc(wt, 16)
                act.dma_start(wk1[:, :], d_wk1).then_inc(wt, 16)
                act.dma_start(wqt1[:, :], d_wqt1).then_inc(wt, 16)
                act.dma_start(we[:, :], d_f_we).then_inc(wt, 16)
                act.dma_start(down[:, :], d_pk_down).then_inc(wt, 16)
                act.dma_start(up[:, :, :], d_pk_up).then_inc(wt, 16)
                act.dma_start(wo_f[:, :], d_f_wo).then_inc(xt_in, 16)
                act.dma_start(xs[:, :, :], d_x).then_inc(xt_in, 16)
                act.wait_ge(small, 16 * NS)
                act.activation(tg[:, 0:2], row("gx"), ACT.Tanh)
                act.activation(tg[:, 2:4], row("gf"), ACT.Tanh).then_inc(A("tanh"), 1)
                act.wait_ge(A.sem, A.after("tanh", 0))
                act.wait_ge(T.sem, T.after("cw0", 0))
                act.activation(cw[:, 0, :], ps[0:CD, 2:4, :], ACT.Copy, scale=tg[0:CD, 0:1]).then_inc(A("cw0"), 1)
                act.wait_ge(T.sem, T.after("cw1", 0))
                act.activation(cw[:, 1:3, :].rearrange("p u n -> p (u n)"), ps[0:CD, 4:8, :], ACT.Copy,
                               scale=tg[0:CD, 1:2]).then_inc(A("cw1"), 1)
                with act.Fori(0, BATCH) as b:
                    act.wait_ge(BT.sem, BT.after("k", b))
                    act.activation(kt0[:, 0:6, :].rearrange("p (k h) m -> p k (h m)", k=2), ps[0:HD0, 0:2, 0:3 * CTX],
                                   ACT.Copy, scale=HD0 ** -0.5)
                    act.activation(kt0[:, 6:8, :].rearrange("p h m -> p (h m)"), ps[0:HD0, 2, 0:2 * CTX], ACT.Copy,
                                   scale=HD0 ** -0.5).then_inc(BA("kt0"), 1)
                    for u in range(3):
                        act.wait_ge(BT.sem, BT.after(f"u{u}", b))
                        act.activation(G[:, bass.ds(b, 1), u, 0:6 * CTX].rearrange("p a (k n) -> p (a k) n", k=2),
                                       ps[:, 2:4, 0:3 * CTX], ACT.Copy)
                        act.activation(G[:, bass.ds(b, 1), u, 6 * CTX:FLAT], ps[:, 4:5, 0:2 * CTX], ACT.Copy)\
                            .then_inc(BA(f"g{u}"), 1)

            @block.gpsimd
            def _(pool):
                pool.memset(ident[:, :], 0.0).then_inc(I("z1"), 1)
                pool.memset(blk[:, :], 1.0).then_inc(I("z2"), 1)
                pool.memset(ones_row[:, :], 1.0).then_inc(I("o1"), 1)
                pool.memset(ones_bf[:, :], 1.0).then_inc(I("o2"), 1)
                pool.wait_ge(I.sem, I.after("z1", 0))
                pool.affine_select(out=ident[:, :], in_=ident[:, :], compare_op=ALU.not_equal, fill=1.0, base=0,
                                   pattern=[[-1, P]], channel_multiplier=1).then_inc(I("eye"), 1)
                pool.wait_ge(I.sem, I.after("z2", 0))
                pool.affine_select(out=blk[:, :], in_=blk[:, :], compare_op=ALU.is_ge, fill=0.0, base=0,
                                   pattern=[[-HD1, 2 * UNIT]], channel_multiplier=1).then_inc(I("b1"), 1)
                pool.wait_ge(I.sem, I.after("b1", 0))
                pool.affine_select(out=blk[:, :], in_=blk[:, :], compare_op=ALU.is_ge, fill=0.0, base=HD1 - 1,
                                   pattern=[[HD1, 2 * UNIT]], channel_multiplier=-1).then_inc(I("b2"), 1)

            @block.vector
            def _(dve):
                g1, g2, g3 = col_sb[:, 0:1], col_sb[:, 1:2], col_sb[:, 2:3]
                dve.wait_ge(small, 16 * NS)
                dve.tensor_scalar(wqkv[:, 0:D], wqkv[:, 0:D], g1, FD ** -0.5, ALU.mult, ALU.mult).then_inc(V("wq"), 1)
                dve.tensor_scalar(bqkv[:, 0:D], row("bq"), FD ** -0.5, None, ALU.mult).then_inc(V("bq"), 1)
                dve.wait_ge(A.sem, A.after("tanh", 0))
                dve.tensor_scalar(bout_g[:, :], row_sb[0:1, 0:D], tg[0:1, 0:1], None, ALU.mult)\
                    .then_inc(V("bout"), 1)
                dve.tensor_copy(bo_row[:, :], row("bo")[0:1, :]).then_inc(V("bo"), 1)
                dve.tensor_copy(bg[:, :], row("bg")).then_inc(V("bg"), 1)
                dve.tensor_scalar(wg[:, :], wg[:, :], g2, None, ALU.mult).then_inc(V("wg"), 1)
                dve.wait_ge(wt, 16 * NW)
                dve.tensor_scalar(we[:, :], we[:, :], g2, None, ALU.mult).then_inc(V("we"), 1)
                dve.tensor_scalar(far_row[:, :, :], mask8[0:1, :, :], -1.0, -FAR, ALU.add, ALU.mult)\
                    .then_inc(V("far_row"), 1)
                dve.wait_ge(I.sem, I.after("b2", 0))
                dve.tensor_tensor(wo_blk, wo1[:, :].unsqueeze(1).to_broadcast([P, 2 * UNIT, D]),
                                  blk[:, :].unsqueeze(2).to_broadcast([P, 2 * UNIT, D]), ALU.mult)\
                    .then_inc(V("wo_blk"), 1)
                dve.wait_ge(T.sem, T.after("wdu", 0))
                dve.tensor_scalar(wqkv[:, D:3 * D], ps[:, 0, 0:2 * D], g1, None, ALU.mult).then_inc(V("wdu"), 1)
                dve.tensor_tensor(bqkv[:, D:3 * D], ps[:, 0, 2 * D:4 * D], row("bup"), ALU.add).then_inc(V("bkv"), 1)
                dve.wait_ge(T.sem, T.after("wc", 0))
                dve.tensor_scalar(wc[:, :], ps[:, 1, :], g3, None, ALU.mult).then_inc(V("wc"), 1)
                dve.tensor_scalar(down[:, :], down[:, :], g3, None, ALU.mult).then_inc(V("down"), 1)
                dve.tensor_scalar(up[:, :, :], up[:, :, :], tg[:, 3:4], None, ALU.mult).then_inc(V("up"), 1)
                with dve.Fori(0, BATCH) as b:
                    dve.wait_ge(BT.sem, BT.after("k", b))
                    dve.scalar_tensor_tensor(out=kt1[:, :].unsqueeze(1), in0=ps[:, 3:4, 0:CTX],
                                             scalar=HD1 ** -0.5, in1=mask8[:, bass.ds(b, 1), :], op0=ALU.mult,
                                             op1=ALU.mult).then_inc(BV("kt1"), 1)
                    dve.wait_ge(BV.sem, BV.after("kt1", b))
                    dve.tensor_tensor(k_blk, kt1[:, :].unsqueeze(1).to_broadcast([P, 2 * UNIT, CTX]),
                                      blk[:, :].unsqueeze(2).to_broadcast([P, 2 * UNIT, CTX]), ALU.mult)\
                        .then_inc(BV("k_blk"), 1)
                    for u in range(3):
                        dve.wait_ge(BT.sem, BT.after(f"u{u}", b))
                        dve.tensor_copy(VW[:, bass.ds(b, 1), u, 0:2 * BANK].rearrange("p a (k n) -> p (a k) n", k=2),
                                        ps[:, 5:7, :])
                        dve.tensor_copy(VW[:, bass.ds(b, 1), u, 2 * BANK:CHUNKS * D], ps[:, 7:8, 0:2 * D])\
                            .then_inc(BV(f"vw{u}"), 1)

            @block.tensor
            def _(pe):
                pe.wait_ge(small, 16 * NS)
                pe.matmul(ps[:, 0, 0:2 * D], f_wdt[:, :], f_wup[:, :], start=True, stop=True)
                pe.matmul(ps[:, 0, 2 * D:4 * D], f_bd[:, :], f_wup[:, :], start=True, stop=True).then_inc(T("wdu"), 1)
                for n in range(2 * PH):
                    mm = pe.matmul(ps[:, 1, n * KEYS:(n + 1) * KEYS], pk_wq[:, n, :], pk_keys[:, n, :],
                                   start=True, stop=True)
                mm.then_inc(T("wc"), 1)
                pe.wait_ge(wt, 16 * NW)
                for h in range(UNIT):
                    mm = pe.matmul(ps[0:CD, 2 + h // 4, (h % 4) * D:(h % 4 + 1) * D], wvt0[:, h, :], wout0[:, h, :],
                                   start=True, stop=True)
                mm.then_inc(T("cw0"), 1)
                pe.wait_ge(V.sem, V.after("wo_blk", 0))
                for q in range(4):
                    mm = pe.matmul(ps[0:CD, 4 + q, :], wvt1[:, :], wo_blk[:, 4 * q:4 * q + 4, :], start=True, stop=True)
                mm.then_inc(T("cw1"), 1)
                pe.wait_ge(A.sem, A.after("cw1", 0))
                pe.wait_ge(V.sem, V.after("up", 0))
                with pe.Fori(0, BATCH) as b:
                    pe.wait_ge(ctx_in, (b + 1) * 16)
                    pe.wait_ge(BV.sem, b * len(BV.names))
                    pe.wait_ge(BA.sem, b * len(BA.names))
                    for h in range(UNIT):
                        pe.matmul(ps[0:HD0, h // 3, (h % 3) * CTX:(h % 3 + 1) * CTX],
                                  wk0[:, h * HD0:(h + 1) * HD0], cbuf[:, P:P + CTX], start=True, stop=True)
                    pe.matmul(ps[:, 3, 0:CTX], wk1[:, :], cbuf[:, P:P + CTX], start=True, stop=True)\
                        .then_inc(BT("k"), 1)
                    for u in range(3):
                        if u == 0:
                            pe.wait_ge(BV.sem, BV.after("k_blk", b))
                            pe.wait_ge(BA.sem, BA.after("kt0", b))
                        else:
                            pe.wait_ge(BV.sem, BV.after(f"vw{u - 1}", b))
                            pe.wait_ge(BA.sem, BA.after(f"g{u - 1}", b))
                        for h in range(UNIT):
                            to = ps[:, 2 + h // 3, (h % 3) * CTX:(h % 3 + 1) * CTX]
                            if u == 0:
                                pe.matmul(to, wqt0[:, h, :], kt0[:, h, :], start=True, stop=True)
                            else:
                                pe.matmul(to, wqt1[:, :], k_blk[:, UNIT * (u - 1) + h, :], start=True, stop=True)
                        for c in range(CHUNKS):
                            heads = [h for h in range(UNIT) if h * CTX < (c + 1) * P and (h + 1) * CTX > c * P]
                            for h in heads:
                                off = P + c * P - h * CTX
                                mm = pe.matmul(ps[:, 5 + c // 4, (c % 4) * D:(c % 4 + 1) * D], cbuf[:, off:off + P],
                                               cw[:, u, h * D:(h + 1) * D], start=(h == heads[0]), stop=(h == heads[-1]))
                        mm.then_inc(BT(f"u{u}"), 1)

        xn = [sb(f"xn_{s}", [P, D]) for s in "abcd"]
        xt = [sb(f"xt_{s}", [P, P]) for s in "abcd"]
        stat = sb("stat", [P, 4, 6])
        mv = sb("mv", [P, 4, 2])
        var = sb("var", [P, 4])
        rs = sb("rs", [P, 4])
        half = sb("half", [P, 1])
        carrier = sb("carrier", [P, 10])
        prob_even, prob_odd = sb("prob_even", [P, FLAT]), sb("prob_odd", [P, FLAT])
        prob = [prob_even, prob_odd, prob_even]
        prob_t = sb("prob_t", [P, CHUNKS, P])
        nmax = sb("nmax", [P, 3, UNIT])
        rsum = sb("rsum", [P, 3, UNIT])
        rinv = sb("rinv", [P, 3, UNIT])
        qkv = sb("qkv", [P, 3 * D])
        prod = sb("prod", [P, 2, FH * FH * FD // 2])
        b_sc = sb("b_sc", [P, 8])
        att = sb("att", [P, FH, FH])
        amax = sb("amax", [P, FH])
        asum = sb("asum", [P, FH])
        arec = sb("arec", [P, FH])
        av = sb("av", [P, D])
        av_t = sb("av_t", [P, P])
        x2 = sb("x2", [P, D])
        x2_t = av_t
        sq = sb("sq", [P, D])
        gate = sb("gate", [P, 3, EXPERTS])
        d_sc = sb("d_sc", [P, 8])
        sim = sb("sim", [P, 2 * PH, KEYS])
        rest = sb("rest", [P, 2 * PH, KEYS])
        best = sb("best", [P, 2 * PH, TOP])
        cand = sb("cand", [P, PH, CANDS])
        cbest = sb("cbest", [P, PH, TOP])
        neg1 = sb("neg1", [P, PH])
        cexp = sb("cexp", [P, PH, TOP])
        zsum = sb("zsum", [P, PH])
        zinv = sb("zinv", [P, PH])
        diag = sb("diag", [P, 2, P])
        NSUM, NEXP = 2, 2
        sums = sb("sums", [P, NSUM, KEYS, KEYS])
        wexp = sb("wexp", [P, NEXP, GRID])
        gel = sb("gel", [P, GRID // P, P])

        A_, B_, C_, D_ = 0, 1, 2, 3
        LAG = [0, 1, 2, 3]
        LV = [Steps(sem("ln_a_v"), "stats aggr eps xn"), Steps(sem("b_v"),
              "stats aggr eps vr vr2 xn qkv qk0 qk1 amax asub asum arec av0 av1 anorm x2 eps3 glog gmax grec "
              "gates y0 y1 y2 y3 y4 y5 y6 y7 res"), Steps(sem("ln_c_v"), "stats aggr eps xn"),
              Steps(sem("d_v"), "stats aggr eps vr n2 sc xn ta tr tb cand ca cr cb nv vs vsum vrec "
                    "g0 m0 g1 m1 g2 m2 g3 m3 g4 m4 g5 m5 g6 m6 g7 m7 gw fin")]
        LP = [Steps(sem("ln_a_p"), "pow"), Steps(sem("b_p"), "pow pow2 qk0 qk1 av0 av1 pow3"),
              Steps(sem("ln_c_p"), "pow"), Steps(sem("d_p"), "pow pow2 s0 s1 s2 s3 s4 s5 s6 s7")]
        LA = [Steps(sem("ln_a_a"), "xt"), Steps(sem("b_a"), "xt aexp avt sq x2t gexp"), Steps(sem("ln_c_a"), "xt"),
              Steps(sem("d_a"), "xt sim gel0 gel1 vexp e0 e1 e2 e3 e4 e5 e6 e7")]
        LT = [Steps(sem("ln_a_t"), "xt"), Steps(sem("b_t"), "xt qkv avt att x2t gate y0 y1"),
              Steps(sem("ln_c_t"), "xt"),
              Steps(sem("d_t"), "xt sim ht0 ht1 w0 w1 w2 w3 w4 w5 w6 w7 out")]
        UV = [Steps(sem(f"unit{u}_v"), "max rec res") for u in range(3)]
        UP = [Steps(sem(f"unit{u}_p"), "norm") for u in range(3)]
        UA = [Steps(sem(f"unit{u}_a"), "exp pt0 pt1 pt2") for u in range(3)]
        UT = [Steps(sem(f"unit{u}_t"), "sc pt0 pt1 pt2 out") for u in range(3)]
        stored = sem("stored")
        const = Steps(sem("const_v"), "half")
        UNIT_STAGE = [A_, C_, C_]
        B4, B5, BT7, B3 = 4, 5, 7, 3

        def slot(h):
            return h % NSUM

        def tile_of(i, stage):
            return i - LAG[stage]

        def on(i, stage):
            return not isinstance(i, int) or 0 <= i - LAG[stage] < TILES

        def x_of(t):
            return xs[:, t, :] if isinstance(t, int) else xs[:, bass.ds(t, 1), :].rearrange("p a d -> p (a d)")

        def batch_of(t):
            return t // PER_BATCH

        def wait(eng, steps, name, t):
            if not isinstance(t, int) or t >= 0:
                eng.wait_ge(steps.sem, steps.after(name, t))

        def bodies(eng, body):
            for i in range(LAG[-1] + 1):
                body(i)
            with eng.Fori(LAG[-1] + 1, TILES) as i:
                body(i)
            for i in range(TILES, TILES + LAG[-1]):
                body(i)

        def before_unit(u, i):
            for back in range(1, 4):
                n = u - back
                w, j = (n, i) if n >= 0 else (n + 3, i - 1)
                if on(j, UNIT_STAGE[w]):
                    return w, tile_of(j, UNIT_STAGE[w])
            return None, None

        block = es.enter_context(nc.Block())

        @block.sync
        def _(sp):
            def body(i):
                if on(i, D_):
                    t = tile_of(i, D_)
                    wait(sp, LV[D_], "fin", t)
                    dst = d_out[t, :, :] if isinstance(t, int) else \
                        d_out[bass.ds(t, 1), :, :].rearrange("a p d -> (a p) d")
                    sp.dma_start(dst, x_of(t)).then_inc(stored, 16)
            bodies(sp, body)
            sp.wait_ge(stored, 16 * TILES)

        @block.gpsimd
        def _(pool):
            def power(s, step, out_, in_, t):
                pool.wait_ge(const.sem, 1)
                pool.tensor_tensor(out_, in_, half[:, :], ALU.pow).then_inc(LP[s](step), 1)

            def rsqrt_var(s, i):
                t = tile_of(i, s)
                wait(pool, LV[s], "eps", t)
                power(s, "pow", rs[:, s:s + 1], var[:, s:s + 1], t)

            def norm(u, i):
                t = tile_of(i, UNIT_STAGE[u])
                wait(pool, UA[u], "exp", t)
                wait(pool, UV[u], "rec", t)
                pr = prob[u][:, :].rearrange("p (h m) -> p h m", m=CTX)
                pool.tensor_tensor(pr, pr, rinv[:, u, :].unsqueeze(2).to_broadcast([P, UNIT, CTX]), ALU.mult)\
                    .then_inc(UP[u]("norm"), 1)

            def b_qk(half_, t):
                wait(pool, LV[B_], "qkv", t)
                wait(pool, LV[B_], f"av{half_}", t - 1)
                n = FH // 2
                q = qkv[:, half_ * n * FD:(half_ + 1) * n * FD].rearrange("p (h d) -> p h d", d=FD)
                k = qkv[:, D:3 * D].rearrange("p (g e) -> p g e", e=2 * FD)[:, :, 0:FD]
                o = prod[:, half_, :].rearrange("p (h g d) -> p h g d", g=FH, d=FD)
                pool.tensor_tensor(o, q.unsqueeze(2).to_broadcast([P, n, FH, FD]),
                                   k.unsqueeze(1).to_broadcast([P, n, FH, FD]), ALU.mult)\
                    .then_inc(LP[B_](f"qk{half_}"), 1)

            def b_av(half_, t):
                wait(pool, LA[B_], "aexp", t)
                wait(pool, LV[B_], f"qk{half_}", t)
                n = FH // 2
                w = att[:, half_ * n:(half_ + 1) * n, :]
                v = qkv[:, D:3 * D].rearrange("p (g e) -> p e g", e=2 * FD)[:, FD:2 * FD, :]
                o = prod[:, half_, :].rearrange("p (h d g) -> p h d g", g=FH, d=FD)
                pool.tensor_tensor(o, w.unsqueeze(2).to_broadcast([P, n, FD, FH]),
                                   v.unsqueeze(1).to_broadcast([P, n, FD, FH]), ALU.mult)\
                    .then_inc(LP[B_](f"av{half_}"), 1)

            def d_sums(h, t):
                if h == 0:
                    wait(pool, LA[D_], "sim", t)
                if h >= NSUM:
                    wait(pool, LV[D_], f"m{h - NSUM}", t)
                else:
                    last = h + (PH - 1 - h) // NSUM * NSUM
                    wait(pool, LV[D_], f"m{last}", t - 1)
                buf = slot(h)
                pool.tensor_tensor(sums[:, buf, :, :],
                                   sim[:, h, :].unsqueeze(2).to_broadcast([P, KEYS, KEYS]),
                                   sim[:, PH + h, :].unsqueeze(1).to_broadcast([P, KEYS, KEYS]), ALU.add)\
                    .then_inc(LP[D_](f"s{h}"), 1)

            def body(i):
                ta, tb, tc, td = (tile_of(i, s) for s in range(4))
                if on(i, A_):
                    rsqrt_var(A_, i)
                if on(i, C_):
                    rsqrt_var(C_, i)
                if on(i, D_):
                    rsqrt_var(D_, i)
                if on(i, B_):
                    rsqrt_var(B_, i)
                if on(i, D_):
                    wait(pool, LV[D_], "n2", td)
                    power(D_, "pow2", d_sc[:, 1:2], d_sc[:, 0:1], td)
                if on(i, B_):
                    wait(pool, LV[B_], "vr2", tb)
                    power(B_, "pow2", b_sc[:, 1:2], b_sc[:, 0:1], tb)
                    b_qk(0, tb)
                    b_qk(1, tb)
                if on(i, A_):
                    norm(0, i)
                if on(i, D_):
                    d_sums(0, td)
                    d_sums(1, td)
                if on(i, B_):
                    b_av(0, tb)
                    b_av(1, tb)
                if on(i, C_):
                    norm(1, i)
                if on(i, D_):
                    d_sums(2, td)
                    d_sums(3, td)
                if on(i, B_):
                    wait(pool, LV[B_], "eps3", tb)
                    power(B_, "pow3", b_sc[:, 4:5], b_sc[:, 3:4], tb)
                if on(i, D_):
                    d_sums(4, td)
                if on(i, C_):
                    norm(2, i)
                if on(i, D_):
                    d_sums(5, td)
                    d_sums(6, td)
                    d_sums(7, td)
            bodies(pool, body)

        @block.scalar
        def _(act):
            def turned(s, i, b):
                t = tile_of(i, s)
                wait(act, LT[s], "xt", t)
                act.activation(xt[s][:, :], bank(b, P), ACT.Copy).then_inc(LA[s]("xt"), 1)

            def exps(u, i):
                t = tile_of(i, UNIT_STAGE[u])
                wait(act, UV[u], "max", t)
                if u == 0:
                    wait(act, UT[2], "pt2", tile_of(i, C_) - 1)
                    if isinstance(i, int):
                        wait(act, UT[0], "pt2", t - 1)
                elif u == 1:
                    wait(act, UT[1], "pt2", t - 1)
                elif on(i, A_):
                    wait(act, UT[0], "pt2", i)
                else:
                    wait(act, UT[2], "pt2", t - 1)
                for h in range(UNIT):
                    ins = act.activation(prob[u][:, h * CTX:(h + 1) * CTX],
                                         ps[:, h // 3, (h % 3) * CTX:(h % 3 + 1) * CTX], ACT.Exp,
                                         bias=nmax[:, u, h:h + 1], accum_out=rsum[:, u, h:h + 1])
                ins.then_inc(UA[u]("exp"), 1)

            def prob_out(u, i):
                t = tile_of(i, UNIT_STAGE[u])
                for r in range(3):
                    wait(act, UT[u], f"pt{r}", t)
                    n = min(4, CHUNKS - 4 * r)
                    act.activation(prob_t[:, 4 * r:4 * r + n, :], bank(BT7, n * P).rearrange("p (c n) -> p c n", n=P),
                                   ACT.Copy).then_inc(UA[u](f"pt{r}"), 1)

            def d_exp(h, t):
                wait(act, LP[D_], f"s{h}", t)
                if h == 0:
                    wait(act, LV[D_], "nv", t)
                if h >= NEXP:
                    wait(act, LT[D_], f"w{h - NEXP}", t)
                act.activation(wexp[:, h % NEXP, :], sums[:, slot(h), :, :].rearrange("p a b -> p (a b)"), ACT.Exp,
                               bias=neg1[:, h:h + 1]).then_inc(LA[D_](f"e{h}"), 1)

            def body(i):
                ta, tb, tc, td = (tile_of(i, s) for s in range(4))
                if on(i, A_):
                    turned(A_, i, BT7)
                if on(i, C_):
                    turned(C_, i, BT7)
                if on(i, D_):
                    turned(D_, i, B4)
                if on(i, B_):
                    turned(B_, i, B3)
                if on(i, D_):
                    wait(act, LT[D_], "sim", td)
                    act.activation(sim[:, :, :], bank(B4).rearrange("p (n k) -> p n k", k=KEYS), ACT.Copy)\
                        .then_inc(LA[D_]("sim"), 1)
                    for r in range(2):
                        wait(act, LT[D_], f"ht{r}", td)
                        wait(act, LT[D_], "out", td - 1)
                        act.activation(gel[:, 4 * r:4 * r + 4, :], bank(B4).rearrange("p (c n) -> p c n", n=P),
                                       ACT.Gelu).then_inc(LA[D_](f"gel{r}"), 1)
                if on(i, A_):
                    exps(0, i)
                if on(i, B_):
                    wait(act, LV[B_], "asub", tb)
                    act.activation(att[:, :, :], att[:, :, :], ACT.Exp).then_inc(LA[B_]("aexp"), 1)
                if on(i, C_):
                    exps(1, i)
                if on(i, A_):
                    prob_out(0, i)
                if on(i, D_):
                    wait(act, LV[D_], "vs", td)
                    act.activation(cexp[:, :, :], cexp[:, :, :], ACT.Exp).then_inc(LA[D_]("vexp"), 1)
                    d_exp(0, td)
                    d_exp(1, td)
                if on(i, B_):
                    wait(act, LT[B_], "avt", tb)
                    act.activation(av_t[:, :], bank(B3, P), ACT.Copy).then_inc(LA[B_]("avt"), 1)
                if on(i, B_):
                    wait(act, LV[B_], "x2", tb)
                    act.activation(sq[:, :], x2[:, :], ACT.Square, accum_out=b_sc[:, 2:3]).then_inc(LA[B_]("sq"), 1)
                if on(i, C_):
                    exps(2, i)
                    prob_out(1, i)
                if on(i, B_):
                    wait(act, LT[B_], "x2t", tb)
                    act.activation(x2_t[:, :], bank(B3, P), ACT.Copy).then_inc(LA[B_]("x2t"), 1)
                if on(i, D_):
                    d_exp(2, td)
                    d_exp(3, td)
                if on(i, B_):
                    wait(act, LV[B_], "gmax", tb)
                    act.activation(gate[:, 1, :], gate[:, 0, :], ACT.Exp, bias=b_sc[:, 5:6],
                                   accum_out=b_sc[:, 6:7]).then_inc(LA[B_]("gexp"), 1)
                if on(i, D_):
                    d_exp(4, td)
                    d_exp(5, td)
                if on(i, C_):
                    prob_out(2, i)
                if on(i, D_):
                    d_exp(6, td)
                    d_exp(7, td)
            bodies(act, body)

        @block.tensor
        def _(pe):
            def turn(s, i, b):
                t = tile_of(i, s)
                wait(pe, LV[s], "xn", t)
                if s == A_:
                    free7(0, i)
                elif s == C_:
                    if on(i, A_):
                        wait(pe, LA[A_], "xt", tile_of(i, A_))
                    else:
                        free7(0, i)
                elif s == B_:
                    wait(pe, LV[B_], "y7", t - 1)
                else:
                    wait(pe, LV[D_], "fin", t - 1)
                pe.transpose(bank(b, P), xn[s][:, :], ident[:, :]).then_inc(LT[s]("xt"), 1)

            def free7(u, i):
                w, j = before_unit(u, i)
                if w is not None:
                    wait(pe, UV[w], "res", j)

            def scores(u, i):
                s = UNIT_STAGE[u]
                t = tile_of(i, s)
                wait(pe, LA[s], "xt", t)
                w, j = before_unit(u, i)
                if w is not None:
                    wait(pe, UA[w], "exp", j)
                b = batch_of(t)
                at = 0
                for k, heads in enumerate(BANK_HEADS):
                    n = heads * CTX
                    rhs = G[:, b, u, at:at + n] if isinstance(b, int) else \
                        G[:, bass.ds(b, 1), u, at:at + n].rearrange("p a n -> p (a n)")
                    mm = pe.matmul(bank(k, n), xt[s][:, :], rhs, start=True, stop=(s == A_))
                    if s == C_:
                        far = far_row[:, b:b + 1, :] if isinstance(b, int) else far_row[:, bass.ds(b, 1), :]
                        mm = pe.matmul(bank(k, n).rearrange("p (h m) -> p h m", m=CTX), ones_bf[:, :],
                                       far.to_broadcast([1, heads, CTX]), start=False, stop=True)
                    at += n
                mm.then_inc(UT[u]("sc"), 1)

            def values(u, i):
                s = UNIT_STAGE[u]
                t = tile_of(i, s)
                wait(pe, UP[u], "norm", t)
                for r in range(3):
                    if r == 0:
                        free7(u, i)
                        for s2 in (A_, C_):
                            if on(i, s2):
                                wait(pe, LA[s2], "xt", tile_of(i, s2))
                    else:
                        wait(pe, UA[u], f"pt{r - 1}", t)
                    for c in range(4 * r, min(4 * r + 4, CHUNKS)):
                        n = min(P, FLAT - c * P)
                        mm = pe.transpose(ps[0:n, BT7, (c % 4) * P:(c % 4 + 1) * P], prob[u][:, c * P:c * P + n],
                                          ident[:, :])
                    mm.then_inc(UT[u](f"pt{r}"), 1)
                wait(pe, UA[u], "pt2", t)
                b = batch_of(t)
                if s == A_:
                    pe.matmul(bank(BT7, D), ones_row[:, :], bout_g[:, :], start=True, stop=False)
                for c in range(CHUNKS):
                    n = min(P, FLAT - c * P)
                    rhs = VW[0:n, b, u, c * D:(c + 1) * D] if isinstance(b, int) else \
                        VW[0:n, bass.ds(b, 1), u, c * D:(c + 1) * D].rearrange("p a n -> p (a n)")
                    mm = pe.matmul(bank(BT7, D), prob_t[0:n, c, :], rhs, start=(c == 0 and s != A_),
                                   stop=(c == CHUNKS - 1))
                mm.then_inc(UT[u]("out"), 1)

            def d_weights(h, t):
                wait(pe, LV[D_], f"m{h}", t)
                if h == 0:
                    wait(pe, LV[D_], "gw", t - 1)
                for c in range(GRID // P):
                    mm = pe.matmul(ps[:, B5 + c // 4, (c % 4) * P:(c % 4 + 1) * P],
                                   wexp[:, h % NEXP, c * P:(c + 1) * P], diag[:, h % 2, :],
                                   start=(h == 0 and c % 4 == 0), stop=(h == PH - 1), skip_group_check=True)
                mm.then_inc(LT[D_](f"w{h}"), 1)

            def b_y(r, t):
                if r == 0:
                    wait(pe, LV[B_], "glog", t)
                else:
                    wait(pe, LV[B_], "y3", t)
                pe.matmul(bank(B3), x2_t[:, :], we[:, r * BANK:(r + 1) * BANK], start=True, stop=True)\
                    .then_inc(LT[B_](f"y{r}"), 1)

            def body(i):
                ta, tb, tc, td = (tile_of(i, s) for s in range(4))
                if on(i, A_):
                    turn(A_, i, BT7)
                if on(i, C_):
                    turn(C_, i, BT7)
                if on(i, D_):
                    turn(D_, i, B4)
                if on(i, B_):
                    turn(B_, i, B3)
                if on(i, A_):
                    scores(0, i)
                if on(i, D_):
                    wait(pe, LA[D_], "xt", td)
                    pe.matmul(bank(B4), xt[D_][:, :], wc[:, :], start=True, stop=True).then_inc(LT[D_]("sim"), 1)
                if on(i, B_):
                    wait(pe, LA[B_], "xt", tb)
                    pe.matmul(bank(B3, 3 * D), xt[B_][:, :], wqkv[:, :], start=True, stop=True)\
                        .then_inc(LT[B_]("qkv"), 1)
                if on(i, D_):
                    for r in range(2):
                        wait(pe, LA[D_], "gel0" if r else "sim", td)
                        for c in range(4):
                            mm = pe.matmul(ps[:, B4, c * P:(c + 1) * P], down[:, (4 * r + c) * P:(4 * r + c + 1) * P],
                                           xt[D_][:, :], start=True, stop=True)
                        mm.then_inc(LT[D_](f"ht{r}"), 1)
                if on(i, C_):
                    scores(1, i)
                if on(i, A_):
                    values(0, i)
                if on(i, B_):
                    wait(pe, LV[B_], "anorm", tb)
                    pe.transpose(bank(B3, P), av[:, :], ident[:, :]).then_inc(LT[B_]("avt"), 1)
                    wait(pe, LA[B_], "avt", tb)
                    pe.matmul(bank(B3, D), ones_row[:, :], bo_row[:, :],
                              start=True, stop=False)
                    pe.matmul(bank(B3, D), av_t[:, :], wo_f[:, :], start=False, stop=True)\
                        .then_inc(LT[B_]("att"), 1)
                if on(i, C_):
                    scores(2, i)
                if on(i, D_):
                    d_weights(0, td)
                if on(i, C_):
                    values(1, i)
                if on(i, D_):
                    d_weights(1, td)
                if on(i, B_):
                    wait(pe, LV[B_], "x2", tb)
                    pe.transpose(bank(B3, P), x2[:, :], ident[:, :]).then_inc(LT[B_]("x2t"), 1)
                    wait(pe, LA[B_], "x2t", tb)
                    pe.matmul(bank(B3, EXPERTS), x2_t[:, :], wg[:, :], start=True, stop=True)\
                        .then_inc(LT[B_]("gate"), 1)
                if on(i, D_):
                    d_weights(2, td)
                if on(i, B_):
                    b_y(0, tb)
                if on(i, D_):
                    d_weights(3, td)
                    d_weights(4, td)
                if on(i, C_):
                    values(2, i)
                if on(i, B_):
                    b_y(1, tb)
                if on(i, D_):
                    d_weights(5, td)
                    d_weights(6, td)
                    d_weights(7, td)
                    wait(pe, LV[D_], "gw", td)
                    wait(pe, LA[D_], "gel1", td)
                    for c in range(GRID // P):
                        mm = pe.matmul(bank(B4, D), gel[:, c, :], up[:, c, :], start=(c == 0),
                                       stop=(c == GRID // P - 1))
                    mm.then_inc(LT[D_]("out"), 1)
            bodies(pe, body)

        @block.vector
        def _(dve):
            dve.memset(half[:, :], -0.5).then_inc(const("half"), 1)

            def carry(n):
                dve.memset(carrier[:, n:n + 1], 0.0)

            def moments(s, i, eps):
                t = tile_of(i, s)
                if s == B_:
                    wait(dve, UV[0], "res", t)
                if s == C_:
                    wait(dve, LV[B_], "res", t)
                if s == D_:
                    wait(dve, UV[2], "res", t)
                wait(dve, LV[s], "xn", t - 1)
                dve.bn_stats(stat[:, s, :], x_of(t)).then_inc(LV[s]("stats"), 1)
                wait(dve, LV[s], "stats", t)
                carry(s)
                dve.bn_aggr(mv[:, s, :], stat[:, s, :]).then_inc(LV[s]("aggr"), 1)
                wait(dve, LV[s], "aggr", t)
                dve.tensor_scalar(var[:, s:s + 1], mv[:, s, 1:2], eps, None, ALU.add).then_inc(LV[s]("eps"), 1)

            def normed(s, i, scale):
                t = tile_of(i, s)
                wait(dve, LT[s], "xt", t - 1)
                dve.tensor_scalar(xn[s][:, :], x_of(t), mv[:, s, 0:1], scale, ALU.subtract, ALU.mult)\
                    .then_inc(LV[s]("xn"), 1)

            def unit_max(u, i):
                t = tile_of(i, UNIT_STAGE[u])
                wait(dve, UT[u], "sc", t)
                wait(dve, UA[u], "exp", t - 1)
                dve.tensor_reduce(nmax[:, u, 0:6], ps[:, 0:2, 0:3 * CTX].rearrange("p k (h m) -> p k h m", m=CTX),
                                  X_AXIS, ALU.max, negate=True)
                dve.tensor_reduce(nmax[:, u, 6:8], ps[:, 2, 0:2 * CTX].rearrange("p (h m) -> p h m", m=CTX),
                                  X_AXIS, ALU.max, negate=True).then_inc(UV[u]("max"), 1)

            def unit_rec(u, i):
                t = tile_of(i, UNIT_STAGE[u])
                wait(dve, UA[u], "exp", t)
                wait(dve, UP[u], "norm", t - 1)
                dve.reciprocal(rinv[:, u, :], rsum[:, u, :]).then_inc(UV[u]("rec"), 1)

            def unit_res(u, i):
                s = UNIT_STAGE[u]
                t = tile_of(i, s)
                wait(dve, UT[u], "out", t)
                if u == 2:
                    wait(dve, UV[1], "res", t)
                xx = x_of(t)
                dve.tensor_tensor(xx, xx, bank(BT7, D), ALU.add).then_inc(UV[u]("res"), 1)

            def b_half(name, k, t):
                wait(dve, LP[B_], f"{name}{k}", t)
                n = FH // 2
                if name == "qk":
                    if k == 0:
                        wait(dve, LP[B_], "av1", t - 1)
                    o = att[:, n * k:n * (k + 1), :]
                    src = prod[:, k, :].rearrange("p (h g d) -> p h g d", g=FH, d=FD)
                else:
                    if k == 0:
                        wait(dve, LT[B_], "avt", t - 1)
                    o = av[:, n * FD * k:n * FD * (k + 1)].rearrange("p (h d) -> p h d", d=FD)
                    src = prod[:, k, :].rearrange("p (h d g) -> p h d g", g=FH, d=FD)
                dve.tensor_reduce(o, src, X_AXIS, ALU.add).then_inc(LV[B_](f"{name}{k}"), 1)

            def b_softmax(t):
                wait(dve, LV[B_], "qk1", t)
                dve.tensor_reduce(amax[:, :], att[:, :, :], X_AXIS, ALU.max).then_inc(LV[B_]("amax"), 1)
                wait(dve, LV[B_], "amax", t)
                dve.tensor_tensor(att[:, :, :], att[:, :, :], amax[:, :].unsqueeze(2).to_broadcast([P, FH, FH]),
                                  ALU.subtract).then_inc(LV[B_]("asub"), 1)

            def b_sum(t):
                wait(dve, LA[B_], "aexp", t)
                dve.tensor_reduce(asum[:, :], att[:, :, :], X_AXIS, ALU.add).then_inc(LV[B_]("asum"), 1)
                wait(dve, LV[B_], "asum", t)
                dve.reciprocal(arec[:, :], asum[:, :]).then_inc(LV[B_]("arec"), 1)

            def b_norm(t):
                wait(dve, LV[B_], "av1", t)
                o = av[:, :].rearrange("p (h d) -> p h d", d=FD)
                dve.tensor_tensor(o, o, arec[:, :].unsqueeze(2).to_broadcast([P, FH, FD]), ALU.mult)\
                    .then_inc(LV[B_]("anorm"), 1)

            def b_x2(t):
                wait(dve, LT[B_], "att", t)
                wait(dve, LT[B_], "x2t", t - 1)
                wait(dve, LV[B_], "y7", t - 1)
                dve.tensor_tensor(x2[:, :], xn[B_][:, :], bank(B3, D), ALU.add).then_inc(LV[B_]("x2"), 1)

            def b_gate(t):
                wait(dve, LA[B_], "sq", t)
                dve.tensor_scalar(b_sc[:, 3:4], b_sc[:, 2:3], 1.0 / D, 1e-6, ALU.mult, ALU.add)\
                    .then_inc(LV[B_]("eps3"), 1)

            def b_logits(t):
                wait(dve, LP[B_], "pow3", t)
                wait(dve, LT[B_], "gate", t)
                wait(dve, LA[B_], "gexp", t - 1)
                dve.scalar_tensor_tensor(out=gate[:, 0, :], in0=bank(B3, EXPERTS), scalar=b_sc[:, 4:5], in1=bg[:, :],
                                         op0=ALU.mult, op1=ALU.add).then_inc(LV[B_]("glog"), 1)
                wait(dve, LV[B_], "glog", t)
                dve.tensor_reduce(b_sc[:, 5:6], gate[:, 0, :], X_AXIS, ALU.max, negate=True)\
                    .then_inc(LV[B_]("gmax"), 1)

            def b_gates(t):
                wait(dve, LA[B_], "gexp", t)
                dve.reciprocal(b_sc[:, 7:8], b_sc[:, 6:7]).then_inc(LV[B_]("grec"), 1)
                wait(dve, LV[B_], "grec", t)
                dve.tensor_scalar(gate[:, 2, :], gate[:, 1, :], b_sc[:, 7:8], b_sc[:, 4:5], ALU.mult, ALU.mult)\
                    .then_inc(LV[B_]("gates"), 1)

            def b_experts(r, t):
                wait(dve, LT[B_], f"y{r}", t)
                for e in range(4 * r, 4 * r + 4):
                    wait(dve, LV[B_], f"y{e - 1}" if e else "gates", t)
                    dve.scalar_tensor_tensor(out=x2[:, :], in0=bank(B3)[:, (e % 4) * D:(e % 4 + 1) * D],
                                             scalar=gate[:, 2, e:e + 1], in1=x2[:, :], op0=ALU.mult, op1=ALU.add)\
                        .then_inc(LV[B_](f"y{e}"), 1)

            def b_res(t):
                wait(dve, LV[B_], "y7", t)
                xx = x_of(t)
                dve.scalar_tensor_tensor(out=xx, in0=x2[:, :], scalar=tg[:, 2:3], in1=xx, op0=ALU.mult, op1=ALU.add)\
                    .then_inc(LV[B_]("res"), 1)

            def d_top(part, t, lists):
                for n in lists:
                    if part == "ta":
                        ins = dve.max(best[:, n, 0:8], sim[:, n, :])
                    elif part == "tr":
                        ins = dve.match_replace(rest[:, n, :], best[:, n, 0:8], sim[:, n, :], LOW)
                    else:
                        ins = dve.max(best[:, n, 8:16], rest[:, n, :])
                return ins

            def d_ctop(part, t):
                for h in range(PH):
                    if part == "ca":
                        ins = dve.max(cbest[:, h, 0:8], cand[:, h, :])
                    elif part == "cr":
                        ins = dve.match_replace(cand[:, h, :], cbest[:, h, 0:8], cand[:, h, :], LOW)
                    else:
                        ins = dve.max(cbest[:, h, 8:16], cand[:, h, :])
                ins.then_inc(LV[D_](part), 1)

            def d_cands(t):
                wait(dve, LV[D_], "tb", t)
                at, i = 0, 0
                while i < TOP:
                    n = STAIRS[i]
                    k = sum(1 for m in STAIRS if m == n)
                    o = cand[:, :, at:at + k * n].rearrange("p h (i j) -> p h i j", j=n)
                    ins = dve.tensor_tensor(o, best[:, 0:PH, i:i + k].unsqueeze(3).to_broadcast([P, PH, k, n]),
                                            best[:, PH:2 * PH, 0:n].unsqueeze(2).to_broadcast([P, PH, k, n]), ALU.add)
                    at += k * n
                    i += k
                ins.then_inc(LV[D_]("cand"), 1)

            def d_mask(h, t):
                if h == 0:
                    wait(dve, LV[D_], "vrec", t)
                if h >= 2:
                    wait(dve, LT[D_], f"w{h - 2}", t)
                else:
                    wait(dve, LT[D_], f"w{h + PH - 2}", t - 1)
                dve.tensor_scalar(diag[:, h % 2, :], ident[:, :], zinv[:, h:h + 1], None, ALU.mult)\
                    .then_inc(LV[D_](f"g{h}"), 1)
                wait(dve, LA[D_], f"e{h}", t)
                if h == 0:
                    wait(dve, LV[D_], "cb", t)
                wx = wexp[:, h % NEXP, :]
                dve.scalar_tensor_tensor(out=wx, in0=sums[:, slot(h), :, :].rearrange("p a b -> p (a b)"),
                                         scalar=cbest[:, h, TOP - 1:TOP], in1=wx, op0=ALU.is_ge, op1=ALU.mult)\
                    .then_inc(LV[D_](f"m{h}"), 1)

            def body(i):
                ta, tb, tc, td = (tile_of(i, s) for s in range(4))
                if on(i, A_):
                    moments(A_, i, 1e-5)
                if on(i, C_):
                    moments(C_, i, 1e-5)
                if on(i, D_):
                    moments(D_, i, 1e-5)
                if on(i, B_):
                    moments(B_, i, 1e-5)
                if on(i, A_):
                    wait(dve, LP[A_], "pow", ta)
                    normed(A_, i, rs[:, A_:A_ + 1])
                if on(i, C_):
                    wait(dve, LP[C_], "pow", tc)
                    normed(C_, i, rs[:, C_:C_ + 1])
                if on(i, D_):
                    wait(dve, LP[D_], "pow", td)
                    dve.tensor_scalar(d_sc[:, 2:3], mv[:, D_, 1:2], rs[:, D_:D_ + 1], rs[:, D_:D_ + 1], ALU.mult,
                                      ALU.mult).then_inc(LV[D_]("vr"), 1)
                    wait(dve, LV[D_], "vr", td)
                    dve.tensor_scalar(d_sc[:, 0:1], d_sc[:, 2:3], float(D), 1e-24, ALU.mult, ALU.max)\
                        .then_inc(LV[D_]("n2"), 1)
                if on(i, B_):
                    wait(dve, LP[B_], "pow", tb)
                    dve.tensor_scalar(b_sc[:, 2:3], mv[:, B_, 1:2], rs[:, B_:B_ + 1], rs[:, B_:B_ + 1], ALU.mult,
                                      ALU.mult).then_inc(LV[B_]("vr"), 1)
                    wait(dve, LV[B_], "vr", tb)
                    dve.tensor_scalar(b_sc[:, 0:1], b_sc[:, 2:3], 1e-6, None, ALU.add).then_inc(LV[B_]("vr2"), 1)
                    normed(B_, i, rs[:, B_:B_ + 1])
                if on(i, D_):
                    wait(dve, LP[D_], "pow2", td)
                    dve.tensor_scalar(d_sc[:, 3:4], d_sc[:, 1:2], rs[:, D_:D_ + 1], float(D) ** 0.5, ALU.mult,
                                      ALU.mult).then_inc(LV[D_]("sc"), 1)
                    wait(dve, LV[D_], "sc", td)
                    normed(D_, i, d_sc[:, 3:4])
                if on(i, A_):
                    unit_max(0, i)
                if on(i, B_):
                    wait(dve, LP[B_], "pow2", tb)
                    wait(dve, LT[B_], "qkv", tb)
                    wait(dve, LP[B_], "av1", tb - 1)
                    dve.scalar_tensor_tensor(out=qkv[:, :], in0=bank(B3, 3 * D), scalar=b_sc[:, 1:2], in1=bqkv[:, :],
                                             op0=ALU.mult, op1=ALU.add).then_inc(LV[B_]("qkv"), 1)
                if on(i, D_):
                    wait(dve, LA[D_], "sim", td)
                    wait(dve, LV[D_], "cb", td - 1)
                    carry(4)
                    d_top("ta", td, range(2 * PH)).then_inc(LV[D_]("ta"), 1)
                if on(i, B_):
                    b_half("qk", 0, tb)
                    b_half("qk", 1, tb)
                if on(i, D_):
                    wait(dve, LV[D_], "ta", td)
                    carry(5)
                    d_top("tr", td, range(2 * PH)).then_inc(LV[D_]("tr"), 1)
                if on(i, A_):
                    unit_rec(0, i)
                if on(i, B_):
                    b_softmax(tb)
                if on(i, C_):
                    unit_max(1, i)
                if on(i, B_):
                    b_sum(tb)
                if on(i, D_):
                    wait(dve, LV[D_], "tr", td)
                    carry(6)
                    d_top("tb", td, range(2 * PH)).then_inc(LV[D_]("tb"), 1)
                if on(i, D_):
                    d_cands(td)
                if on(i, A_):
                    unit_res(0, i)
                if on(i, C_):
                    unit_rec(1, i)
                if on(i, D_):
                    wait(dve, LV[D_], "cand", td)
                    carry(7)
                    d_ctop("ca", td)
                if on(i, B_):
                    b_half("av", 0, tb)
                    b_half("av", 1, tb)
                    b_norm(tb)
                if on(i, D_):
                    wait(dve, LV[D_], "ca", td)
                    carry(8)
                    d_ctop("cr", td)
                    wait(dve, LV[D_], "cr", td)
                    carry(9)
                    d_ctop("cb", td)
                    wait(dve, LV[D_], "cb", td)
                    wait(dve, LA[D_], "e7", td - 1)
                    dve.tensor_scalar(neg1[:, :].unsqueeze(2), cbest[:, :, 0:1], -1.0, None, ALU.mult)\
                        .then_inc(LV[D_]("nv"), 1)
                    dve.tensor_tensor(cexp[:, :, :], cbest[:, :, :], cbest[:, :, 0:1].to_broadcast([P, PH, TOP]),
                                      ALU.subtract).then_inc(LV[D_]("vs"), 1)
                if on(i, B_):
                    b_x2(tb)
                if on(i, C_):
                    unit_max(2, i)
                if on(i, D_):
                    wait(dve, LA[D_], "vexp", td)
                    dve.tensor_reduce(zsum[:, :], cexp[:, :, :], X_AXIS, ALU.add).then_inc(LV[D_]("vsum"), 1)
                    wait(dve, LV[D_], "vsum", td)
                    dve.reciprocal(zinv[:, :], zsum[:, :]).then_inc(LV[D_]("vrec"), 1)
                    d_mask(0, td)
                if on(i, B_):
                    b_gate(tb)
                if on(i, C_):
                    unit_rec(2, i)
                    unit_res(1, i)
                if on(i, D_):
                    d_mask(1, td)
                if on(i, B_):
                    b_logits(tb)
                if on(i, D_):
                    d_mask(2, td)
                if on(i, B_):
                    b_gates(tb)
                if on(i, D_):
                    d_mask(3, td)
                if on(i, B_):
                    b_experts(0, tb)
                if on(i, D_):
                    d_mask(4, td)
                if on(i, C_):
                    unit_res(2, i)
                if on(i, D_):
                    d_mask(5, td)
                if on(i, B_):
                    b_experts(1, tb)
                    b_res(tb)
                if on(i, D_):
                    d_mask(6, td)
                    d_mask(7, td)
                    wait(dve, LT[D_], "w7", td)
                    wait(dve, LA[D_], "gel1", td)
                    dve.tensor_tensor(gel[:, :, :].rearrange("p (k c) n -> p k (c n)", k=2),
                                      gel[:, :, :].rearrange("p (k c) n -> p k (c n)", k=2), ps[:, B5:B5 + 2, :],
                                      ALU.mult).then_inc(LV[D_]("gw"), 1)
                    wait(dve, LT[D_], "out", td)
                    dve.tensor_tensor(x_of(td), x_of(td), bank(B4, D), ALU.add).then_inc(LV[D_]("fin"), 1)
            bodies(dve, body)


def kernel(**inputs):
    import numpy as np
    import concourse.bacc as bacc
    from concourse.bass_utils import run_bass_kernel_spmd

    a = {k: np.asarray(v) for k, v in inputs.items()}

    def by_head(w):
        return w.reshape(UNIT, HD0, w.shape[1]).transpose(1, 0, 2)

    def chunks(w):
        return w.reshape(-1, P, w.shape[1]).transpose(1, 0, 2)

    ctx_t = np.zeros((BATCH, CD, 2 * P + CTX), np.float32)
    ctx_t[:, :, P:P + CTX] = a["ctx_768"].transpose(0, 2, 1)
    rows = np.concatenate([a["L0_xattn_bout"], a["L0_ffn_bq"], a["L0_ffn_bup"], a["L0_ffn_bo"], a["L0_ffn_bg"],
                           a["g_xattn"], a["g_ffn"]])
    arrays = {
        "x": chunks(a["x"].reshape(-1, D)),
        "ctx_t": ctx_t,
        "mask": np.broadcast_to(a["mask_BxS2_bf1"].view(np.uint8)[None], (P, BATCH, CTX)),
        "rows": np.broadcast_to(rows[None], (P, ROW_TOTAL)),
        "cols": np.stack([a["L0_ffn_gamma1"], a["L0_ffn_gamma2"], a["L1_ffn_gamma"]], 1),
        "wk0": a["L0_xattn_Wk"],
        "wqt0": by_head(a["L0_xattn_Wq"].T),
        "wvt0": by_head(a["L0_xattn_Wv"].T),
        "wout0": by_head(a["L0_xattn_Wout"]),
        "f_wq": a["L0_ffn_Wq"],
        "f_wdt": a["L0_ffn_Wdown"].T,
        "f_wup": a["L0_ffn_Wup"],
        "f_bd": np.broadcast_to(a["L0_ffn_bdown"][:, None], (64, P)),
        "f_wo": a["L0_ffn_Wo"],
        "f_wg": a["L0_ffn_Wg"],
        "f_we": a["L0_ffn_We"].transpose(1, 0, 2).reshape(D, EXPERTS * D),
        "wk1": a["L1_xattn_Wk"],
        "wqt1": a["L1_xattn_Wq"].T,
        "wvt1": a["L1_xattn_Wv"].T,
        "wo1": a["L1_xattn_Wo"],
        "pk_wq": a["L1_ffn_wq"].reshape(2 * PH, PK, D).transpose(1, 0, 2),
        "pk_keys": a["L1_ffn_keys"].transpose(3, 2, 0, 1).reshape(PK, 2 * PH, KEYS),
        "pk_down": a["L1_ffn_table_down"][:GRID].T,
        "pk_up": chunks(a["L1_ffn_table_up"][:GRID]),
    }
    nc = bacc.Bacc("TRN2", target_bir_lowering=False, num_devices=1)
    feed, args = {}, []
    for name, value in arrays.items():
        value = np.ascontiguousarray(value)
        feed[f"in_{name}"] = value
        args.append(nc.dram_tensor(f"in_{name}", value.shape, mybir.dt.from_np(value.dtype), kind="ExternalInput").ap())
    args.append(nc.dram_tensor("out_x", (TILES, P, D), F32, kind="ExternalOutput").ap())
    flamingo_kernel(nc, *args)
    got = run_bass_kernel_spmd(nc, [feed], core_ids=[0])
    return got.results[0]["out_x"].reshape(BATCH, SEQ, D)
```

```python
from contextlib import ExitStack

import concourse.bass as bass
from concourse import mybir

F32 = mybir.dt.float32
BF16 = mybir.dt.bfloat16
U8 = mybir.dt.uint8
ALU = mybir.AluOpType
ACT = mybir.ActivationFunctionType
X_AXIS = mybir.AxisListType.X

P = 128
BANK = 512
BATCH, SEQ, D = 4, 512, 128
CTX, CD = 154, 96
TILES = BATCH * SEQ // P
PER_BATCH = SEQ // P
UNIT = 8
FLAT = UNIT * CTX
CHUNKS = -(-FLAT // P)
TAIL = FLAT - (CHUNKS - 1) * P
HD0, HD1 = 64, 8
FH, FD = 16, 8
EXPERTS = 8
PH, KEYS, PK, TOP = 8, 32, 64, 16
GRID = KEYS * KEYS
STAIRS = [TOP // (i + 1) for i in range(TOP)]
CANDS = sum(STAIRS)
LOW = -3.0e38
FAR = -(2.0 ** 126)
BANK_HEADS = [3, 3, 2]

ROW_SIZES = [("bout", D), ("bq", D), ("bup", 2 * D), ("bo", D), ("bg", EXPERTS), ("gx", 2), ("gf", 2)]
ROWS = {}
_at = 0
for _name, _size in ROW_SIZES:
    ROWS[_name] = (_at, _at + _size)
    _at += _size
ROW_TOTAL = _at


class Steps:

    def __init__(self, sem, names):
        self.sem = sem
        self.names = names.split()
        self.n = 0

    def __call__(self, name):
        assert self.names[self.n % len(self.names)] == name, (self.names[self.n % len(self.names)], name)
        self.n += 1
        return self.sem

    def after(self, name, tile):
        return tile * len(self.names) + (self.names.index(name) + 1)


def flamingo_kernel(nc, d_x, d_ctx_t, d_mask, d_rows, d_cols, d_wk0, d_wqt0, d_wvt0, d_wout0, d_f_wq, d_f_wdt, d_f_wup, d_f_bd, d_f_wo, d_f_wg, d_f_we, d_wk1, d_wqt1, d_wvt1, d_wo1, d_pk_wq, d_pk_keys, d_pk_down, d_pk_up, d_out):
    es = ExitStack()
    with es:
        def sb(name, shape, dt=F32, stack=es):
            return stack.enter_context(nc.sbuf_tensor(name, shape, dt))

        def sem(name):
            return es.enter_context(nc.semaphore(name))

        ps = es.enter_context(nc.psum_tensor("ps", [P, 8, BANK], F32))

        xs = sb("xs", [P, TILES, D])
        G = sb("G", [P, BATCH, 3, FLAT])
        VW = sb("VW", [P, BATCH, 3, CHUNKS * D])
        far_row = sb("far_row", [1, BATCH, CTX], BF16)
        bo_row = sb("bo_row", [1, D])
        bg = sb("bg", [P, EXPERTS])
        col_sb = sb("col_sb", [P, 3])
        tg = sb("tg", [P, 4])
        ident = sb("ident", [P, P])
        ones_row = sb("ones_row", [1, P])
        ones_bf = sb("ones_bf", [1, P], BF16)
        wqkv = sb("wqkv", [P, 3 * D])
        bqkv = sb("bqkv", [P, 3 * D])
        wo_f = sb("wo_f", [P, D])
        bout_g = sb("bout_g", [1, D])
        wg = sb("wg", [P, EXPERTS])
        we = sb("we", [P, EXPERTS * D])
        wc = sb("wc", [P, 2 * PH * KEYS])
        down = sb("down", [P, GRID])
        up = sb("up", [P, GRID // P, D])

        def bank(n, cols=BANK):
            return ps[:, n, 0:cols]


        with ExitStack() as tmp:
            def scratch(name, shape, dt=F32):
                return tmp.enter_context(nc.sbuf_tensor(name, shape, dt))

            row_sb = scratch("row_sb", [P, ROW_TOTAL])

            def row(name):
                a, b = ROWS[name]
                return row_sb[:, a:b]

            cbuf = scratch("cbuf", [CD, 2 * P + CTX])
            wk0 = scratch("wk0", [CD, 4 * P])
            wqt0 = scratch("wqt0", [HD0, UNIT, D])
            wvt0 = scratch("wvt0", [HD0, UNIT, CD])
            wout0 = scratch("wout0", [HD0, UNIT, D])
            wk1 = scratch("wk1", [CD, D])
            wqt1 = scratch("wqt1", [P, D])
            wvt1 = scratch("wvt1", [P, CD])
            wo1 = scratch("wo1", [P, D])
            f_wdt = scratch("f_wdt", [64, D])
            f_wup = scratch("f_wup", [64, 2 * D])
            f_bd = scratch("f_bd", [64, P])
            pk_wq = scratch("pk_wq", [PK, 2 * PH, D])
            pk_keys = scratch("pk_keys", [PK, 2 * PH, KEYS])
            blk = scratch("blk", [P, 2 * UNIT])
            cw = scratch("cw", [CD, 3, UNIT * D])
            kt0 = scratch("kt0", [HD0, UNIT, CTX])
            kt1 = scratch("kt1", [P, CTX])
            by_head = scratch("by_head", [P, 2 * UNIT * CTX])
            wo_blk = by_head[:, 0:2 * UNIT * D].rearrange("p (h n) -> p h n", n=D)
            k_blk = by_head[:, :].rearrange("p (h m) -> p h m", m=CTX)
            mask8 = scratch("mask8", [P, BATCH, CTX], U8)

            ctx_in, small, wt, xt_in = sem("ctx_in"), sem("loaded_small"), sem("loaded_weights"), sem("loaded_x")
            V = Steps(sem("fold_v"), "wq bq bout bo bg wg we far_row wo_blk wdu bkv wc down up")
            A = Steps(sem("fold_a"), "tanh cw0 cw1")
            T = Steps(sem("fold_t"), "wdu wc cw0 cw1")
            I = Steps(sem("const_p"), "z1 z2 o1 o2 eye b1 b2")
            BT = Steps(sem("ctx_t"), "k u0 u1 u2")
            BV = Steps(sem("ctx_v"), "kt1 k_blk vw0 vw1 vw2")
            BA = Steps(sem("ctx_a"), "kt0 g0 g1 g2")
            NS, NW = 10, 11

            block = tmp.enter_context(nc.Block())

            @block.sync
            def _(sp):
                sp.dma_start(row_sb[:, :], d_rows).then_inc(small, 16)
                sp.dma_start(col_sb[:, :], d_cols).then_inc(small, 16)
                sp.dma_start(mask8[:, :, :], d_mask).then_inc(small, 16)
                sp.dma_start(f_wdt[:, :], d_f_wdt).then_inc(small, 16)
                sp.dma_start(f_wup[:, :], d_f_wup).then_inc(small, 16)
                sp.dma_start(f_bd[:, :], d_f_bd).then_inc(small, 16)
                sp.dma_start(pk_wq[:, :, :], d_pk_wq).then_inc(small, 16)
                sp.dma_start(pk_keys[:, :, :], d_pk_keys).then_inc(small, 16)
                sp.dma_start(wqkv[:, 0:D], d_f_wq).then_inc(small, 16)
                sp.dma_start(wg[:, :], d_f_wg).then_inc(small, 16)
                sp.dma_start(cbuf[:, :], d_ctx_t[0, :, :]).then_inc(ctx_in, 16)
                with sp.Fori(1, BATCH) as b:
                    sp.wait_ge(BT.sem, b * len(BT.names))
                    sp.dma_start(cbuf[:, :], d_ctx_t[bass.ds(b, 1), :, :].rearrange("a c m -> (a c) m"))\
                        .then_inc(ctx_in, 16)
                sp.wait_ge(xt_in, 32)

            @block.scalar
            def _(act):
                act.dma_start(wvt0[:, :, :], d_wvt0).then_inc(wt, 16)
                act.dma_start(wout0[:, :, :], d_wout0).then_inc(wt, 16)
                act.dma_start(wvt1[:, :], d_wvt1).then_inc(wt, 16)
                act.dma_start(wo1[:, :], d_wo1).then_inc(wt, 16)
                act.dma_start(wk0[:, :], d_wk0).then_inc(wt, 16)
                act.dma_start(wqt0[:, :, :], d_wqt0).then_inc(wt, 16)
                act.dma_start(wk1[:, :], d_wk1).then_inc(wt, 16)
                act.dma_start(wqt1[:, :], d_wqt1).then_inc(wt, 16)
                act.dma_start(we[:, :], d_f_we).then_inc(wt, 16)
                act.dma_start(down[:, :], d_pk_down).then_inc(wt, 16)
                act.dma_start(up[:, :, :], d_pk_up).then_inc(wt, 16)
                act.dma_start(wo_f[:, :], d_f_wo).then_inc(xt_in, 16)
                act.dma_start(xs[:, :, :], d_x).then_inc(xt_in, 16)
                act.wait_ge(small, 16 * NS)
                act.activation(tg[:, 0:2], row("gx"), ACT.Tanh)
                act.activation(tg[:, 2:4], row("gf"), ACT.Tanh).then_inc(A("tanh"), 1)
                act.wait_ge(A.sem, A.after("tanh", 0))
                act.wait_ge(T.sem, T.after("cw0", 0))
                act.activation(cw[:, 0, :], ps[0:CD, 2:4, :], ACT.Copy, scale=tg[0:CD, 0:1]).then_inc(A("cw0"), 1)
                act.wait_ge(T.sem, T.after("cw1", 0))
                act.activation(cw[:, 1:3, :].rearrange("p u n -> p (u n)"), ps[0:CD, 4:8, :], ACT.Copy,
                               scale=tg[0:CD, 1:2]).then_inc(A("cw1"), 1)
                with act.Fori(0, BATCH) as b:
                    act.wait_ge(BT.sem, BT.after("k", b))
                    act.activation(kt0[:, 0:6, :].rearrange("p (k h) m -> p k (h m)", k=2), ps[0:HD0, 0:2, 0:3 * CTX],
                                   ACT.Copy, scale=HD0 ** -0.5)
                    act.activation(kt0[:, 6:8, :].rearrange("p h m -> p (h m)"), ps[0:HD0, 2, 0:2 * CTX], ACT.Copy,
                                   scale=HD0 ** -0.5).then_inc(BA("kt0"), 1)
                    for u in range(3):
                        act.wait_ge(BT.sem, BT.after(f"u{u}", b))
                        act.activation(G[:, bass.ds(b, 1), u, 0:6 * CTX].rearrange("p a (k n) -> p (a k) n", k=2),
                                       ps[:, 2:4, 0:3 * CTX], ACT.Copy)
                        act.activation(G[:, bass.ds(b, 1), u, 6 * CTX:FLAT], ps[:, 4:5, 0:2 * CTX], ACT.Copy)\
                            .then_inc(BA(f"g{u}"), 1)

            @block.gpsimd
            def _(pool):
                pool.memset(ident[:, :], 0.0).then_inc(I("z1"), 1)
                pool.memset(blk[:, :], 1.0).then_inc(I("z2"), 1)
                pool.memset(ones_row[:, :], 1.0).then_inc(I("o1"), 1)
                pool.memset(ones_bf[:, :], 1.0).then_inc(I("o2"), 1)
                pool.wait_ge(I.sem, I.after("z1", 0))
                pool.affine_select(out=ident[:, :], in_=ident[:, :], compare_op=ALU.not_equal, fill=1.0, base=0,
                                   pattern=[[-1, P]], channel_multiplier=1).then_inc(I("eye"), 1)
                pool.wait_ge(I.sem, I.after("z2", 0))
                pool.affine_select(out=blk[:, :], in_=blk[:, :], compare_op=ALU.is_ge, fill=0.0, base=0,
                                   pattern=[[-HD1, 2 * UNIT]], channel_multiplier=1).then_inc(I("b1"), 1)
                pool.wait_ge(I.sem, I.after("b1", 0))
                pool.affine_select(out=blk[:, :], in_=blk[:, :], compare_op=ALU.is_ge, fill=0.0, base=HD1 - 1,
                                   pattern=[[HD1, 2 * UNIT]], channel_multiplier=-1).then_inc(I("b2"), 1)

            @block.vector
            def _(dve):
                g1, g2, g3 = col_sb[:, 0:1], col_sb[:, 1:2], col_sb[:, 2:3]
                dve.wait_ge(small, 16 * NS)
                dve.tensor_scalar(wqkv[:, 0:D], wqkv[:, 0:D], g1, FD ** -0.5, ALU.mult, ALU.mult).then_inc(V("wq"), 1)
                dve.tensor_scalar(bqkv[:, 0:D], row("bq"), FD ** -0.5, None, ALU.mult).then_inc(V("bq"), 1)
                dve.wait_ge(A.sem, A.after("tanh", 0))
                dve.tensor_scalar(bout_g[:, :], row_sb[0:1, 0:D], tg[0:1, 0:1], None, ALU.mult)\
                    .then_inc(V("bout"), 1)
                dve.tensor_copy(bo_row[:, :], row("bo")[0:1, :]).then_inc(V("bo"), 1)
                dve.tensor_copy(bg[:, :], row("bg")).then_inc(V("bg"), 1)
                dve.tensor_scalar(wg[:, :], wg[:, :], g2, None, ALU.mult).then_inc(V("wg"), 1)
                dve.wait_ge(wt, 16 * NW)
                dve.tensor_scalar(we[:, :], we[:, :], g2, None, ALU.mult).then_inc(V("we"), 1)
                dve.tensor_scalar(far_row[:, :, :], mask8[0:1, :, :], -1.0, -FAR, ALU.add, ALU.mult)\
                    .then_inc(V("far_row"), 1)
                dve.wait_ge(I.sem, I.after("b2", 0))
                dve.tensor_tensor(wo_blk, wo1[:, :].unsqueeze(1).to_broadcast([P, 2 * UNIT, D]),
                                  blk[:, :].unsqueeze(2).to_broadcast([P, 2 * UNIT, D]), ALU.mult)\
                    .then_inc(V("wo_blk"), 1)
                dve.wait_ge(T.sem, T.after("wdu", 0))
                dve.tensor_scalar(wqkv[:, D:3 * D], ps[:, 0, 0:2 * D], g1, None, ALU.mult).then_inc(V("wdu"), 1)
                dve.tensor_tensor(bqkv[:, D:3 * D], ps[:, 0, 2 * D:4 * D], row("bup"), ALU.add).then_inc(V("bkv"), 1)
                dve.wait_ge(T.sem, T.after("wc", 0))
                dve.tensor_scalar(wc[:, :], ps[:, 1, :], g3, None, ALU.mult).then_inc(V("wc"), 1)
                dve.tensor_scalar(down[:, :], down[:, :], g3, None, ALU.mult).then_inc(V("down"), 1)
                dve.tensor_scalar(up[:, :, :], up[:, :, :], tg[:, 3:4], None, ALU.mult).then_inc(V("up"), 1)
                with dve.Fori(0, BATCH) as b:
                    dve.wait_ge(BT.sem, BT.after("k", b))
                    dve.scalar_tensor_tensor(out=kt1[:, :].unsqueeze(1), in0=ps[:, 3:4, 0:CTX],
                                             scalar=HD1 ** -0.5, in1=mask8[:, bass.ds(b, 1), :], op0=ALU.mult,
                                             op1=ALU.mult).then_inc(BV("kt1"), 1)
                    dve.wait_ge(BV.sem, BV.after("kt1", b))
                    dve.tensor_tensor(k_blk, kt1[:, :].unsqueeze(1).to_broadcast([P, 2 * UNIT, CTX]),
                                      blk[:, :].unsqueeze(2).to_broadcast([P, 2 * UNIT, CTX]), ALU.mult)\
                        .then_inc(BV("k_blk"), 1)
                    for u in range(3):
                        dve.wait_ge(BT.sem, BT.after(f"u{u}", b))
                        dve.tensor_copy(VW[:, bass.ds(b, 1), u, 0:2 * BANK].rearrange("p a (k n) -> p (a k) n", k=2),
                                        ps[:, 5:7, :])
                        dve.tensor_copy(VW[:, bass.ds(b, 1), u, 2 * BANK:CHUNKS * D], ps[:, 7:8, 0:2 * D])\
                            .then_inc(BV(f"vw{u}"), 1)

            @block.tensor
            def _(pe):
                pe.wait_ge(small, 16 * NS)
                pe.matmul(ps[:, 0, 0:2 * D], f_wdt[:, :], f_wup[:, :], start=True, stop=True)
                pe.matmul(ps[:, 0, 2 * D:4 * D], f_bd[:, :], f_wup[:, :], start=True, stop=True).then_inc(T("wdu"), 1)
                for n in range(2 * PH):
                    mm = pe.matmul(ps[:, 1, n * KEYS:(n + 1) * KEYS], pk_wq[:, n, :], pk_keys[:, n, :],
                                   start=True, stop=True)
                mm.then_inc(T("wc"), 1)
                pe.wait_ge(wt, 16 * NW)
                for h in range(UNIT):
                    mm = pe.matmul(ps[0:CD, 2 + h // 4, (h % 4) * D:(h % 4 + 1) * D], wvt0[:, h, :], wout0[:, h, :],
                                   start=True, stop=True)
                mm.then_inc(T("cw0"), 1)
                pe.wait_ge(V.sem, V.after("wo_blk", 0))
                for q in range(4):
                    mm = pe.matmul(ps[0:CD, 4 + q, :], wvt1[:, :], wo_blk[:, 4 * q:4 * q + 4, :], start=True, stop=True)
                mm.then_inc(T("cw1"), 1)
                pe.wait_ge(A.sem, A.after("cw1", 0))
                pe.wait_ge(V.sem, V.after("up", 0))
                def products(b):
                    pe.wait_ge(ctx_in, (b + 1) * 16)
                    if not isinstance(b, int):
                        pe.wait_ge(BV.sem, b * len(BV.names))
                        pe.wait_ge(BA.sem, b * len(BA.names))
                    for h in range(UNIT):
                        pe.matmul(ps[0:HD0, h // 3, (h % 3) * CTX:(h % 3 + 1) * CTX],
                                  wk0[:, h * HD0:(h + 1) * HD0], cbuf[:, P:P + CTX], start=True, stop=True)
                    pe.matmul(ps[:, 3, 0:CTX], wk1[:, :], cbuf[:, P:P + CTX], start=True, stop=True)\
                        .then_inc(BT("k"), 1)
                    for u in range(3):
                        if u == 0:
                            pe.wait_ge(BV.sem, BV.after("k_blk", b))
                            pe.wait_ge(BA.sem, BA.after("kt0", b))
                        else:
                            pe.wait_ge(BV.sem, BV.after(f"vw{u - 1}", b))
                            pe.wait_ge(BA.sem, BA.after(f"g{u - 1}", b))
                        for h in range(UNIT):
                            to = ps[:, 2 + h // 3, (h % 3) * CTX:(h % 3 + 1) * CTX]
                            if u == 0:
                                pe.matmul(to, wqt0[:, h, :], kt0[:, h, :], start=True, stop=True)
                            else:
                                pe.matmul(to, wqt1[:, :], k_blk[:, UNIT * (u - 1) + h, :], start=True, stop=True)
                        for c in range(CHUNKS):
                            heads = [h for h in range(UNIT) if h * CTX < (c + 1) * P and (h + 1) * CTX > c * P]
                            for h in heads:
                                off = P + c * P - h * CTX
                                mm = pe.matmul(ps[:, 5 + c // 4, (c % 4) * D:(c % 4 + 1) * D], cbuf[:, off:off + P],
                                               cw[:, u, h * D:(h + 1) * D], start=(h == heads[0]), stop=(h == heads[-1]))
                        mm.then_inc(BT(f"u{u}"), 1)

                products(0)
                with pe.Fori(1, BATCH) as b:
                    products(b)

        xn = {s: sb(f"xn_{s}", [P, D]) for s in "abcd"}
        xt = {s: sb(f"xt_{s}", [P, P]) for s in "abcd"}
        stat = {s: sb(f"stat_{s}", [P, 6]) for s in "abcd"}
        mv = {s: sb(f"mv_{s}", [P, 2]) for s in "abcd"}
        var = {s: sb(f"var_{s}", [P, 1]) for s in "abcd"}
        rs = {s: sb(f"rs_{s}", [P, 1]) for s in "abcd"}
        half = sb("half", [P, 1])
        carrier = sb("carrier", [P, 14])
        prob_even, prob_odd = sb("prob_even", [P, FLAT]), sb("prob_odd", [P, FLAT])
        prob = [prob_even, prob_odd, prob_even]
        prob_t = sb("prob_t", [P, CHUNKS, P])
        nmax = sb("nmax", [P, 3, UNIT])
        rsum = sb("rsum", [P, 3, UNIT])
        rinv = sb("rinv", [P, 3, UNIT])
        qkv = sb("qkv", [P, 3 * D])
        prod = sb("prod", [P, 2, FH * FH * FD // 2])
        b_sc = sb("b_sc", [P, 8])
        att = sb("att", [P, FH, FH])
        amax = sb("amax", [P, FH])
        asum = sb("asum", [P, FH])
        arec = sb("arec", [P, FH])
        av = sb("av", [P, D])
        av_t = sb("av_t", [P, P])
        x2 = sb("x2", [P, D])
        x2_t = av_t
        sq = sb("sq", [P, D])
        gate = sb("gate", [P, 3, EXPERTS])
        d_sc = sb("d_sc", [P, 8])
        sim = sb("sim", [P, 2 * PH, KEYS])
        rest = sb("rest", [P, 2 * PH, KEYS])
        best = sb("best", [P, 2 * PH, TOP])
        cand = sb("cand", [P, PH, CANDS])
        cbest = sb("cbest", [P, PH, TOP])
        neg1 = sb("neg1", [P, PH])
        cexp = sb("cexp", [P, PH, TOP])
        zsum = sb("zsum", [P, PH])
        zinv = sb("zinv", [P, PH])
        diag = sb("diag", [P, 2, P])
        NSUM, NEXP = 2, 2
        sums = sb("sums", [P, NSUM, KEYS, KEYS])
        wexp = sb("wexp", [P, NEXP, GRID])
        gel = sb("gel", [P, GRID // P, P])

        LINES = [
            "a_stats a_aggr a_eps", "a_xn", "c_stats c_aggr c_eps", "c_xn",
            "b_stats b_aggr b_eps", "b_vr b_vr2 b_xn", "b_qkv", "b_qk0 b_qk1 b_amax b_asub", "b_asum b_arec",
            "b_av0 b_av1 b_anorm", "b_x2 b_eps3 b_glog b_gmax b_grec b_gates", "b_y0 b_y1 b_y2 b_y3 b_y4 b_y5 b_y6 b_y7 b_res",
            "d_stats d_aggr d_eps", "d_vr d_n2", "d_sc d_xn", "d_ta d_tr d_tb", "d_cand d_ca d_cr d_cb d_nv d_vs",
            "d_vsum d_vrec", "d_m0 d_m1 d_m2 d_m3 d_m4 d_m5 d_m6 d_m7", "d_gw", "d_fin",
            "u0_max", "u0_rec", "u0_res", "u1_max", "u1_rec", "u1_res", "u2_max", "u2_rec", "u2_res",
            "a_pow", "c_pow", "b_pow", "b_pow2", "b_pqk0 b_pqk1", "b_pav0 b_pav1", "b_pow3", "d_pow", "d_pow2",
            "d_s0 d_s1 d_s2 d_s3 d_s4 d_s5 d_s6 d_s7", "u0_norm", "u1_norm", "u2_norm",
            "a_axt", "b_axt", "c_axt", "d_axt", "b_aexp", "b_aavt", "b_sq", "b_ax2t", "b_gexp", "d_sim", "d_gel",
            "d_vexp", "d_g0 d_e0 d_g1 d_e1 d_g2 d_e2 d_g3 d_e3 d_g4 d_e4 d_g5 d_e5 d_g6 d_e6 d_g7 d_e7",
            "u0_exp", "u0_apt0 u0_apt1 u0_apt2", "u1_exp", "u1_apt0 u1_apt1 u1_apt2", "u2_exp",
            "u2_apt0 u2_apt1 u2_apt2",
            "a_txt", "b_txt", "c_txt", "d_txt", "b_tqkv", "b_tavt", "b_tatt", "b_tx2t", "b_tgate", "b_ty0 b_ty1",
            "d_tsim", "d_ht0 d_ht1", "d_w0 d_w1 d_w2 d_w3 d_w4 d_w5 d_w6 d_w7", "d_out",
            "u0_sc", "u0_pt0 u0_pt1 u0_pt2 u0_out", "u1_sc", "u1_pt0 u1_pt1 u1_pt2 u1_out", "u2_sc",
            "u2_pt0 u2_pt1 u2_pt2 u2_out",
        ]
        STEPS = {}
        for line in LINES:
            steps = Steps(sem("s_" + line.split()[0]), line)
            for name in steps.names:
                STEPS[name] = steps
        stored = sem("stored")
        half_set = sem("half_set")

        DEPTH = 4
        SHARED = {
            "score_banks": [("u1_sc", "u1_exp", 2), ("u2_sc", "u2_exp", 2), ("u0_sc", "u0_exp", 0)],
            "bank7": [("u0_pt0", "u0_apt0", 1), ("c_txt", "c_axt", 2), ("u0_pt1", "u0_apt1", 1),
                      ("u0_pt2", "u0_apt2", 1), ("u0_out", "u0_res", 1), ("a_txt", "a_axt", 0),
                      ("u1_pt0", "u1_apt0", 2), ("u1_pt1", "u1_apt1", 2), ("u1_pt2", "u1_apt2", 2),
                      ("u1_out", "u1_res", 2), ("u2_pt0", "u2_apt0", 2), ("u2_pt1", "u2_apt1", 2),
                      ("u2_pt2", "u2_apt2", 2), ("u2_out", "u2_res", 2)],
            "bank3": [("b_tatt", "b_x2", 2), ("b_tx2t", "b_ax2t", 2), ("b_tgate", "b_glog", 2),
                      ("b_ty0", "b_y3", 2), ("b_ty1", "b_y7", 2), ("b_txt", "b_axt", 1),
                      ("b_tqkv", "b_qkv", 1), ("d_ht1", "d_gel", 3), ("b_tavt", "b_aavt", 1)],
            "bank4": [("d_txt", "d_axt", 3), ("d_tsim", "d_sim", 3), ("d_out", "d_fin", 4),
                      ("d_ht0", "d_gel", 3)],
            "prob_even": [("u0_exp", "u0_pt2", 1), ("u2_exp", "u2_pt2", 2)],
            "prob_odd": [("u1_exp", "u1_pt2", 2)],
            "prob_t": [("u0_apt0", "u0_out", 1), ("u1_apt0", "u1_out", 2), ("u2_apt0", "u2_out", 2)],
        }
        BEFORE = {}
        for users in SHARED.values():
            n = len(users)
            for k, (first, end, lag) in enumerate(users):
                BEFORE[first] = [(users[(k - back) % n][1],
                                  lag - users[(k - back) % n][2] - (1 if back > k else 0) - (back > n) * ((back - 1) // n))
                                 for back in range(1, n * (DEPTH + 1))]

        def wait(eng, name, t):
            if not isinstance(t, int) or 0 <= t < TILES:
                eng.wait_ge(STEPS[name].sem, STEPS[name].after(name, t))

        def done(name):
            return STEPS[name](name)

        def vacated(eng, first, t):
            for end, ahead in BEFORE[first]:
                if not isinstance(t, int) or 0 <= t + ahead < TILES:
                    wait(eng, end, t + ahead)
                    return

        def there(t):
            return not isinstance(t, int) or 0 <= t < TILES

        def x_of(t):
            return xs[:, t, :] if isinstance(t, int) else xs[:, bass.ds(t, 1), :].rearrange("p a d -> p (a d)")

        def batch_of(t):
            return t // PER_BATCH

        def bodies(eng, body):
            for i in range(DEPTH + 1):
                body(i)
            with eng.Fori(DEPTH + 1, TILES) as i:
                body(i)
            for i in range(TILES, TILES + DEPTH):
                body(i)

        U_OF = ["a", "c", "c"]
        BANK3, BANK4, BANK7, WBANK = 3, 4, 7, 5

        block = es.enter_context(nc.Block())

        @block.sync
        def _(sp):
            def store(t):
                if not there(t):
                    return
                wait(sp, "d_fin", t)
                dst = d_out[t, :, :] if isinstance(t, int) else \
                    d_out[bass.ds(t, 1), :, :].rearrange("a p d -> (a p) d")
                sp.dma_start(dst, x_of(t)).then_inc(stored, 16)

            def body(i):
                store(i - DEPTH)
            bodies(sp, body)
            sp.wait_ge(stored, 16 * TILES)

        @block.gpsimd
        def _(pool):
            def power(name, out_, in_):
                pool.tensor_tensor(out_[:, :], in_[:, :], half[:, :], ALU.pow).then_inc(done(name), 1)

            def rsqrt_var(s, t):
                if not there(t):
                    return
                wait(pool, f"{s}_eps", t)
                wait(pool, f"{s}_xn", t - 1)
                power(f"{s}_pow", rs[s], var[s])

            def d_pow2(t):
                if not there(t):
                    return
                wait(pool, "d_n2", t)
                wait(pool, "d_sc", t - 1)
                power("d_pow2", d_sc[:, 1:2], d_sc[:, 0:1])

            def b_pow2(t):
                if not there(t):
                    return
                wait(pool, "b_vr2", t)
                wait(pool, "b_qkv", t - 1)
                power("b_pow2", b_sc[:, 1:2], b_sc[:, 0:1])

            def b_pow3(t):
                if not there(t):
                    return
                wait(pool, "b_eps3", t)
                wait(pool, "b_gates", t - 1)
                power("b_pow3", b_sc[:, 4:5], b_sc[:, 3:4])

            def norm(u, t):
                if not there(t):
                    return
                wait(pool, f"u{u}_exp", t)
                wait(pool, f"u{u}_rec", t)
                pr = prob[u][:, :].rearrange("p (h m) -> p h m", m=CTX)
                pool.tensor_tensor(pr, pr, rinv[:, u, :].unsqueeze(2).to_broadcast([P, UNIT, CTX]), ALU.mult)\
                    .then_inc(done(f"u{u}_norm"), 1)

            def b_qk(k, t):
                if not there(t):
                    return
                wait(pool, "b_qkv", t)
                wait(pool, f"b_av{k}", t - 1)
                n = FH // 2
                q = qkv[:, k * n * FD:(k + 1) * n * FD].rearrange("p (h d) -> p h d", d=FD)
                kk = qkv[:, D:3 * D].rearrange("p (g e) -> p g e", e=2 * FD)[:, :, 0:FD]
                pool.tensor_tensor(prod[:, k, :].rearrange("p (h g d) -> p h g d", g=FH, d=FD),
                                   q.unsqueeze(2).to_broadcast([P, n, FH, FD]),
                                   kk.unsqueeze(1).to_broadcast([P, n, FH, FD]), ALU.mult)\
                    .then_inc(done(f"b_pqk{k}"), 1)

            def b_av(k, t):
                if not there(t):
                    return
                wait(pool, "b_aexp", t)
                wait(pool, f"b_qk{k}", t)
                n = FH // 2
                v = qkv[:, D:3 * D].rearrange("p (g e) -> p e g", e=2 * FD)[:, FD:2 * FD, :]
                pool.tensor_tensor(prod[:, k, :].rearrange("p (h d g) -> p h d g", g=FH, d=FD),
                                   att[:, k * n:(k + 1) * n, :].unsqueeze(2).to_broadcast([P, n, FD, FH]),
                                   v.unsqueeze(1).to_broadcast([P, n, FD, FH]), ALU.mult)\
                    .then_inc(done(f"b_pav{k}"), 1)

            def d_sums(h, t):
                if not there(t):
                    return
                if h == 0:
                    wait(pool, "d_sim", t)
                if h >= NSUM:
                    wait(pool, f"d_m{h - NSUM}", t)
                else:
                    wait(pool, f"d_m{h + (PH - 1 - h) // NSUM * NSUM}", t - 1)
                pool.tensor_tensor(sums[:, h % NSUM, :, :],
                                   sim[:, h, :].unsqueeze(2).to_broadcast([P, KEYS, KEYS]),
                                   sim[:, PH + h, :].unsqueeze(1).to_broadcast([P, KEYS, KEYS]), ALU.add)\
                    .then_inc(done(f"d_s{h}"), 1)

            pool.wait_ge(half_set, 1)

            def body(i):
                b_pow3(i - 2)
                d_pow2(i - 3)
                d_sums(7, i - 4)
                norm(0, i - 1)
                rsqrt_var("a", i)
                rsqrt_var("c", i - 2)
                d_sums(0, i - 3)
                d_sums(1, i - 3)
                norm(1, i - 2)
                rsqrt_var("b", i - 1)
                d_sums(2, i - 3)
                b_pow2(i - 1)
                d_sums(3, i - 3)
                b_qk(0, i - 1)
                b_qk(1, i - 1)
                norm(2, i - 2)
                d_sums(4, i - 3)
                b_av(0, i - 1)
                b_av(1, i - 1)
                d_sums(5, i - 3)
                rsqrt_var("d", i - 2)
                d_sums(6, i - 3)
            bodies(pool, body)

        @block.scalar
        def _(act):
            def turned(s, t):
                if not there(t):
                    return
                wait(act, f"{s}_txt", t)
                wait(act, {"a": "u0_sc", "b": "b_tqkv", "c": "u2_sc", "d": "d_ht1"}[s], t - 1)
                act.activation(xt[s][:, :], ps[:, {"a": BANK7, "b": BANK3, "c": BANK7, "d": BANK4}[s], 0:P],
                               ACT.Copy).then_inc(done(f"{s}_axt"), 1)

            def exps(u, t):
                if not there(t):
                    return
                wait(act, f"u{u}_max", t)
                vacated(act, f"u{u}_exp", t)
                wait(act, f"u{u}_rec", t - 1)
                for h in range(UNIT):
                    ins = act.activation(prob[u][:, h * CTX:(h + 1) * CTX],
                                         ps[:, h // 3, (h % 3) * CTX:(h % 3 + 1) * CTX], ACT.Exp,
                                         bias=nmax[:, u, h:h + 1], accum_out=rsum[:, u, h:h + 1])
                ins.then_inc(done(f"u{u}_exp"), 1)

            def prob_out(u, r, t):
                if not there(t):
                    return
                wait(act, f"u{u}_pt{r}", t)
                if r == 0:
                    vacated(act, f"u{u}_apt0", t)
                n = min(4, CHUNKS - 4 * r)
                act.activation(prob_t[:, 4 * r:4 * r + n, :], ps[:, BANK7, 0:n * P].rearrange("p (c n) -> p c n", n=P),
                               ACT.Copy).then_inc(done(f"u{u}_apt{r}"), 1)

            def d_sim(t):
                if not there(t):
                    return
                wait(act, "d_tsim", t)
                wait(act, "d_s7", t - 1)
                wait(act, "d_tr", t - 1)
                act.activation(sim[:, :, :], ps[:, BANK4, :].rearrange("p (n k) -> p n k", k=KEYS), ACT.Copy)\
                    .then_inc(done("d_sim"), 1)

            def d_gelu(t):
                if not there(t):
                    return
                wait(act, "d_ht0", t)
                wait(act, "d_out", t - 1)
                act.activation(gel[:, 0:4, :], ps[:, BANK4, :].rearrange("p (c n) -> p c n", n=P), ACT.Gelu)
                wait(act, "d_ht1", t)
                act.activation(gel[:, 4:8, :], ps[:, BANK3, :].rearrange("p (c n) -> p c n", n=P), ACT.Gelu)\
                    .then_inc(done("d_gel"), 1)

            def b_aexp(t):
                if not there(t):
                    return
                wait(act, "b_asub", t)
                act.activation(att[:, :, :], att[:, :, :], ACT.Exp).then_inc(done("b_aexp"), 1)

            def b_aavt(t):
                if not there(t):
                    return
                wait(act, "b_tavt", t)
                wait(act, "b_ty1", t - 1)
                act.activation(av_t[:, :], ps[:, BANK3, 0:P], ACT.Copy).then_inc(done("b_aavt"), 1)

            def b_sq(t):
                if not there(t):
                    return
                wait(act, "b_x2", t)
                wait(act, "b_eps3", t - 1)
                wait(act, "b_sq", t - 1)
                act.activation(sq[:, :], x2[:, :], ACT.Square, accum_out=b_sc[:, 2:3]).then_inc(done("b_sq"), 1)

            def b_ax2t(t):
                if not there(t):
                    return
                wait(act, "b_tx2t", t)
                act.activation(x2_t[:, :], ps[:, BANK3, 0:P], ACT.Copy).then_inc(done("b_ax2t"), 1)

            def b_gexp(t):
                if not there(t):
                    return
                wait(act, "b_gmax", t)
                wait(act, "b_gates", t - 1)
                act.activation(gate[:, 1, :], gate[:, 0, :], ACT.Exp, bias=b_sc[:, 5:6],
                               accum_out=b_sc[:, 6:7]).then_inc(done("b_gexp"), 1)

            def d_vexp(t):
                if not there(t):
                    return
                wait(act, "d_vs", t)
                act.activation(cexp[:, :, :], cexp[:, :, :], ACT.Exp).then_inc(done("d_vexp"), 1)

            def d_exp(h, t):
                if not there(t):
                    return
                wait(act, "d_vrec", t)
                wait(act, f"d_w{h - 2}" if h >= 2 else f"d_w{h + PH - 2}", t if h >= 2 else t - 1)
                act.activation(diag[:, h % 2, :], ident[:, :], ACT.Copy, scale=zinv[:, h:h + 1])\
                    .then_inc(done(f"d_g{h}"), 1)
                wait(act, f"d_s{h}", t)
                act.activation(wexp[:, h % NEXP, :], sums[:, h % NSUM, :, :].rearrange("p a b -> p (a b)"), ACT.Exp,
                               bias=neg1[:, h:h + 1]).then_inc(done(f"d_e{h}"), 1)

            def body(i):
                b_sq(i - 2)
                b_ax2t(i - 2)
                d_exp(6, i - 4)
                b_gexp(i - 2)
                turned("d", i - 3)
                d_sim(i - 3)
                d_exp(7, i - 4)
                prob_out(0,0, i - 1)
                turned("c", i - 2)
                prob_out(0,1, i - 1)
                prob_out(0,2, i - 1)
                exps(1, i - 2)
                d_vexp(i - 3)
                turned("a", i)
                d_exp(0, i - 3)
                d_exp(1, i - 3)
                prob_out(1,0, i - 2)
                turned("b", i - 1)
                prob_out(1,1, i - 2)
                exps(2, i - 2)
                prob_out(1,2, i - 2)
                d_exp(2, i - 3)
                d_gelu(i - 3)
                d_exp(3, i - 3)
                b_aexp(i - 1)
                prob_out(2,0, i - 2)
                prob_out(2,1, i - 2)
                d_exp(4, i - 3)
                prob_out(2,2, i - 2)
                exps(0, i)
                b_aavt(i - 1)
                d_exp(5, i - 3)
            bodies(act, body)

        @block.tensor
        def _(pe):
            def turn(s, t):
                if not there(t):
                    return
                wait(pe, f"{s}_xn", t)
                vacated(pe, f"{s}_txt", t)
                pe.transpose(ps[:, {"a": BANK7, "b": BANK3, "c": BANK7, "d": BANK4}[s], 0:P], xn[s][:, :],
                             ident[:, :]).then_inc(done(f"{s}_txt"), 1)

            def scores(u, t):
                if not there(t):
                    return
                s = U_OF[u]
                wait(pe, f"{s}_axt", t)
                vacated(pe, f"u{u}_sc", t)
                b = batch_of(t)
                at = 0
                for k, heads in enumerate(BANK_HEADS):
                    n = heads * CTX
                    rhs = G[:, b, u, at:at + n] if isinstance(b, int) else \
                        G[:, bass.ds(b, 1), u, at:at + n].rearrange("p a n -> p (a n)")
                    mm = pe.matmul(ps[:, k, 0:n], xt[s][:, :], rhs, start=True, stop=(s == "a"))
                    if s == "c":
                        far = far_row[:, b:b + 1, :] if isinstance(b, int) else far_row[:, bass.ds(b, 1), :]
                        mm = pe.matmul(ps[:, k, 0:n].rearrange("p (h m) -> p h m", m=CTX), ones_bf[:, :],
                                       far.to_broadcast([1, heads, CTX]), start=False, stop=True)
                    at += n
                mm.then_inc(done(f"u{u}_sc"), 1)

            def turn_prob(u, r, t):
                if not there(t):
                    return
                if r == 0:
                    wait(pe, f"u{u}_norm", t)
                vacated(pe, f"u{u}_pt{r}", t)
                for c in range(4 * r, min(4 * r + 4, CHUNKS)):
                    n = min(P, FLAT - c * P)
                    mm = pe.transpose(ps[0:n, BANK7, (c % 4) * P:(c % 4 + 1) * P], prob[u][:, c * P:c * P + n],
                                      ident[:, :])
                mm.then_inc(done(f"u{u}_pt{r}"), 1)

            def values(u, t):
                if not there(t):
                    return
                wait(pe, f"u{u}_apt2", t)
                vacated(pe, f"u{u}_out", t)
                b = batch_of(t)
                if u == 0:
                    pe.matmul(ps[:, BANK7, 0:D], ones_row[:, :], bout_g[:, :], start=True, stop=False)
                for c in range(CHUNKS):
                    n = min(P, FLAT - c * P)
                    rhs = VW[0:n, b, u, c * D:(c + 1) * D] if isinstance(b, int) else \
                        VW[0:n, bass.ds(b, 1), u, c * D:(c + 1) * D].rearrange("p a n -> p (a n)")
                    mm = pe.matmul(ps[:, BANK7, 0:D], prob_t[0:n, c, :], rhs, start=(c == 0 and u != 0),
                                   stop=(c == CHUNKS - 1))
                mm.then_inc(done(f"u{u}_out"), 1)

            def b_tqkv(t):
                if not there(t):
                    return
                wait(pe, "b_axt", t)
                vacated(pe, "b_tqkv", t)
                pe.matmul(ps[:, BANK3, 0:3 * D], xt["b"][:, :], wqkv[:, :], start=True, stop=True)\
                    .then_inc(done("b_tqkv"), 1)

            def b_tavt(t):
                if not there(t):
                    return
                wait(pe, "b_anorm", t)
                vacated(pe, "b_tavt", t)
                pe.transpose(ps[:, BANK3, 0:P], av[:, :], ident[:, :]).then_inc(done("b_tavt"), 1)

            def b_tatt(t):
                if not there(t):
                    return
                wait(pe, "b_aavt", t)
                vacated(pe, "b_tatt", t)
                pe.matmul(ps[:, BANK3, 0:D], ones_row[:, :], bo_row[:, :], start=True, stop=False)
                pe.matmul(ps[:, BANK3, 0:D], av_t[:, :], wo_f[:, :], start=False, stop=True)\
                    .then_inc(done("b_tatt"), 1)

            def b_tx2t(t):
                if not there(t):
                    return
                wait(pe, "b_x2", t)
                vacated(pe, "b_tx2t", t)
                pe.transpose(ps[:, BANK3, 0:P], x2[:, :], ident[:, :]).then_inc(done("b_tx2t"), 1)

            def b_tgate(t):
                if not there(t):
                    return
                wait(pe, "b_ax2t", t)
                vacated(pe, "b_tgate", t)
                pe.matmul(ps[:, BANK3, 0:EXPERTS], x2_t[:, :], wg[:, :], start=True, stop=True)\
                    .then_inc(done("b_tgate"), 1)

            def b_ty(r, t):
                if not there(t):
                    return
                vacated(pe, f"b_ty{r}", t)
                pe.matmul(ps[:, BANK3, :], x2_t[:, :], we[:, r * BANK:(r + 1) * BANK], start=True, stop=True)\
                    .then_inc(done(f"b_ty{r}"), 1)

            def d_tsim(t):
                if not there(t):
                    return
                wait(pe, "d_axt", t)
                vacated(pe, "d_tsim", t)
                pe.matmul(ps[:, BANK4, :], xt["d"][:, :], wc[:, :], start=True, stop=True).then_inc(done("d_tsim"), 1)

            def d_ht(r, t):
                if not there(t):
                    return
                wait(pe, "d_axt", t)
                vacated(pe, f"d_ht{r}", t)
                for c in range(4):
                    mm = pe.matmul(ps[:, BANK3 if r else BANK4, c * P:(c + 1) * P],
                                   down[:, (4 * r + c) * P:(4 * r + c + 1) * P], xt["d"][:, :], start=True, stop=True)
                mm.then_inc(done(f"d_ht{r}"), 1)

            def d_weights(h, t):
                if not there(t):
                    return
                wait(pe, f"d_m{h}", t)
                wait(pe, f"d_g{h}", t)
                if h == 0:
                    wait(pe, "d_gw", t - 1)
                for c in range(GRID // P):
                    mm = pe.matmul(ps[:, WBANK + c // 4, (c % 4) * P:(c % 4 + 1) * P],
                                   wexp[:, h % NEXP, c * P:(c + 1) * P], diag[:, h % 2, :],
                                   start=(h == 0 and c % 4 == 0), stop=(h == PH - 1), skip_group_check=True)
                mm.then_inc(done(f"d_w{h}"), 1)

            def d_out_(t):
                if not there(t):
                    return
                wait(pe, "d_gw", t)
                vacated(pe, "d_out", t)
                for c in range(GRID // P):
                    mm = pe.matmul(ps[:, BANK4, 0:D], gel[:, c, :], up[:, c, :], start=(c == 0),
                                   stop=(c == GRID // P - 1))
                mm.then_inc(done("d_out"), 1)

            def body(i):
                b_tatt(i - 2)
                b_tx2t(i - 2)
                b_tgate(i - 2)
                b_ty(0, i - 2)
                turn("d", i - 3)
                b_ty(1, i - 2)
                d_tsim(i - 3)
                d_weights(5, i - 4)
                turn_prob(0,0, i - 1)
                d_weights(6, i - 4)
                turn("c", i - 2)
                scores(1, i - 2)
                turn_prob(0,1, i - 1)
                turn_prob(0,2, i - 1)
                values(0, i - 1)
                d_weights(7, i - 4)
                turn("a", i)
                scores(2, i - 2)
                turn_prob(1,0, i - 2)
                d_out_(i - 4)
                turn("b", i - 1)
                turn_prob(1,1, i - 2)
                b_tqkv(i - 1)
                d_weights(0, i - 3)
                turn_prob(1,2, i - 2)
                d_weights(1, i - 3)
                d_ht(0, i - 3)
                d_ht(1, i - 3)
                values(1, i - 2)
                d_weights(2, i - 3)
                turn_prob(2,0, i - 2)
                scores(0, i)
                turn_prob(2,1, i - 2)
                d_weights(3, i - 3)
                turn_prob(2,2, i - 2)
                values(2, i - 2)
                b_tavt(i - 1)
                d_weights(4, i - 3)
            bodies(pe, body)

        @block.vector
        def _(dve):
            dve.memset(half[:, :], -0.5).then_inc(half_set, 1)

            def carry(n):
                dve.memset(carrier[:, n:n + 1], 0.0)

            def moments(s, t):
                if not there(t):
                    return
                before = {"b": "u0_res", "c": "b_res", "d": "u2_res"}
                if s in before:
                    wait(dve, before[s], t)
                wait(dve, f"{s}_xn", t - 1)
                wait(dve, f"{s}_aggr", t - 1)
                carry(10 + "abcd".index(s))
                dve.bn_stats(stat[s][:, :], x_of(t)).then_inc(done(f"{s}_stats"), 1)
                wait(dve, f"{s}_stats", t)
                carry("abcd".index(s))
                dve.bn_aggr(mv[s][:, :], stat[s][:, :]).then_inc(done(f"{s}_aggr"), 1)
                wait(dve, f"{s}_aggr", t)
                wait(dve, f"{s}_pow", t - 1)
                dve.tensor_scalar(var[s][:, :], mv[s][:, 1:2], 1e-5, None, ALU.add).then_inc(done(f"{s}_eps"), 1)

            def normed(s, t):
                if not there(t):
                    return
                if s != "d":
                    wait(dve, f"{s}_pow", t)
                wait(dve, f"{s}_txt", t - 1)
                if s == "b":
                    wait(dve, "b_x2", t - 1)
                dve.tensor_scalar(xn[s][:, :], x_of(t), mv[s][:, 0:1], d_sc[:, 3:4] if s == "d" else rs[s][:, :],
                                  ALU.subtract, ALU.mult).then_inc(done(f"{s}_xn"), 1)

            def b_moments2(t):
                if not there(t):
                    return
                wait(dve, "b_pow", t)
                wait(dve, "b_pow2", t - 1)
                dve.tensor_scalar(b_sc[:, 0:1], mv["b"][:, 1:2], rs["b"][:, :], rs["b"][:, :], ALU.mult, ALU.mult)\
                    .then_inc(done("b_vr"), 1)
                wait(dve, "b_vr", t)
                dve.tensor_scalar(b_sc[:, 0:1], b_sc[:, 0:1], 1e-6, None, ALU.add).then_inc(done("b_vr2"), 1)

            def d_moments2(t):
                if not there(t):
                    return
                wait(dve, "d_pow", t)
                wait(dve, "d_pow2", t - 1)
                dve.tensor_scalar(d_sc[:, 0:1], mv["d"][:, 1:2], rs["d"][:, :], rs["d"][:, :], ALU.mult, ALU.mult)\
                    .then_inc(done("d_vr"), 1)
                wait(dve, "d_vr", t)
                dve.tensor_scalar(d_sc[:, 0:1], d_sc[:, 0:1], float(D), 1e-24, ALU.mult, ALU.max)\
                    .then_inc(done("d_n2"), 1)

            def d_scale(t):
                if not there(t):
                    return
                wait(dve, "d_pow2", t)
                wait(dve, "d_xn", t - 1)
                dve.tensor_scalar(d_sc[:, 3:4], d_sc[:, 1:2], rs["d"][:, :], float(D) ** 0.5, ALU.mult, ALU.mult)\
                    .then_inc(done("d_sc"), 1)
                wait(dve, "d_sc", t)
                normed("d", t)

            def unit_max(u, t):
                if not there(t):
                    return
                wait(dve, f"u{u}_sc", t)
                wait(dve, f"u{u}_exp", t - 1)
                dve.tensor_reduce(nmax[:, u, 0:6], ps[:, 0:2, 0:3 * CTX].rearrange("p k (h m) -> p k h m", m=CTX),
                                  X_AXIS, ALU.max, negate=True)
                dve.tensor_reduce(nmax[:, u, 6:8], ps[:, 2, 0:2 * CTX].rearrange("p (h m) -> p h m", m=CTX),
                                  X_AXIS, ALU.max, negate=True).then_inc(done(f"u{u}_max"), 1)

            def unit_rec(u, t):
                if not there(t):
                    return
                wait(dve, f"u{u}_exp", t)
                wait(dve, f"u{u}_norm", t - 1)
                dve.reciprocal(rinv[:, u, :], rsum[:, u, :]).then_inc(done(f"u{u}_rec"), 1)

            def unit_res(u, t):
                if not there(t):
                    return
                wait(dve, f"u{u}_out", t)
                if u == 1:
                    wait(dve, "b_res", t)
                if u == 2:
                    wait(dve, "u1_res", t)
                dve.tensor_tensor(x_of(t), x_of(t), ps[:, BANK7, 0:D], ALU.add).then_inc(done(f"u{u}_res"), 1)

            def b_qkv(t):
                if not there(t):
                    return
                wait(dve, "b_pow2", t)
                wait(dve, "b_tqkv", t)
                wait(dve, "b_pav1", t - 1)
                dve.scalar_tensor_tensor(out=qkv[:, :], in0=ps[:, BANK3, 0:3 * D], scalar=b_sc[:, 1:2], in1=bqkv[:, :],
                                         op0=ALU.mult, op1=ALU.add).then_inc(done("b_qkv"), 1)

            def b_sum_qk(k, t):
                if not there(t):
                    return
                wait(dve, f"b_pqk{k}", t)
                if k == 0:
                    wait(dve, "b_pav1", t - 1)
                    wait(dve, "b_asum", t - 1)
                n = FH // 2
                dve.tensor_reduce(att[:, n * k:n * (k + 1), :], prod[:, k, :].rearrange("p (h g d) -> p h g d", g=FH, d=FD),
                                  X_AXIS, ALU.add).then_inc(done(f"b_qk{k}"), 1)

            def b_sum_av(k, t):
                if not there(t):
                    return
                wait(dve, f"b_pav{k}", t)
                if k == 0:
                    wait(dve, "b_tavt", t - 1)
                n = FH // 2
                dve.tensor_reduce(av[:, n * FD * k:n * FD * (k + 1)].rearrange("p (h d) -> p h d", d=FD),
                                  prod[:, k, :].rearrange("p (h d g) -> p h d g", g=FH, d=FD),
                                  X_AXIS, ALU.add).then_inc(done(f"b_av{k}"), 1)

            def b_shift(t):
                if not there(t):
                    return
                wait(dve, "b_qk1", t)
                dve.tensor_reduce(amax[:, :], att[:, :, :], X_AXIS, ALU.max).then_inc(done("b_amax"), 1)
                wait(dve, "b_amax", t)
                dve.tensor_tensor(att[:, :, :], att[:, :, :], amax[:, :].unsqueeze(2).to_broadcast([P, FH, FH]),
                                  ALU.subtract).then_inc(done("b_asub"), 1)

            def b_sum(t):
                if not there(t):
                    return
                wait(dve, "b_aexp", t)
                wait(dve, "b_anorm", t - 1)
                dve.tensor_reduce(asum[:, :], att[:, :, :], X_AXIS, ALU.add).then_inc(done("b_asum"), 1)
                wait(dve, "b_asum", t)
                dve.reciprocal(arec[:, :], asum[:, :]).then_inc(done("b_arec"), 1)

            def b_norm(t):
                if not there(t):
                    return
                wait(dve, "b_av1", t)
                wait(dve, "b_arec", t)
                o = av[:, :].rearrange("p (h d) -> p h d", d=FD)
                dve.tensor_tensor(o, o, arec[:, :].unsqueeze(2).to_broadcast([P, FH, FD]), ALU.mult)\
                    .then_inc(done("b_anorm"), 1)

            def b_x2(t):
                if not there(t):
                    return
                wait(dve, "b_tatt", t)
                wait(dve, "b_res", t - 1)
                dve.tensor_tensor(x2[:, :], xn["b"][:, :], ps[:, BANK3, 0:D], ALU.add).then_inc(done("b_x2"), 1)

            def b_mean_square(t):
                if not there(t):
                    return
                wait(dve, "b_sq", t)
                wait(dve, "b_pow3", t - 1)
                dve.tensor_scalar(b_sc[:, 3:4], b_sc[:, 2:3], 1.0 / D, 1e-6, ALU.mult, ALU.add)\
                    .then_inc(done("b_eps3"), 1)

            def b_logits(t):
                if not there(t):
                    return
                wait(dve, "b_pow3", t)
                wait(dve, "b_tgate", t)
                wait(dve, "b_gexp", t - 1)
                dve.scalar_tensor_tensor(out=gate[:, 0, :], in0=ps[:, BANK3, 0:EXPERTS], scalar=b_sc[:, 4:5],
                                         in1=bg[:, :], op0=ALU.mult, op1=ALU.add).then_inc(done("b_glog"), 1)
                wait(dve, "b_glog", t)
                dve.tensor_reduce(b_sc[:, 5:6], gate[:, 0, :], X_AXIS, ALU.max, negate=True)\
                    .then_inc(done("b_gmax"), 1)

            def b_gates(t):
                if not there(t):
                    return
                wait(dve, "b_gexp", t)
                dve.reciprocal(b_sc[:, 7:8], b_sc[:, 6:7]).then_inc(done("b_grec"), 1)
                wait(dve, "b_grec", t)
                wait(dve, "b_y7", t - 1)
                dve.tensor_scalar(gate[:, 2, :], gate[:, 1, :], b_sc[:, 7:8], b_sc[:, 4:5], ALU.mult, ALU.mult)\
                    .then_inc(done("b_gates"), 1)

            def b_experts(r, t):
                if not there(t):
                    return
                wait(dve, f"b_ty{r}", t)
                for e in range(4 * r, 4 * r + 4):
                    wait(dve, f"b_y{e - 1}" if e else "b_gates", t)
                    if e == 0:
                        wait(dve, "b_tx2t", t)
                        wait(dve, "b_sq", t)
                    dve.scalar_tensor_tensor(out=x2[:, :], in0=ps[:, BANK3, (e % 4) * D:(e % 4 + 1) * D],
                                             scalar=gate[:, 2, e:e + 1], in1=x2[:, :], op0=ALU.mult, op1=ALU.add)\
                        .then_inc(done(f"b_y{e}"), 1)

            def b_res(t):
                if not there(t):
                    return
                wait(dve, "b_y7", t)
                dve.scalar_tensor_tensor(out=x_of(t), in0=x2[:, :], scalar=tg[:, 2:3], in1=x_of(t), op0=ALU.mult,
                                         op1=ALU.add).then_inc(done("b_res"), 1)

            def d_top(part, t):
                if not there(t):
                    return
                if part == 0:
                    wait(dve, "d_sim", t)
                    wait(dve, "d_cand", t - 1)
                else:
                    wait(dve, ["d_ta", "d_tr"][part - 1], t)
                carry(4 + part)
                for n in range(2 * PH):
                    if part == 0:
                        ins = dve.max(best[:, n, 0:8], sim[:, n, :])
                    elif part == 1:
                        ins = dve.match_replace(rest[:, n, :], best[:, n, 0:8], sim[:, n, :], LOW)
                    else:
                        ins = dve.max(best[:, n, 8:16], rest[:, n, :])
                ins.then_inc(done(["d_ta", "d_tr", "d_tb"][part]), 1)

            def d_ctop(part, t):
                if not there(t):
                    return
                wait(dve, ["d_cand", "d_ca", "d_cr"][part], t)
                if part == 0:
                    wait(dve, "d_m7", t - 1)
                carry(7 + part)
                for h in range(PH):
                    if part == 0:
                        ins = dve.max(cbest[:, h, 0:8], cand[:, h, :])
                    elif part == 1:
                        ins = dve.match_replace(cand[:, h, :], cbest[:, h, 0:8], cand[:, h, :], LOW)
                    else:
                        ins = dve.max(cbest[:, h, 8:16], cand[:, h, :])
                ins.then_inc(done(["d_ca", "d_cr", "d_cb"][part]), 1)

            def d_cands(t):
                if not there(t):
                    return
                wait(dve, "d_tb", t)
                wait(dve, "d_cb", t - 1)
                at, i = 0, 0
                while i < TOP:
                    n = STAIRS[i]
                    k = sum(1 for m in STAIRS if m == n)
                    o = cand[:, :, at:at + k * n].rearrange("p h (i j) -> p h i j", j=n)
                    ins = dve.tensor_tensor(o, best[:, 0:PH, i:i + k].unsqueeze(3).to_broadcast([P, PH, k, n]),
                                            best[:, PH:2 * PH, 0:n].unsqueeze(2).to_broadcast([P, PH, k, n]), ALU.add)
                    at += k * n
                    i += k
                ins.then_inc(done("d_cand"), 1)

            def d_shift(t):
                if not there(t):
                    return
                wait(dve, "d_cb", t)
                wait(dve, "d_e7", t - 1)
                dve.tensor_scalar(neg1[:, :].unsqueeze(2), cbest[:, :, 0:1], -1.0, None, ALU.mult)\
                    .then_inc(done("d_nv"), 1)
                wait(dve, "d_vsum", t - 1)
                dve.tensor_tensor(cexp[:, :, :], cbest[:, :, :], cbest[:, :, 0:1].to_broadcast([P, PH, TOP]),
                                  ALU.subtract).then_inc(done("d_vs"), 1)

            def d_zinv(t):
                if not there(t):
                    return
                wait(dve, "d_vexp", t)
                dve.tensor_reduce(zsum[:, :], cexp[:, :, :], X_AXIS, ALU.add).then_inc(done("d_vsum"), 1)
                wait(dve, "d_vsum", t)
                wait(dve, "d_g7", t - 1)
                dve.reciprocal(zinv[:, :], zsum[:, :]).then_inc(done("d_vrec"), 1)

            def d_mask(h, t):
                if not there(t):
                    return
                wait(dve, f"d_e{h}", t)
                wait(dve, "d_cb", t)
                wx = wexp[:, h % NEXP, :]
                dve.scalar_tensor_tensor(out=wx, in0=sums[:, h % NSUM, :, :].rearrange("p a b -> p (a b)"),
                                         scalar=cbest[:, h, TOP - 1:TOP], in1=wx, op0=ALU.is_ge, op1=ALU.mult)\
                    .then_inc(done(f"d_m{h}"), 1)

            def d_gw(t):
                if not there(t):
                    return
                wait(dve, "d_w7", t)
                wait(dve, "d_gel", t)
                g = gel[:, :, :].rearrange("p (k c) n -> p k (c n)", k=2)
                dve.tensor_tensor(g, g, ps[:, WBANK:WBANK + 2, :], ALU.mult).then_inc(done("d_gw"), 1)

            def d_fin(t):
                if not there(t):
                    return
                wait(dve, "d_out", t)
                dve.tensor_tensor(x_of(t), x_of(t), ps[:, BANK4, 0:D], ALU.add).then_inc(done("d_fin"), 1)

            def body(i):
                moments("a", i)
                b_x2(i - 2)
                d_moments2(i - 3)
                unit_rec(0, i - 1)
                b_mean_square(i - 2)
                d_mask(5, i - 4)
                b_logits(i - 2)
                d_scale(i - 3)
                b_gates(i - 2)
                b_experts(0, i - 2)
                d_mask(6, i - 4)
                b_experts(1, i - 2)
                b_res(i - 2)
                moments("c", i - 2)
                d_top(0, i - 3)
                normed("c", i - 2)
                d_top(1, i - 3)
                d_mask(7, i - 4)
                d_top(2, i - 3)
                unit_max(1, i - 2)
                d_cands(i - 3)
                d_ctop(0, i - 3)
                d_ctop(1, i - 3)
                d_ctop(2, i - 3)
                d_shift(i - 3)
                normed("a", i)
                unit_rec(1, i - 2)
                unit_res(0, i - 1)
                d_zinv(i - 3)
                moments("b", i - 1)
                d_gw(i - 4)
                d_mask(0, i - 3)
                b_moments2(i - 1)
                d_mask(1, i - 3)
                normed("b", i - 1)
                unit_max(2, i - 2)
                d_fin(i - 4)
                b_qkv(i - 1)
                b_sum_qk(0, i - 1)
                unit_rec(2, i - 2)
                d_mask(2, i - 3)
                b_sum_qk(1, i - 1)
                b_shift(i - 1)
                unit_res(1, i - 2)
                d_mask(3, i - 3)
                b_sum(i - 1)
                unit_max(0, i)
                b_sum_av(0, i - 1)
                d_mask(4, i - 3)
                b_sum_av(1, i - 1)
                b_norm(i - 1)
                unit_res(2, i - 2)
                moments("d", i - 2)
            bodies(dve, body)


def kernel(**inputs):
    import numpy as np
    import concourse.bacc as bacc
    from concourse.bass_utils import run_bass_kernel_spmd

    a = {k: np.asarray(v) for k, v in inputs.items()}

    def by_head(w):
        return w.reshape(UNIT, HD0, w.shape[1]).transpose(1, 0, 2)

    def chunks(w):
        return w.reshape(-1, P, w.shape[1]).transpose(1, 0, 2)

    ctx_t = np.zeros((BATCH, CD, 2 * P + CTX), np.float32)
    ctx_t[:, :, P:P + CTX] = a["ctx_768"].transpose(0, 2, 1)
    rows = np.concatenate([a["L0_xattn_bout"], a["L0_ffn_bq"], a["L0_ffn_bup"], a["L0_ffn_bo"], a["L0_ffn_bg"],
                           a["g_xattn"], a["g_ffn"]])
    arrays = {
        "x": chunks(a["x"].reshape(-1, D)),
        "ctx_t": ctx_t,
        "mask": np.broadcast_to(a["mask_BxS2_bf1"].view(np.uint8)[None], (P, BATCH, CTX)),
        "rows": np.broadcast_to(rows[None], (P, ROW_TOTAL)),
        "cols": np.stack([a["L0_ffn_gamma1"], a["L0_ffn_gamma2"], a["L1_ffn_gamma"]], 1),
        "wk0": a["L0_xattn_Wk"],
        "wqt0": by_head(a["L0_xattn_Wq"].T),
        "wvt0": by_head(a["L0_xattn_Wv"].T),
        "wout0": by_head(a["L0_xattn_Wout"]),
        "f_wq": a["L0_ffn_Wq"],
        "f_wdt": a["L0_ffn_Wdown"].T,
        "f_wup": a["L0_ffn_Wup"],
        "f_bd": np.broadcast_to(a["L0_ffn_bdown"][:, None], (64, P)),
        "f_wo": a["L0_ffn_Wo"],
        "f_wg": a["L0_ffn_Wg"],
        "f_we": a["L0_ffn_We"].transpose(1, 0, 2).reshape(D, EXPERTS * D),
        "wk1": a["L1_xattn_Wk"],
        "wqt1": a["L1_xattn_Wq"].T,
        "wvt1": a["L1_xattn_Wv"].T,
        "wo1": a["L1_xattn_Wo"],
        "pk_wq": a["L1_ffn_wq"].reshape(2 * PH, PK, D).transpose(1, 0, 2),
        "pk_keys": a["L1_ffn_keys"].transpose(3, 2, 0, 1).reshape(PK, 2 * PH, KEYS),
        "pk_down": a["L1_ffn_table_down"][:GRID].T,
        "pk_up": chunks(a["L1_ffn_table_up"][:GRID]),
    }
    nc = bacc.Bacc("TRN2", target_bir_lowering=False, num_devices=1)
    feed, args = {}, []
    for name, value in arrays.items():
        value = np.ascontiguousarray(value)
        feed[f"in_{name}"] = value
        args.append(nc.dram_tensor(f"in_{name}", value.shape, mybir.dt.from_np(value.dtype), kind="ExternalInput").ap())
    args.append(nc.dram_tensor("out_x", (TILES, P, D), F32, kind="ExternalOutput").ap())
    flamingo_kernel(nc, *args)
    got = run_bass_kernel_spmd(nc, [feed], core_ids=[0])
    return got.results[0]["out_x"].reshape(BATCH, SEQ, D)
```

```python
from contextlib import ExitStack

import concourse.bass as bass
from concourse import mybir

F32 = mybir.dt.float32
BF16 = mybir.dt.bfloat16
U8 = mybir.dt.uint8
ALU = mybir.AluOpType
ACT = mybir.ActivationFunctionType
X_AXIS = mybir.AxisListType.X

P = 128
BANK = 512
BATCH, SEQ, D = 4, 512, 128
CTX, CD = 154, 96
TILES = BATCH * SEQ // P
PER_BATCH = SEQ // P
UNIT = 8
FLAT = UNIT * CTX
CHUNKS = -(-FLAT // P)
TAIL = FLAT - (CHUNKS - 1) * P
HD0, HD1 = 64, 8
FH, FD = 16, 8
EXPERTS = 8
PH, KEYS, PK, TOP = 8, 32, 64, 16
GRID = KEYS * KEYS
STAIRS = [TOP // (i + 1) for i in range(TOP)]
CANDS = sum(STAIRS)
LOW = -3.0e38
FAR = -(2.0 ** 126)
BANK_HEADS = [3, 3, 2]

ROW_SIZES = [("bout", D), ("bq", D), ("bup", 2 * D), ("bo", D), ("bg", EXPERTS), ("gx", 2), ("gf", 2)]
ROWS = {}
_at = 0
for _name, _size in ROW_SIZES:
    ROWS[_name] = (_at, _at + _size)
    _at += _size
ROW_TOTAL = _at


class Steps:

    def __init__(self, sem, names):
        self.sem = sem
        self.names = names.split()
        self.n = 0

    def __call__(self, name):
        assert self.names[self.n % len(self.names)] == name, (self.names[self.n % len(self.names)], name)
        self.n += 1
        return self.sem

    def after(self, name, tile):
        return tile * len(self.names) + (self.names.index(name) + 1)


def flamingo_kernel(nc, d_x, d_ctx_t, d_mask, d_rows, d_cols, d_wk0, d_wqt0, d_wvt0, d_wout0, d_f_wq, d_f_wdt, d_f_wup, d_f_bd, d_f_wo, d_f_wg, d_f_we, d_wk1, d_wqt1, d_wv1, d_wo1, d_pk_wq, d_pk_keys, d_pk_down, d_pk_up, d_out):
    es = ExitStack()
    with es:
        def sb(name, shape, dt=F32, stack=es):
            return stack.enter_context(nc.sbuf_tensor(name, shape, dt))

        def sem(name):
            return es.enter_context(nc.semaphore(name))

        ps = es.enter_context(nc.psum_tensor("ps", [P, 8, BANK], F32))

        xs = sb("xs", [P, TILES, D])
        G = sb("G", [P, BATCH, 3, FLAT])
        VW = sb("VW", [P, BATCH, 3, CHUNKS * D])
        far_row = sb("far_row", [1, BATCH, CTX], BF16)
        bo_row = sb("bo_row", [1, D])
        bg = sb("bg", [P, EXPERTS])
        col_sb = sb("col_sb", [P, 3])
        tg = sb("tg", [P, 4])
        ident = sb("ident", [P, P])
        ones_row = sb("ones_row", [1, P])
        ones_bf = sb("ones_bf", [1, P], BF16)
        wqkv = sb("wqkv", [P, 3 * D])
        bqkv = sb("bqkv", [P, 3 * D])
        wo_f = sb("wo_f", [P, D])
        bout_g = sb("bout_g", [1, D])
        wg = sb("wg", [P, EXPERTS])
        we = sb("we", [P, EXPERTS * D])
        wc = sb("wc", [P, 2 * PH * KEYS])
        down = sb("down", [P, GRID])
        up = sb("up", [P, GRID // P, D])

        def bank(n, cols=BANK):
            return ps[:, n, 0:cols]


        with ExitStack() as tmp:
            def scratch(name, shape, dt=F32):
                return tmp.enter_context(nc.sbuf_tensor(name, shape, dt))

            row_sb = scratch("row_sb", [P, ROW_TOTAL])

            def row(name):
                a, b = ROWS[name]
                return row_sb[:, a:b]

            cbuf = scratch("cbuf", [CD, 2 * P + CTX])
            wk0 = scratch("wk0", [CD, 4 * P])
            wqt0 = scratch("wqt0", [HD0, UNIT, D])
            wvt0 = scratch("wvt0", [HD0, UNIT, CD])
            wout0 = scratch("wout0", [HD0, UNIT, D])
            wk1 = scratch("wk1", [CD, D])
            wqt1 = scratch("wqt1", [P, D])
            wv1 = scratch("wv1", [CD, P])
            wo1 = scratch("wo1", [P, D])
            f_wdt = scratch("f_wdt", [64, D])
            f_wup = scratch("f_wup", [64, 2 * D])
            f_bd = scratch("f_bd", [64, P])
            pk_wq = scratch("pk_wq", [PK, 2 * PH, D])
            pk_keys = scratch("pk_keys", [PK, 2 * PH, KEYS])
            blk = scratch("blk", [P, 2 * UNIT])
            cw = scratch("cw", [CD, UNIT * D])
            kt0 = scratch("kt0", [HD0, UNIT, CTX])
            kt1 = scratch("kt1", [P, CTX])
            vt1 = row_sb[:, 0:CTX]
            k_blk = scratch("k_blk", [P, 2 * UNIT, CTX])
            v_blk = scratch("v_blk", [P, 2 * UNIT, CTX])
            mask8 = scratch("mask8", [P, BATCH, CTX], U8)

            ctx_in, fold_in, small, wt = sem("ctx_in"), sem("loaded_folded"), sem("loaded_small"), sem("loaded_weights")
            late, xt_in = sem("loaded_tables"), sem("loaded_x")
            V = Steps(sem("fold_v"), "wq bq bout bo bg wg we far_row wdu bkv wc down up")
            A = Steps(sem("fold_a"), "tanh cw0")
            T = Steps(sem("fold_t"), "wdu wc cw0")
            I = Steps(sem("const_p"), "z1 z2 o1 o2 eye b1 b2")
            BT = Steps(sem("ctx_t"), "k vw0 g0 vw1 g1 vw2 g2")
            BV = Steps(sem("ctx_v"), "kt1 v_blk vw0 k_blk vw1 vw2")
            BA = Steps(sem("ctx_a"), "kt0 g0 g1 g2")
            NF, NS, NW, NL = 5, 5, 8, 3

            block = tmp.enter_context(nc.Block())

            @block.sync
            def _(sp):
                sp.dma_start(f_wdt[:, :], d_f_wdt).then_inc(fold_in, 16)
                sp.dma_start(f_wup[:, :], d_f_wup).then_inc(fold_in, 16)
                sp.dma_start(f_bd[:, :], d_f_bd).then_inc(fold_in, 16)
                sp.dma_start(pk_wq[:, :, :], d_pk_wq).then_inc(fold_in, 16)
                sp.dma_start(pk_keys[:, :, :], d_pk_keys).then_inc(fold_in, 16)
                sp.dma_start(row_sb[:, :], d_rows).then_inc(small, 16)
                sp.dma_start(col_sb[:, :], d_cols).then_inc(small, 16)
                sp.dma_start(mask8[:, :, :], d_mask).then_inc(small, 16)
                sp.dma_start(wqkv[:, 0:D], d_f_wq).then_inc(small, 16)
                sp.dma_start(wg[:, :], d_f_wg).then_inc(small, 16)
                sp.dma_start(cbuf[:, :], d_ctx_t[0, :, :]).then_inc(ctx_in, 16)
                with sp.Fori(1, BATCH) as b:
                    sp.wait_ge(BT.sem, BT.after("vw2", b - 1))
                    sp.dma_start(cbuf[:, :], d_ctx_t[bass.ds(b, 1), :, :].rearrange("a c m -> (a c) m"))\
                        .then_inc(ctx_in, 16)
                sp.wait_ge(xt_in, 32)

            @block.scalar
            def _(act):
                act.dma_start(wvt0[:, :, :], d_wvt0).then_inc(wt, 16)
                act.dma_start(wout0[:, :, :], d_wout0).then_inc(wt, 16)
                act.dma_start(wv1[:, :], d_wv1).then_inc(wt, 16)
                act.dma_start(wo1[:, :], d_wo1).then_inc(wt, 16)
                act.dma_start(wk0[:, :], d_wk0).then_inc(wt, 16)
                act.dma_start(wqt0[:, :, :], d_wqt0).then_inc(wt, 16)
                act.dma_start(wk1[:, :], d_wk1).then_inc(wt, 16)
                act.dma_start(wqt1[:, :], d_wqt1).then_inc(wt, 16)
                act.dma_start(we[:, :], d_f_we).then_inc(late, 16)
                act.dma_start(down[:, :], d_pk_down).then_inc(late, 16)
                act.dma_start(up[:, :, :], d_pk_up).then_inc(late, 16)
                act.dma_start(wo_f[:, :], d_f_wo).then_inc(xt_in, 16)
                act.dma_start(xs[:, :, :], d_x).then_inc(xt_in, 16)
                act.wait_ge(small, 16 * NS)
                act.activation(tg[:, 0:2], row("gx"), ACT.Tanh)
                act.activation(tg[:, 2:4], row("gf"), ACT.Tanh).then_inc(A("tanh"), 1)
                act.wait_ge(A.sem, A.after("tanh", 0))
                act.wait_ge(T.sem, T.after("cw0", 0))
                act.activation(cw[:, :], ps[0:CD, 2:4, :].rearrange("p k n -> p (k n)"), ACT.Copy,
                               scale=tg[0:CD, 0:1]).then_inc(A("cw0"), 1)
                with act.Fori(0, BATCH) as b:
                    act.wait_ge(BT.sem, BT.after("k", b))
                    act.activation(kt0[:, 0:6, :].rearrange("p (k h) m -> p k (h m)", k=2), ps[0:HD0, 0:2, 0:3 * CTX],
                                   ACT.Copy, scale=HD0 ** -0.5)
                    act.activation(kt0[:, 6:8, :].rearrange("p h m -> p (h m)"), ps[0:HD0, 2, 0:2 * CTX], ACT.Copy,
                                   scale=HD0 ** -0.5)
                    act.wait_ge(BV.sem, BV.after("kt1", b))
                    act.activation(vt1, ps[:, 3, CTX:2 * CTX], ACT.Copy, scale=tg[:, 1:2]).then_inc(BA("kt0"), 1)
                    for u in range(3):
                        act.wait_ge(BT.sem, BT.after(f"g{u}", b))
                        act.activation(G[:, bass.ds(b, 1), u, 0:6 * CTX].rearrange("p a (k n) -> p (a k) n", k=2),
                                       ps[:, 2:4, 0:3 * CTX], ACT.Copy)
                        act.activation(G[:, bass.ds(b, 1), u, 6 * CTX:FLAT], ps[:, 4:5, 0:2 * CTX], ACT.Copy)\
                            .then_inc(BA(f"g{u}"), 1)

            @block.gpsimd
            def _(pool):
                pool.memset(ident[:, :], 0.0).then_inc(I("z1"), 1)
                pool.memset(blk[:, :], 1.0).then_inc(I("z2"), 1)
                pool.memset(ones_row[:, :], 1.0).then_inc(I("o1"), 1)
                pool.memset(ones_bf[:, :], 1.0).then_inc(I("o2"), 1)
                pool.wait_ge(I.sem, I.after("z1", 0))
                pool.affine_select(out=ident[:, :], in_=ident[:, :], compare_op=ALU.not_equal, fill=1.0, base=0,
                                   pattern=[[-1, P]], channel_multiplier=1).then_inc(I("eye"), 1)
                pool.wait_ge(I.sem, I.after("z2", 0))
                pool.affine_select(out=blk[:, :], in_=blk[:, :], compare_op=ALU.is_ge, fill=0.0, base=0,
                                   pattern=[[-HD1, 2 * UNIT]], channel_multiplier=1).then_inc(I("b1"), 1)
                pool.wait_ge(I.sem, I.after("b1", 0))
                pool.affine_select(out=blk[:, :], in_=blk[:, :], compare_op=ALU.is_ge, fill=0.0, base=HD1 - 1,
                                   pattern=[[HD1, 2 * UNIT]], channel_multiplier=-1).then_inc(I("b2"), 1)

            @block.vector
            def _(dve):
                g1, g2, g3 = col_sb[:, 0:1], col_sb[:, 1:2], col_sb[:, 2:3]
                dve.wait_ge(small, 16 * NS)
                dve.tensor_scalar(wqkv[:, 0:D], wqkv[:, 0:D], g1, FD ** -0.5, ALU.mult, ALU.mult).then_inc(V("wq"), 1)
                dve.tensor_scalar(bqkv[:, 0:D], row("bq"), FD ** -0.5, None, ALU.mult).then_inc(V("bq"), 1)
                dve.wait_ge(A.sem, A.after("tanh", 0))
                dve.tensor_scalar(bout_g[:, :], row_sb[0:1, 0:D], tg[0:1, 0:1], None, ALU.mult)\
                    .then_inc(V("bout"), 1)
                dve.tensor_copy(bo_row[:, :], row("bo")[0:1, :]).then_inc(V("bo"), 1)
                dve.tensor_copy(bg[:, :], row("bg")).then_inc(V("bg"), 1)
                dve.tensor_scalar(wg[:, :], wg[:, :], g2, None, ALU.mult).then_inc(V("wg"), 1)
                dve.wait_ge(late, 16 * NL)
                dve.tensor_scalar(we[:, :], we[:, :], g2, None, ALU.mult).then_inc(V("we"), 1)
                dve.tensor_scalar(far_row[:, :, :], mask8[0:1, :, :], -1.0, -FAR, ALU.add, ALU.mult)\
                    .then_inc(V("far_row"), 1)
                dve.wait_ge(T.sem, T.after("wdu", 0))
                dve.tensor_scalar(wqkv[:, D:3 * D], ps[:, 0, 0:2 * D], g1, None, ALU.mult).then_inc(V("wdu"), 1)
                dve.tensor_tensor(bqkv[:, D:3 * D], ps[:, 0, 2 * D:4 * D], row("bup"), ALU.add).then_inc(V("bkv"), 1)
                dve.wait_ge(T.sem, T.after("wc", 0))
                dve.tensor_scalar(wc[:, :], ps[:, 1, :], g3, None, ALU.mult).then_inc(V("wc"), 1)
                dve.tensor_scalar(down[:, :], down[:, :], g3, None, ALU.mult).then_inc(V("down"), 1)
                dve.tensor_scalar(up[:, :, :], up[:, :, :], tg[:, 3:4], None, ALU.mult).then_inc(V("up"), 1)
                dve.wait_ge(I.sem, I.after("b2", 0))
                with dve.Fori(0, BATCH) as b:
                    dve.wait_ge(BT.sem, BT.after("k", b))
                    dve.scalar_tensor_tensor(out=kt1[:, :].unsqueeze(1), in0=ps[:, 3:4, 0:CTX],
                                             scalar=HD1 ** -0.5, in1=mask8[:, bass.ds(b, 1), :], op0=ALU.mult,
                                             op1=ALU.mult).then_inc(BV("kt1"), 1)
                    dve.wait_ge(BA.sem, BA.after("kt0", b))
                    dve.tensor_tensor(v_blk[:, :, :], vt1.unsqueeze(1).to_broadcast([P, 2 * UNIT, CTX]),
                                      blk[:, :].unsqueeze(2).to_broadcast([P, 2 * UNIT, CTX]), ALU.mult)\
                        .then_inc(BV("v_blk"), 1)
                    for u in range(3):
                        dve.wait_ge(BT.sem, BT.after(f"vw{u}", b))
                        dve.tensor_copy(VW[:, bass.ds(b, 1), u, 0:2 * BANK].rearrange("p a (k n) -> p (a k) n", k=2),
                                        ps[:, 5:7, :])
                        dve.tensor_copy(VW[:, bass.ds(b, 1), u, 2 * BANK:CHUNKS * D], ps[:, 7:8, 0:2 * D])\
                            .then_inc(BV(f"vw{u}"), 1)
                        if u == 0:
                            dve.wait_ge(BV.sem, BV.after("kt1", b))
                            dve.tensor_tensor(k_blk[:, :, :], kt1[:, :].unsqueeze(1).to_broadcast([P, 2 * UNIT, CTX]),
                                              blk[:, :].unsqueeze(2).to_broadcast([P, 2 * UNIT, CTX]), ALU.mult)\
                                .then_inc(BV("k_blk"), 1)

            @block.tensor
            def _(pe):
                pe.wait_ge(fold_in, 16 * NF)
                pe.matmul(ps[:, 0, 0:2 * D], f_wdt[:, :], f_wup[:, :], start=True, stop=True)
                pe.matmul(ps[:, 0, 2 * D:4 * D], f_bd[:, :], f_wup[:, :], start=True, stop=True).then_inc(T("wdu"), 1)
                for n in range(2 * PH):
                    mm = pe.matmul(ps[:, 1, n * KEYS:(n + 1) * KEYS], pk_wq[:, n, :], pk_keys[:, n, :],
                                   start=True, stop=True)
                mm.then_inc(T("wc"), 1)
                pe.wait_ge(wt, 16 * NW)
                for h in range(UNIT):
                    mm = pe.matmul(ps[0:CD, 2 + h // 4, (h % 4) * D:(h % 4 + 1) * D], wvt0[:, h, :], wout0[:, h, :],
                                   start=True, stop=True)
                mm.then_inc(T("cw0"), 1)

                pe.wait_ge(V.sem, V.after("wc", 0))
                pe.wait_ge(A.sem, A.after("cw0", 0))

                v_flat = v_blk[:, :, :].rearrange("p h m -> p (h m)")

                def products(b):
                    first = isinstance(b, int)
                    pe.wait_ge(ctx_in, (b + 1) * 16)
                    for h in range(UNIT):
                        if h == 6 and not first:
                            pe.wait_ge(BA.sem, BA.after("g2", b - 1))
                        pe.matmul(ps[0:HD0, h // 3, (h % 3) * CTX:(h % 3 + 1) * CTX],
                                  wk0[:, h * HD0:(h + 1) * HD0], cbuf[:, P:P + CTX], start=True, stop=True)
                    pe.matmul(ps[:, 3, 0:CTX], wk1[:, :], cbuf[:, P:P + CTX], start=True, stop=True)
                    pe.matmul(ps[:, 3, CTX:2 * CTX], wv1[:, :], cbuf[:, P:P + CTX], start=True, stop=True)\
                        .then_inc(BT("k"), 1)
                    for u in range(3):
                        if u > 0:
                            pe.wait_ge(BV.sem, BV.after(f"vw{u - 1}", b))
                        elif not first:
                            pe.wait_ge(BV.sem, BV.after("vw2", b - 1))
                        if u == 1:
                            pe.wait_ge(BV.sem, BV.after("v_blk", b))
                        for c in range(CHUNKS):
                            to = ps[:, 5 + c // 4, (c % 4) * D:(c % 4 + 1) * D]
                            if u > 0:
                                n, at = min(P, FLAT - c * P), (u - 1) * FLAT + c * P
                                mm = pe.matmul(to[0:n, :], v_flat[:, at:at + n], wo1[:, :], start=True, stop=True)
                                continue
                            heads = [h for h in range(UNIT) if h * CTX < (c + 1) * P and (h + 1) * CTX > c * P]
                            for h in heads:
                                off = P + c * P - h * CTX
                                mm = pe.matmul(to, cbuf[:, off:off + P], cw[:, h * D:(h + 1) * D],
                                               start=(h == heads[0]), stop=(h == heads[-1]))
                        mm.then_inc(BT(f"vw{u}"), 1)
                        if u == 0:
                            pe.wait_ge(BV.sem, BV.after("kt1", b))
                            pe.wait_ge(BA.sem, BA.after("kt0", b))
                        else:
                            pe.wait_ge(BV.sem, BV.after("k_blk", b))
                            pe.wait_ge(BA.sem, BA.after(f"g{u - 1}", b))
                        for h in range(UNIT):
                            to = ps[:, 2 + h // 3, (h % 3) * CTX:(h % 3 + 1) * CTX]
                            if u == 0:
                                mm = pe.matmul(to, wqt0[:, h, :], kt0[:, h, :], start=True, stop=True)
                            else:
                                mm = pe.matmul(to, wqt1[:, :], k_blk[:, UNIT * (u - 1) + h, :], start=True, stop=True)
                        mm.then_inc(BT(f"g{u}"), 1)

                products(0)
                with pe.Fori(1, BATCH) as b:
                    products(b)

        xn = {s: sb(f"xn_{s}", [P, D]) for s in "abcd"}
        xt = {s: sb(f"xt_{s}", [P, P]) for s in "abcd"}
        stat = {s: sb(f"stat_{s}", [P, 6]) for s in "abcd"}
        mv = {s: sb(f"mv_{s}", [P, 2]) for s in "abcd"}
        var = {s: sb(f"var_{s}", [P, 1]) for s in "abcd"}
        rs = {s: sb(f"rs_{s}", [P, 1]) for s in "abcd"}
        half = sb("half", [P, 1])
        carrier = sb("carrier", [P, 14])
        prob_even, prob_odd = sb("prob_even", [P, FLAT]), sb("prob_odd", [P, FLAT])
        prob = [prob_even, prob_odd, prob_even]
        prob_t = sb("prob_t", [P, CHUNKS, P])
        nmax = sb("nmax", [P, 3, UNIT])
        rsum = sb("rsum", [P, 3, UNIT])
        rinv = sb("rinv", [P, 3, UNIT])
        qkv = sb("qkv", [P, 3 * D])
        prod = sb("prod", [P, 2, FH * FH * FD // 2])
        b_sc = sb("b_sc", [P, 8])
        att = sb("att", [P, FH, FH])
        amax = sb("amax", [P, FH])
        asum = sb("asum", [P, FH])
        arec = sb("arec", [P, FH])
        av = sb("av", [P, D])
        av_t = sb("av_t", [P, P])
        x2 = sb("x2", [P, D])
        x2_t = av_t
        sq = sb("sq", [P, D])
        odd = sq
        gate = sb("gate", [P, 3, EXPERTS])
        d_sc = sb("d_sc", [P, 8])
        sim = sb("sim", [P, 2 * PH, KEYS])
        rest = sb("rest", [P, 2 * PH, KEYS])
        best = sb("best", [P, 2 * PH, TOP])
        cand = sb("cand", [P, PH, CANDS])
        cbest = sb("cbest", [P, PH, TOP])
        neg1 = sb("neg1", [P, PH])
        cexp = sb("cexp", [P, PH, TOP])
        zsum = sb("zsum", [P, PH])
        zinv = sb("zinv", [P, PH])
        diag = sb("diag", [P, 2, P])
        NSUM, NEXP = 2, 2
        sums = sb("sums", [P, NSUM, KEYS, KEYS])
        wexp = sb("wexp", [P, NEXP, GRID])
        gel = sb("gel", [P, GRID // P, P])

        LINES = [
            "a_stats a_aggr a_eps", "a_xn", "c_stats c_aggr c_eps", "c_xn",
            "b_stats b_aggr b_eps", "b_vr b_vr2 b_xn", "b_qkv", "b_qk0 b_qk1 b_amax b_asub", "b_asum b_arec",
            "b_av0 b_av1 b_anorm", "b_x2 b_eps3 b_glog b_gmax b_grec b_gates", "b_y0 b_y1 b_y2 b_y3 b_y4 b_y5 b_y6 b_y7 b_both b_res",
            "d_stats d_aggr d_eps", "d_vr d_n2", "d_sc d_xn", "d_ta d_tr d_tb", "d_cand d_ca d_cr d_cb d_nv d_vs",
            "d_vsum d_vrec", "d_m0 d_m1 d_m2 d_m3 d_m4 d_m5 d_m6 d_m7", "d_gw", "d_fin",
            "u0_max", "u0_rec", "u0_res", "u1_max", "u1_rec", "u1_res", "u2_max", "u2_rec", "u2_res",
            "a_pow", "c_pow", "b_pow", "b_pow2", "b_pqk0 b_pqk1", "b_pav0 b_pav1", "b_pow3", "d_pow", "d_pow2",
            "d_s0 d_s1 d_s2 d_s3 d_s4 d_s5 d_s6 d_s7", "u0_norm", "u1_norm", "u2_norm",
            "a_axt", "b_axt", "c_axt", "d_axt", "b_aexp", "b_aavt", "b_sq", "b_ax2t", "b_gexp", "d_sim", "d_gel",
            "d_vexp", "d_g0 d_e0 d_g1 d_e1 d_g2 d_e2 d_g3 d_e3 d_g4 d_e4 d_g5 d_e5 d_g6 d_e6 d_g7 d_e7",
            "u0_exp", "u0_apt0 u0_apt1 u0_apt2", "u1_exp", "u1_apt0 u1_apt1 u1_apt2", "u2_exp",
            "u2_apt0 u2_apt1 u2_apt2",
            "a_txt", "b_txt", "c_txt", "d_txt", "b_tqkv", "b_tavt", "b_tatt", "b_tx2t", "b_tgate", "b_ty0 b_ty1",
            "d_tsim", "d_ht0 d_ht1", "d_w0 d_w1 d_w2 d_w3 d_w4 d_w5 d_w6 d_w7", "d_out",
            "u0_sc", "u0_pt0 u0_pt1 u0_pt2 u0_out", "u1_sc", "u1_pt0 u1_pt1 u1_pt2 u1_out", "u2_sc",
            "u2_pt0 u2_pt1 u2_pt2 u2_out",
        ]
        STEPS = {}
        for line in LINES:
            steps = Steps(sem("s_" + line.split()[0]), line)
            for name in steps.names:
                STEPS[name] = steps
        stored = sem("stored")
        half_set = sem("half_set")

        DEPTH = 4
        SHARED = {
            "score_banks": [("u0_sc", "u0_exp", 0), ("u1_sc", "u1_exp", 1), ("u2_sc", "u2_exp", 1)],
            "bank7": [("u1_pt1", "u1_apt1", 2), ("a_txt", "a_axt", 0), ("u1_pt2", "u1_apt2", 2),
                      ("u1_out", "u1_res", 2), ("u2_pt0", "u2_apt0", 2), ("u2_pt1", "u2_apt1", 2),
                      ("u2_pt2", "u2_apt2", 2), ("u2_out", "u2_res", 2), ("u0_pt0", "u0_apt0", 0),
                      ("u0_pt1", "u0_apt1", 0), ("u0_pt2", "u0_apt2", 0), ("c_txt", "c_axt", 1),
                      ("u0_out", "u0_res", 0), ("u1_pt0", "u1_apt0", 1)],
            "bank3": [("d_ht1", "d_gel", 3), ("b_tavt", "b_aavt", 1), ("b_tatt", "b_x2", 1),
                      ("b_tx2t", "b_ax2t", 1), ("b_tgate", "b_glog", 1), ("b_ty0", "b_y3", 1),
                      ("b_ty1", "b_y7", 1), ("b_txt", "b_axt", 0), ("b_tqkv", "b_qkv", 0)],
            "bank4": [("d_ht0", "d_gel", 3), ("d_txt", "d_axt", 2), ("d_tsim", "d_sim", 2),
                      ("d_out", "d_fin", 3)],
            "prob_even": [("u2_exp", "u2_pt2", 2), ("u0_exp", "u0_pt2", 0)],
            "prob_odd": [("u1_exp", "u1_pt2", 1)],
            "prob_t": [("u1_apt0", "u1_out", 2), ("u2_apt0", "u2_out", 2), ("u0_apt0", "u0_out", 0)],
        }
        BEFORE = {}
        for users in SHARED.values():
            n = len(users)
            for k, (first, end, lag) in enumerate(users):
                BEFORE[first] = [(users[(k - back) % n][1],
                                  lag - users[(k - back) % n][2] - (1 if back > k else 0) - (back > n) * ((back - 1) // n))
                                 for back in range(1, n * (DEPTH + 1))]

        def wait(eng, name, t):
            if not isinstance(t, int) or 0 <= t < TILES:
                eng.wait_ge(STEPS[name].sem, STEPS[name].after(name, t))

        def done(name):
            return STEPS[name](name)

        def vacated(eng, first, t):
            for end, ahead in BEFORE[first]:
                if not isinstance(t, int) or 0 <= t + ahead < TILES:
                    wait(eng, end, t + ahead)
                    return

        def there(t):
            return not isinstance(t, int) or 0 <= t < TILES

        def x_of(t):
            return xs[:, t, :] if isinstance(t, int) else xs[:, bass.ds(t, 1), :].rearrange("p a d -> p (a d)")

        def batch_of(t):
            return t // PER_BATCH

        def bodies(eng, body):
            for i in range(DEPTH + 1):
                body(i)
            with eng.Fori(DEPTH + 1, TILES) as i:
                body(i)
            for i in range(TILES, TILES + DEPTH):
                body(i)

        U_OF = ["a", "c", "c"]
        BANK3, BANK4, BANK7, WBANK = 3, 4, 7, 5

        block = es.enter_context(nc.Block())

        @block.sync
        def _(sp):
            def store(t):
                if not there(t):
                    return
                wait(sp, "d_fin", t)
                dst = d_out[t, :, :] if isinstance(t, int) else \
                    d_out[bass.ds(t, 1), :, :].rearrange("a p d -> (a p) d")
                sp.dma_start(dst, x_of(t)).then_inc(stored, 16)

            def body(i):
                store(i - DEPTH)
            bodies(sp, body)
            sp.wait_ge(stored, 16 * TILES)

        @block.gpsimd
        def _(pool):
            def power(name, out_, in_):
                pool.tensor_tensor(out_[:, :], in_[:, :], half[:, :], ALU.pow).then_inc(done(name), 1)

            def rsqrt_var(s, t):
                if not there(t):
                    return
                wait(pool, f"{s}_eps", t)
                wait(pool, f"{s}_xn", t - 1)
                power(f"{s}_pow", rs[s], var[s])

            def d_pow2(t):
                if not there(t):
                    return
                wait(pool, "d_n2", t)
                wait(pool, "d_sc", t - 1)
                power("d_pow2", d_sc[:, 1:2], d_sc[:, 0:1])

            def b_pow2(t):
                if not there(t):
                    return
                wait(pool, "b_vr2", t)
                wait(pool, "b_qkv", t - 1)
                power("b_pow2", b_sc[:, 1:2], b_sc[:, 0:1])

            def b_pow3(t):
                if not there(t):
                    return
                wait(pool, "b_eps3", t)
                wait(pool, "b_gates", t - 1)
                power("b_pow3", b_sc[:, 4:5], b_sc[:, 3:4])

            def norm(u, t):
                if not there(t):
                    return
                wait(pool, f"u{u}_exp", t)
                wait(pool, f"u{u}_rec", t)
                pr = prob[u][:, :].rearrange("p (h m) -> p h m", m=CTX)
                pool.tensor_tensor(pr, pr, rinv[:, u, :].unsqueeze(2).to_broadcast([P, UNIT, CTX]), ALU.mult)\
                    .then_inc(done(f"u{u}_norm"), 1)

            def b_qk(k, t):
                if not there(t):
                    return
                wait(pool, "b_qkv", t)
                wait(pool, f"b_av{k}", t - 1)
                n = FH // 2
                q = qkv[:, k * n * FD:(k + 1) * n * FD].rearrange("p (h d) -> p h d", d=FD)
                kk = qkv[:, D:3 * D].rearrange("p (g e) -> p g e", e=2 * FD)[:, :, 0:FD]
                pool.tensor_tensor(prod[:, k, :].rearrange("p (h g d) -> p h g d", g=FH, d=FD),
                                   q.unsqueeze(2).to_broadcast([P, n, FH, FD]),
                                   kk.unsqueeze(1).to_broadcast([P, n, FH, FD]), ALU.mult)\
                    .then_inc(done(f"b_pqk{k}"), 1)

            def b_av(k, t):
                if not there(t):
                    return
                wait(pool, "b_aexp", t)
                wait(pool, f"b_qk{k}", t)
                n = FH // 2
                v = qkv[:, D:3 * D].rearrange("p (g e) -> p e g", e=2 * FD)[:, FD:2 * FD, :]
                pool.tensor_tensor(prod[:, k, :].rearrange("p (h d g) -> p h d g", g=FH, d=FD),
                                   att[:, k * n:(k + 1) * n, :].unsqueeze(2).to_broadcast([P, n, FD, FH]),
                                   v.unsqueeze(1).to_broadcast([P, n, FD, FH]), ALU.mult)\
                    .then_inc(done(f"b_pav{k}"), 1)

            def d_sums(h, t):
                if not there(t):
                    return
                if h == 0:
                    wait(pool, "d_sim", t)
                if h >= NSUM:
                    wait(pool, f"d_m{h - NSUM}", t)
                else:
                    wait(pool, f"d_m{h + (PH - 1 - h) // NSUM * NSUM}", t - 1)
                pool.tensor_tensor(sums[:, h % NSUM, :, :],
                                   sim[:, h, :].unsqueeze(2).to_broadcast([P, KEYS, KEYS]),
                                   sim[:, PH + h, :].unsqueeze(1).to_broadcast([P, KEYS, KEYS]), ALU.add)\
                    .then_inc(done(f"d_s{h}"), 1)

            pool.wait_ge(half_set, 1)

            def body(i):
                rsqrt_var("a", i)
                b_qk(1, i - 1)
                norm(2, i - 2)
                d_sums(2, i - 3)
                d_sums(3, i - 3)
                b_av(0, i - 1)
                b_av(1, i - 1)
                d_sums(4, i - 3)
                norm(0, i)
                b_pow3(i - 1)
                rsqrt_var("d", i - 2)
                d_sums(5, i - 3)
                d_pow2(i - 2)
                d_sums(6, i - 3)
                d_sums(7, i - 3)
                rsqrt_var("c", i - 1)
                d_sums(0, i - 2)
                d_sums(1, i - 2)
                rsqrt_var("b", i)
                norm(1, i - 1)
                b_pow2(i)
                b_qk(0, i)
            bodies(pool, body)

        @block.scalar
        def _(act):
            def turned(s, t):
                if not there(t):
                    return
                wait(act, f"{s}_txt", t)
                wait(act, {"a": "u0_sc", "b": "b_tqkv", "c": "u2_sc", "d": "d_ht1"}[s], t - 1)
                act.activation(xt[s][:, :], ps[:, {"a": BANK7, "b": BANK3, "c": BANK7, "d": BANK4}[s], 0:P],
                               ACT.Copy).then_inc(done(f"{s}_axt"), 1)

            def exps(u, t):
                if not there(t):
                    return
                wait(act, f"u{u}_max", t)
                vacated(act, f"u{u}_exp", t)
                wait(act, f"u{u}_rec", t - 1)
                for h in range(UNIT):
                    ins = act.activation(prob[u][:, h * CTX:(h + 1) * CTX],
                                         ps[:, h // 3, (h % 3) * CTX:(h % 3 + 1) * CTX], ACT.Exp,
                                         bias=nmax[:, u, h:h + 1], accum_out=rsum[:, u, h:h + 1])
                ins.then_inc(done(f"u{u}_exp"), 1)

            def prob_out(u, r, t):
                if not there(t):
                    return
                wait(act, f"u{u}_pt{r}", t)
                if r == 0:
                    vacated(act, f"u{u}_apt0", t)
                n = min(4, CHUNKS - 4 * r)
                act.activation(prob_t[:, 4 * r:4 * r + n, :], ps[:, BANK7, 0:n * P].rearrange("p (c n) -> p c n", n=P),
                               ACT.Copy).then_inc(done(f"u{u}_apt{r}"), 1)

            def d_sim(t):
                if not there(t):
                    return
                wait(act, "d_tsim", t)
                wait(act, "d_s7", t - 1)
                wait(act, "d_tr", t - 1)
                act.activation(sim[:, :, :], ps[:, BANK4, :].rearrange("p (n k) -> p n k", k=KEYS), ACT.Copy)\
                    .then_inc(done("d_sim"), 1)

            def d_gelu(t):
                if not there(t):
                    return
                wait(act, "d_ht0", t)
                wait(act, "d_out", t - 1)
                act.activation(gel[:, 0:4, :], ps[:, BANK4, :].rearrange("p (c n) -> p c n", n=P), ACT.Gelu)
                wait(act, "d_ht1", t)
                act.activation(gel[:, 4:8, :], ps[:, BANK3, :].rearrange("p (c n) -> p c n", n=P), ACT.Gelu)\
                    .then_inc(done("d_gel"), 1)

            def b_aexp(t):
                if not there(t):
                    return
                wait(act, "b_asub", t)
                act.activation(att[:, :, :], att[:, :, :], ACT.Exp).then_inc(done("b_aexp"), 1)

            def b_aavt(t):
                if not there(t):
                    return
                wait(act, "b_tavt", t)
                wait(act, "b_ty1", t - 1)
                act.activation(av_t[:, :], ps[:, BANK3, 0:P], ACT.Copy).then_inc(done("b_aavt"), 1)

            def b_sq(t):
                if not there(t):
                    return
                wait(act, "b_x2", t)
                wait(act, "b_eps3", t - 1)
                wait(act, "b_sq", t - 1)
                act.activation(sq[:, :], x2[:, :], ACT.Square, accum_out=b_sc[:, 2:3]).then_inc(done("b_sq"), 1)

            def b_ax2t(t):
                if not there(t):
                    return
                wait(act, "b_tx2t", t)
                act.activation(x2_t[:, :], ps[:, BANK3, 0:P], ACT.Copy).then_inc(done("b_ax2t"), 1)

            def b_gexp(t):
                if not there(t):
                    return
                wait(act, "b_gmax", t)
                wait(act, "b_gates", t - 1)
                act.activation(gate[:, 1, :], gate[:, 0, :], ACT.Exp, bias=b_sc[:, 5:6],
                               accum_out=b_sc[:, 6:7]).then_inc(done("b_gexp"), 1)

            def d_vexp(t):
                if not there(t):
                    return
                wait(act, "d_vs", t)
                act.activation(cexp[:, :, :], cexp[:, :, :], ACT.Exp).then_inc(done("d_vexp"), 1)

            def d_exp(h, t):
                if not there(t):
                    return
                wait(act, "d_vrec", t)
                wait(act, f"d_w{h - 2}" if h >= 2 else f"d_w{h + PH - 2}", t if h >= 2 else t - 1)
                act.activation(diag[:, h % 2, :], ident[:, :], ACT.Copy, scale=zinv[:, h:h + 1])\
                    .then_inc(done(f"d_g{h}"), 1)
                wait(act, f"d_s{h}", t)
                act.activation(wexp[:, h % NEXP, :], sums[:, h % NSUM, :, :].rearrange("p a b -> p (a b)"), ACT.Exp,
                               bias=neg1[:, h:h + 1]).then_inc(done(f"d_e{h}"), 1)

            def body(i):
                prob_out(1, 1, i - 2)
                d_vexp(i - 3)
                turned("a", i)
                d_exp(0, i - 3)
                prob_out(1, 2, i - 2)
                d_exp(1, i - 3)
                d_gelu(i - 3)
                b_aexp(i - 1)
                prob_out(2, 0, i - 2)
                d_exp(2, i - 3)
                prob_out(2, 1, i - 2)
                d_exp(3, i - 3)
                prob_out(2, 2, i - 2)
                exps(0, i)
                b_aavt(i - 1)
                d_exp(4, i - 3)
                b_sq(i - 1)
                b_ax2t(i - 1)
                b_gexp(i - 1)
                prob_out(0, 0, i)
                d_exp(5, i - 3)
                turned("d", i - 2)
                d_exp(6, i - 3)
                prob_out(0, 1, i)
                d_sim(i - 2)
                prob_out(0, 2, i)
                turned("c", i - 1)
                d_exp(7, i - 3)
                exps(1, i - 1)
                turned("b", i)
                prob_out(1, 0, i - 1)
                exps(2, i - 1)
            bodies(act, body)

        @block.tensor
        def _(pe):
            def turn(s, t):
                if not there(t):
                    return
                wait(pe, f"{s}_xn", t)
                vacated(pe, f"{s}_txt", t)
                pe.transpose(ps[:, {"a": BANK7, "b": BANK3, "c": BANK7, "d": BANK4}[s], 0:P], xn[s][:, :],
                             ident[:, :]).then_inc(done(f"{s}_txt"), 1)

            def scores(u, t):
                if not there(t):
                    return
                s = U_OF[u]
                wait(pe, f"{s}_axt", t)
                vacated(pe, f"u{u}_sc", t)
                b = batch_of(t)
                at = 0
                for k, heads in enumerate(BANK_HEADS):
                    n = heads * CTX
                    rhs = G[:, b, u, at:at + n] if isinstance(b, int) else \
                        G[:, bass.ds(b, 1), u, at:at + n].rearrange("p a n -> p (a n)")
                    mm = pe.matmul(ps[:, k, 0:n], xt[s][:, :], rhs, start=True, stop=(s == "a"))
                    if s == "c":
                        far = far_row[:, b:b + 1, :] if isinstance(b, int) else far_row[:, bass.ds(b, 1), :]
                        mm = pe.matmul(ps[:, k, 0:n].rearrange("p (h m) -> p h m", m=CTX), ones_bf[:, :],
                                       far.to_broadcast([1, heads, CTX]), start=False, stop=True)
                    at += n
                mm.then_inc(done(f"u{u}_sc"), 1)

            def turn_prob(u, r, t):
                if not there(t):
                    return
                if r == 0:
                    wait(pe, f"u{u}_norm", t)
                vacated(pe, f"u{u}_pt{r}", t)
                for c in range(4 * r, min(4 * r + 4, CHUNKS)):
                    n = min(P, FLAT - c * P)
                    mm = pe.transpose(ps[0:n, BANK7, (c % 4) * P:(c % 4 + 1) * P], prob[u][:, c * P:c * P + n],
                                      ident[:, :])
                mm.then_inc(done(f"u{u}_pt{r}"), 1)

            def values(u, t):
                if not there(t):
                    return
                wait(pe, f"u{u}_apt2", t)
                vacated(pe, f"u{u}_out", t)
                b = batch_of(t)
                if u == 0:
                    pe.matmul(ps[:, BANK7, 0:D], ones_row[:, :], bout_g[:, :], start=True, stop=False)
                for c in range(CHUNKS):
                    n = min(P, FLAT - c * P)
                    rhs = VW[0:n, b, u, c * D:(c + 1) * D] if isinstance(b, int) else \
                        VW[0:n, bass.ds(b, 1), u, c * D:(c + 1) * D].rearrange("p a n -> p (a n)")
                    mm = pe.matmul(ps[:, BANK7, 0:D], prob_t[0:n, c, :], rhs, start=(c == 0 and u != 0),
                                   stop=(c == CHUNKS - 1))
                mm.then_inc(done(f"u{u}_out"), 1)

            def b_tqkv(t):
                if not there(t):
                    return
                wait(pe, "b_axt", t)
                vacated(pe, "b_tqkv", t)
                pe.matmul(ps[:, BANK3, 0:3 * D], xt["b"][:, :], wqkv[:, :], start=True, stop=True)\
                    .then_inc(done("b_tqkv"), 1)

            def b_tavt(t):
                if not there(t):
                    return
                wait(pe, "b_anorm", t)
                vacated(pe, "b_tavt", t)
                pe.transpose(ps[:, BANK3, 0:P], av[:, :], ident[:, :]).then_inc(done("b_tavt"), 1)

            def b_tatt(t):
                if not there(t):
                    return
                wait(pe, "b_aavt", t)
                vacated(pe, "b_tatt", t)
                pe.matmul(ps[:, BANK3, 0:D], ones_row[:, :], bo_row[:, :], start=True, stop=False)
                pe.matmul(ps[:, BANK3, 0:D], av_t[:, :], wo_f[:, :], start=False, stop=True)\
                    .then_inc(done("b_tatt"), 1)

            def b_tx2t(t):
                if not there(t):
                    return
                wait(pe, "b_x2", t)
                vacated(pe, "b_tx2t", t)
                pe.transpose(ps[:, BANK3, 0:P], x2[:, :], ident[:, :]).then_inc(done("b_tx2t"), 1)

            def b_tgate(t):
                if not there(t):
                    return
                wait(pe, "b_ax2t", t)
                vacated(pe, "b_tgate", t)
                pe.matmul(ps[:, BANK3, 0:EXPERTS], x2_t[:, :], wg[:, :], start=True, stop=True)\
                    .then_inc(done("b_tgate"), 1)

            def b_ty(r, t):
                if not there(t):
                    return
                vacated(pe, f"b_ty{r}", t)
                pe.matmul(ps[:, BANK3, :], x2_t[:, :], we[:, r * BANK:(r + 1) * BANK], start=True, stop=True)\
                    .then_inc(done(f"b_ty{r}"), 1)

            def d_tsim(t):
                if not there(t):
                    return
                wait(pe, "d_axt", t)
                vacated(pe, "d_tsim", t)
                pe.matmul(ps[:, BANK4, :], xt["d"][:, :], wc[:, :], start=True, stop=True).then_inc(done("d_tsim"), 1)

            def d_ht(r, t):
                if not there(t):
                    return
                wait(pe, "d_axt", t)
                vacated(pe, f"d_ht{r}", t)
                for c in range(4):
                    mm = pe.matmul(ps[:, BANK3 if r else BANK4, c * P:(c + 1) * P],
                                   down[:, (4 * r + c) * P:(4 * r + c + 1) * P], xt["d"][:, :], start=True, stop=True)
                mm.then_inc(done(f"d_ht{r}"), 1)

            def d_weights(h, t):
                if not there(t):
                    return
                wait(pe, f"d_m{h}", t)
                wait(pe, f"d_g{h}", t)
                if h == 0:
                    wait(pe, "d_gw", t - 1)
                for c in range(GRID // P):
                    mm = pe.matmul(ps[:, WBANK + c // 4, (c % 4) * P:(c % 4 + 1) * P],
                                   wexp[:, h % NEXP, c * P:(c + 1) * P], diag[:, h % 2, :],
                                   start=(h == 0 and c % 4 == 0), stop=(h == PH - 1), skip_group_check=True)
                mm.then_inc(done(f"d_w{h}"), 1)

            def d_out_(t):
                if not there(t):
                    return
                wait(pe, "d_gw", t)
                vacated(pe, "d_out", t)
                for c in range(GRID // P):
                    mm = pe.matmul(ps[:, BANK4, 0:D], gel[:, c, :], up[:, c, :], start=(c == 0),
                                   stop=(c == GRID // P - 1))
                mm.then_inc(done("d_out"), 1)

            def body(i):
                d_ht(0, i - 3)
                d_ht(1, i - 3)
                turn("a", i)
                turn_prob(1, 2, i - 2)
                scores(0, i)
                values(1, i - 2)
                d_weights(0, i - 3)
                turn_prob(2, 0, i - 2)
                d_weights(1, i - 3)
                turn_prob(2, 1, i - 2)
                turn_prob(2, 2, i - 2)
                d_weights(2, i - 3)
                values(2, i - 2)
                b_tavt(i - 1)
                b_tatt(i - 1)
                b_tx2t(i - 1)
                d_weights(3, i - 3)
                b_tgate(i - 1)
                turn_prob(0, 0, i)
                b_ty(0, i - 1)
                d_weights(4, i - 3)
                b_ty(1, i - 1)
                turn("d", i - 2)
                turn_prob(0, 1, i)
                d_tsim(i - 2)
                d_weights(5, i - 3)
                turn_prob(0, 2, i)
                turn("c", i - 1)
                scores(1, i - 1)
                values(0, i)
                d_weights(6, i - 3)
                d_weights(7, i - 3)
                scores(2, i - 1)
                turn("b", i)
                turn_prob(1, 0, i - 1)
                b_tqkv(i)
                d_out_(i - 3)
                turn_prob(1, 1, i - 1)
            bodies(pe, body)

        @block.vector
        def _(dve):
            dve.memset(half[:, :], -0.5).then_inc(half_set, 1)

            def carry(n):
                dve.memset(carrier[:, n:n + 1], 0.0)

            def moments(s, t):
                if not there(t):
                    return
                before = {"b": "u0_res", "c": "b_res", "d": "u2_res"}
                if s in before:
                    wait(dve, before[s], t)
                wait(dve, f"{s}_aggr", t - 1)
                carry(10 + "abcd".index(s))
                dve.bn_stats(stat[s][:, :], x_of(t)).then_inc(done(f"{s}_stats"), 1)

            def mean_var(s, t):
                if not there(t):
                    return
                wait(dve, f"{s}_stats", t)
                wait(dve, f"{s}_xn", t - 1)
                carry("abcd".index(s))
                dve.bn_aggr(mv[s][:, :], stat[s][:, :]).then_inc(done(f"{s}_aggr"), 1)

            def var_eps(s, t):
                if not there(t):
                    return
                wait(dve, f"{s}_aggr", t)
                wait(dve, f"{s}_pow", t - 1)
                dve.tensor_scalar(var[s][:, :], mv[s][:, 1:2], 1e-5, None, ALU.add).then_inc(done(f"{s}_eps"), 1)

            def normed(s, t):
                if not there(t):
                    return
                if s != "d":
                    wait(dve, f"{s}_pow", t)
                wait(dve, f"{s}_txt", t - 1)
                if s == "b":
                    wait(dve, "b_x2", t - 1)
                dve.tensor_scalar(xn[s][:, :], x_of(t), mv[s][:, 0:1], d_sc[:, 3:4] if s == "d" else rs[s][:, :],
                                  ALU.subtract, ALU.mult).then_inc(done(f"{s}_xn"), 1)

            def b_moments2(t):
                if not there(t):
                    return
                wait(dve, "b_pow", t)
                wait(dve, "b_pow2", t - 1)
                dve.tensor_scalar(b_sc[:, 0:1], mv["b"][:, 1:2], rs["b"][:, :], rs["b"][:, :], ALU.mult, ALU.mult)\
                    .then_inc(done("b_vr"), 1)
                wait(dve, "b_vr", t)
                dve.tensor_scalar(b_sc[:, 0:1], b_sc[:, 0:1], 1e-6, None, ALU.add).then_inc(done("b_vr2"), 1)

            def d_moments2(t):
                if not there(t):
                    return
                wait(dve, "d_pow", t)
                wait(dve, "d_pow2", t - 1)
                dve.tensor_scalar(d_sc[:, 0:1], mv["d"][:, 1:2], rs["d"][:, :], rs["d"][:, :], ALU.mult, ALU.mult)\
                    .then_inc(done("d_vr"), 1)
                wait(dve, "d_vr", t)
                dve.tensor_scalar(d_sc[:, 0:1], d_sc[:, 0:1], float(D), 1e-24, ALU.mult, ALU.max)\
                    .then_inc(done("d_n2"), 1)

            def d_scale(t):
                if not there(t):
                    return
                wait(dve, "d_pow2", t)
                wait(dve, "d_xn", t - 1)
                dve.tensor_scalar(d_sc[:, 3:4], d_sc[:, 1:2], rs["d"][:, :], float(D) ** 0.5, ALU.mult, ALU.mult)\
                    .then_inc(done("d_sc"), 1)
                wait(dve, "d_sc", t)
                normed("d", t)

            def unit_max(u, t):
                if not there(t):
                    return
                wait(dve, f"u{u}_sc", t)
                wait(dve, f"u{u}_exp", t - 1)
                dve.tensor_reduce(nmax[:, u, 0:6], ps[:, 0:2, 0:3 * CTX].rearrange("p k (h m) -> p k h m", m=CTX),
                                  X_AXIS, ALU.max, negate=True)
                dve.tensor_reduce(nmax[:, u, 6:8], ps[:, 2, 0:2 * CTX].rearrange("p (h m) -> p h m", m=CTX),
                                  X_AXIS, ALU.max, negate=True).then_inc(done(f"u{u}_max"), 1)

            def unit_rec(u, t):
                if not there(t):
                    return
                wait(dve, f"u{u}_exp", t)
                wait(dve, f"u{u}_norm", t - 1)
                dve.reciprocal(rinv[:, u, :], rsum[:, u, :]).then_inc(done(f"u{u}_rec"), 1)

            def unit_res(u, t):
                if not there(t):
                    return
                wait(dve, f"u{u}_out", t)
                if u == 1:
                    wait(dve, "b_res", t)
                if u == 2:
                    wait(dve, "u1_res", t)
                dve.tensor_tensor(x_of(t), x_of(t), ps[:, BANK7, 0:D], ALU.add).then_inc(done(f"u{u}_res"), 1)

            def b_qkv(t):
                if not there(t):
                    return
                wait(dve, "b_pow2", t)
                wait(dve, "b_tqkv", t)
                wait(dve, "b_pav1", t - 1)
                dve.scalar_tensor_tensor(out=qkv[:, :], in0=ps[:, BANK3, 0:3 * D], scalar=b_sc[:, 1:2], in1=bqkv[:, :],
                                         op0=ALU.mult, op1=ALU.add).then_inc(done("b_qkv"), 1)

            def b_sum_qk(k, t):
                if not there(t):
                    return
                wait(dve, f"b_pqk{k}", t)
                if k == 0:
                    wait(dve, "b_pav1", t - 1)
                    wait(dve, "b_asum", t - 1)
                n = FH // 2
                dve.tensor_reduce(att[:, n * k:n * (k + 1), :], prod[:, k, :].rearrange("p (h g d) -> p h g d", g=FH, d=FD),
                                  X_AXIS, ALU.add).then_inc(done(f"b_qk{k}"), 1)

            def b_sum_av(k, t):
                if not there(t):
                    return
                wait(dve, f"b_pav{k}", t)
                if k == 0:
                    wait(dve, "b_tavt", t - 1)
                n = FH // 2
                dve.tensor_reduce(av[:, n * FD * k:n * FD * (k + 1)].rearrange("p (h d) -> p h d", d=FD),
                                  prod[:, k, :].rearrange("p (h d g) -> p h d g", g=FH, d=FD),
                                  X_AXIS, ALU.add).then_inc(done(f"b_av{k}"), 1)

            def b_largest(t):
                if not there(t):
                    return
                wait(dve, "b_qk1", t)
                wait(dve, "b_asub", t - 1)
                dve.tensor_reduce(amax[:, :], att[:, :, :], X_AXIS, ALU.max).then_inc(done("b_amax"), 1)

            def b_shift(t):
                if not there(t):
                    return
                wait(dve, "b_amax", t)
                dve.tensor_tensor(att[:, :, :], att[:, :, :], amax[:, :].unsqueeze(2).to_broadcast([P, FH, FH]),
                                  ALU.subtract).then_inc(done("b_asub"), 1)

            def b_sum(t):
                if not there(t):
                    return
                wait(dve, "b_aexp", t)
                wait(dve, "b_arec", t - 1)
                dve.tensor_reduce(asum[:, :], att[:, :, :], X_AXIS, ALU.add).then_inc(done("b_asum"), 1)

            def b_sum_inv(t):
                if not there(t):
                    return
                wait(dve, "b_asum", t)
                wait(dve, "b_anorm", t - 1)
                dve.reciprocal(arec[:, :], asum[:, :]).then_inc(done("b_arec"), 1)

            def b_norm(t):
                if not there(t):
                    return
                wait(dve, "b_av1", t)
                wait(dve, "b_arec", t)
                o = av[:, :].rearrange("p (h d) -> p h d", d=FD)
                dve.tensor_tensor(o, o, arec[:, :].unsqueeze(2).to_broadcast([P, FH, FD]), ALU.mult)\
                    .then_inc(done("b_anorm"), 1)

            def b_x2(t):
                if not there(t):
                    return
                wait(dve, "b_tatt", t)
                wait(dve, "b_res", t - 1)
                dve.tensor_tensor(x2[:, :], xn["b"][:, :], ps[:, BANK3, 0:D], ALU.add).then_inc(done("b_x2"), 1)

            def b_mean_square(t):
                if not there(t):
                    return
                wait(dve, "b_sq", t)
                wait(dve, "b_pow3", t - 1)
                dve.tensor_scalar(b_sc[:, 3:4], b_sc[:, 2:3], 1.0 / D, 1e-6, ALU.mult, ALU.add)\
                    .then_inc(done("b_eps3"), 1)

            def b_logits(t):
                if not there(t):
                    return
                wait(dve, "b_pow3", t)
                wait(dve, "b_tgate", t)
                wait(dve, "b_gexp", t - 1)
                dve.scalar_tensor_tensor(out=gate[:, 0, :], in0=ps[:, BANK3, 0:EXPERTS], scalar=b_sc[:, 4:5],
                                         in1=bg[:, :], op0=ALU.mult, op1=ALU.add).then_inc(done("b_glog"), 1)
                wait(dve, "b_glog", t)
                dve.tensor_reduce(b_sc[:, 5:6], gate[:, 0, :], X_AXIS, ALU.max, negate=True)\
                    .then_inc(done("b_gmax"), 1)

            def b_gates(t):
                if not there(t):
                    return
                wait(dve, "b_gexp", t)
                dve.reciprocal(b_sc[:, 7:8], b_sc[:, 6:7]).then_inc(done("b_grec"), 1)
                wait(dve, "b_grec", t)
                wait(dve, "b_y7", t - 1)
                dve.tensor_scalar(gate[:, 2, :], gate[:, 1, :], b_sc[:, 7:8], b_sc[:, 4:5], ALU.mult, ALU.mult)\
                    .then_inc(done("b_gates"), 1)

            def b_experts(r, t):
                if not there(t):
                    return
                wait(dve, f"b_ty{r}", t)
                for e in range(4 * r, 4 * r + 4):
                    y = ps[:, BANK3, (e % 4) * D:(e % 4 + 1) * D]
                    gate_e = gate[:, 2, e:e + 1]
                    if e == 0:
                        wait(dve, "b_gates", t)
                        wait(dve, "b_tx2t", t)
                        wait(dve, "b_sq", t)
                    if e >= 2:
                        wait(dve, f"b_y{e - 2}", t)
                    if e == 1:
                        dve.tensor_scalar(odd[:, :], y, gate_e, None, ALU.mult).then_inc(done("b_y1"), 1)
                    else:
                        to = odd if e % 2 else x2
                        dve.scalar_tensor_tensor(out=to[:, :], in0=y, scalar=gate_e, in1=to[:, :], op0=ALU.mult,
                                                 op1=ALU.add).then_inc(done(f"b_y{e}"), 1)

            def b_both(t):
                if not there(t):
                    return
                wait(dve, "b_y7", t)
                dve.tensor_tensor(x2[:, :], x2[:, :], odd[:, :], ALU.add).then_inc(done("b_both"), 1)

            def b_res(t):
                if not there(t):
                    return
                wait(dve, "b_both", t)
                dve.scalar_tensor_tensor(out=x_of(t), in0=x2[:, :], scalar=tg[:, 2:3], in1=x_of(t), op0=ALU.mult,
                                         op1=ALU.add).then_inc(done("b_res"), 1)

            def d_top(part, t):
                if not there(t):
                    return
                if part == 0:
                    wait(dve, "d_sim", t)
                    wait(dve, "d_cand", t - 1)
                else:
                    wait(dve, ["d_ta", "d_tr"][part - 1], t)
                carry(4 + part)
                for n in range(2 * PH):
                    if part == 0:
                        ins = dve.max(best[:, n, 0:8], sim[:, n, :])
                    elif part == 1:
                        ins = dve.match_replace(rest[:, n, :], best[:, n, 0:8], sim[:, n, :], LOW)
                    else:
                        ins = dve.max(best[:, n, 8:16], rest[:, n, :])
                ins.then_inc(done(["d_ta", "d_tr", "d_tb"][part]), 1)

            def d_ctop(part, t):
                if not there(t):
                    return
                wait(dve, ["d_cand", "d_ca", "d_cr"][part], t)
                if part == 0:
                    wait(dve, "d_m7", t - 1)
                carry(7 + part)
                for h in range(PH):
                    if part == 0:
                        ins = dve.max(cbest[:, h, 0:8], cand[:, h, :])
                    elif part == 1:
                        ins = dve.match_replace(cand[:, h, :], cbest[:, h, 0:8], cand[:, h, :], LOW)
                    else:
                        ins = dve.max(cbest[:, h, 8:16], cand[:, h, :])
                ins.then_inc(done(["d_ca", "d_cr", "d_cb"][part]), 1)

            def d_cands(t):
                if not there(t):
                    return
                wait(dve, "d_tb", t)
                wait(dve, "d_cb", t - 1)
                at, i = 0, 0
                while i < TOP:
                    n = STAIRS[i]
                    k = sum(1 for m in STAIRS if m == n)
                    o = cand[:, :, at:at + k * n].rearrange("p h (i j) -> p h i j", j=n)
                    ins = dve.tensor_tensor(o, best[:, 0:PH, i:i + k].unsqueeze(3).to_broadcast([P, PH, k, n]),
                                            best[:, PH:2 * PH, 0:n].unsqueeze(2).to_broadcast([P, PH, k, n]), ALU.add)
                    at += k * n
                    i += k
                ins.then_inc(done("d_cand"), 1)

            def d_shift(t):
                if not there(t):
                    return
                wait(dve, "d_cb", t)
                wait(dve, "d_e7", t - 1)
                dve.tensor_scalar(neg1[:, :].unsqueeze(2), cbest[:, :, 0:1], -1.0, None, ALU.mult)\
                    .then_inc(done("d_nv"), 1)
                wait(dve, "d_vsum", t - 1)
                dve.tensor_tensor(cexp[:, :, :], cbest[:, :, :], cbest[:, :, 0:1].to_broadcast([P, PH, TOP]),
                                  ALU.subtract).then_inc(done("d_vs"), 1)

            def d_zsum(t):
                if not there(t):
                    return
                wait(dve, "d_vexp", t)
                wait(dve, "d_vrec", t - 1)
                dve.tensor_reduce(zsum[:, :], cexp[:, :, :], X_AXIS, ALU.add).then_inc(done("d_vsum"), 1)

            def d_zinv(t):
                if not there(t):
                    return
                wait(dve, "d_vsum", t)
                wait(dve, "d_g7", t - 1)
                dve.reciprocal(zinv[:, :], zsum[:, :]).then_inc(done("d_vrec"), 1)

            def d_mask(h, t):
                if not there(t):
                    return
                wait(dve, f"d_e{h}", t)
                wait(dve, "d_cb", t)
                wx = wexp[:, h % NEXP, :]
                dve.scalar_tensor_tensor(out=wx, in0=sums[:, h % NSUM, :, :].rearrange("p a b -> p (a b)"),
                                         scalar=cbest[:, h, TOP - 1:TOP], in1=wx, op0=ALU.is_ge, op1=ALU.mult)\
                    .then_inc(done(f"d_m{h}"), 1)

            def d_gw(t):
                if not there(t):
                    return
                wait(dve, "d_w7", t)
                wait(dve, "d_gel", t)
                g = gel[:, :, :].rearrange("p (k c) n -> p k (c n)", k=2)
                dve.tensor_tensor(g, g, ps[:, WBANK:WBANK + 2, :], ALU.mult).then_inc(done("d_gw"), 1)

            def d_fin(t):
                if not there(t):
                    return
                wait(dve, "d_out", t)
                dve.tensor_tensor(x_of(t), x_of(t), ps[:, BANK4, 0:D], ALU.add).then_inc(done("d_fin"), 1)

            def body(i):
                moments("a", i)
                d_fin(i - 4)
                mean_var("a", i)
                var_eps("a", i)
                d_ctop(2, i - 3)
                unit_rec(2, i - 2)
                d_shift(i - 3)
                normed("a", i)
                d_zsum(i - 3)
                d_zinv(i - 3)
                b_sum_qk(0, i - 1)
                d_mask(0, i - 3)
                b_sum_qk(1, i - 1)
                d_mask(1, i - 3)
                b_largest(i - 1)
                b_shift(i - 1)
                unit_res(1, i - 2)
                b_sum(i - 1)
                unit_max(0, i)
                d_mask(2, i - 3)
                b_sum_av(0, i - 1)
                b_sum_inv(i - 1)
                d_mask(3, i - 3)
                b_sum_av(1, i - 1)
                b_norm(i - 1)
                unit_res(2, i - 2)
                unit_rec(0, i)
                moments("d", i - 2)
                b_x2(i - 1)
                mean_var("d", i - 2)
                var_eps("d", i - 2)
                b_mean_square(i - 1)
                d_mask(4, i - 3)
                b_logits(i - 1)
                d_moments2(i - 2)
                b_gates(i - 1)
                b_experts(0, i - 1)
                d_scale(i - 2)
                d_mask(5, i - 3)
                b_experts(1, i - 1)
                b_both(i - 1)
                b_res(i - 1)
                moments("c", i - 1)
                mean_var("c", i - 1)
                var_eps("c", i - 1)
                d_mask(6, i - 3)
                normed("c", i - 1)
                d_top(0, i - 2)
                d_top(1, i - 2)
                d_mask(7, i - 3)
                unit_max(1, i - 1)
                d_top(2, i - 2)
                unit_res(0, i)
                moments("b", i)
                d_cands(i - 2)
                mean_var("b", i)
                unit_rec(1, i - 1)
                var_eps("b", i)
                d_ctop(0, i - 2)
                b_moments2(i)
                normed("b", i)
                d_gw(i - 3)
                unit_max(2, i - 1)
                b_qkv(i)
                d_ctop(1, i - 2)
            bodies(dve, body)


def kernel(**inputs):
    import numpy as np
    import concourse.bacc as bacc
    from concourse.bass_utils import run_bass_kernel_spmd

    a = {k: np.asarray(v) for k, v in inputs.items()}

    def by_head(w):
        return w.reshape(UNIT, HD0, w.shape[1]).transpose(1, 0, 2)

    def chunks(w):
        return w.reshape(-1, P, w.shape[1]).transpose(1, 0, 2)

    ctx_t = np.zeros((BATCH, CD, 2 * P + CTX), np.float32)
    ctx_t[:, :, P:P + CTX] = a["ctx_768"].transpose(0, 2, 1)
    rows = np.concatenate([a["L0_xattn_bout"], a["L0_ffn_bq"], a["L0_ffn_bup"], a["L0_ffn_bo"], a["L0_ffn_bg"],
                           a["g_xattn"], a["g_ffn"]])
    arrays = {
        "x": chunks(a["x"].reshape(-1, D)),
        "ctx_t": ctx_t,
        "mask": np.broadcast_to(a["mask_BxS2_bf1"].view(np.uint8)[None], (P, BATCH, CTX)),
        "rows": np.broadcast_to(rows[None], (P, ROW_TOTAL)),
        "cols": np.stack([a["L0_ffn_gamma1"], a["L0_ffn_gamma2"], a["L1_ffn_gamma"]], 1),
        "wk0": a["L0_xattn_Wk"],
        "wqt0": by_head(a["L0_xattn_Wq"].T),
        "wvt0": by_head(a["L0_xattn_Wv"].T),
        "wout0": by_head(a["L0_xattn_Wout"]),
        "f_wq": a["L0_ffn_Wq"],
        "f_wdt": a["L0_ffn_Wdown"].T,
        "f_wup": a["L0_ffn_Wup"],
        "f_bd": np.broadcast_to(a["L0_ffn_bdown"][:, None], (64, P)),
        "f_wo": a["L0_ffn_Wo"],
        "f_wg": a["L0_ffn_Wg"],
        "f_we": a["L0_ffn_We"].transpose(1, 0, 2).reshape(D, EXPERTS * D),
        "wk1": a["L1_xattn_Wk"],
        "wqt1": a["L1_xattn_Wq"].T,
        "wv1": a["L1_xattn_Wv"],
        "wo1": a["L1_xattn_Wo"],
        "pk_wq": a["L1_ffn_wq"].reshape(2 * PH, PK, D).transpose(1, 0, 2),
        "pk_keys": a["L1_ffn_keys"].transpose(3, 2, 0, 1).reshape(PK, 2 * PH, KEYS),
        "pk_down": a["L1_ffn_table_down"][:GRID].T,
        "pk_up": chunks(a["L1_ffn_table_up"][:GRID]),
    }
    nc = bacc.Bacc("TRN2", target_bir_lowering=False, num_devices=1)
    feed, args = {}, []
    for name, value in arrays.items():
        value = np.ascontiguousarray(value)
        feed[f"in_{name}"] = value
        args.append(nc.dram_tensor(f"in_{name}", value.shape, mybir.dt.from_np(value.dtype), kind="ExternalInput").ap())
    args.append(nc.dram_tensor("out_x", (TILES, P, D), F32, kind="ExternalOutput").ap())
    flamingo_kernel(nc, *args)
    got = run_bass_kernel_spmd(nc, [feed], core_ids=[0])
    return got.results[0]["out_x"].reshape(BATCH, SEQ, D)
```
